# Optimizing a Trainium2 kernel written in Bass

```python
import numpy as np
import jax
import jax.numpy as jnp

def _softmax(x, axis=-1):
    return jax.nn.softmax(x, axis=axis)

def _gelu(x):
    return jax.nn.gelu(x, approximate=True)

def _silu(x):
    return jax.nn.silu(x)

def _sigmoid(x):
    return jax.nn.sigmoid(x)

def _layernorm(x, axis=-1, eps=1e-05):
    m = jnp.mean(x, axis=axis, keepdims=True)
    v = jnp.var(x, axis=axis, keepdims=True)
    return (x - m) / jnp.sqrt(v + eps)

def _scatter_add(tgt, idx, src, axis=0):
    return tgt.at[idx].add(src)

def _segment_sum(src, seg, n):
    return jax.ops.segment_sum(src, seg, n)
kernel_name = 'mk_metaformer_d2_conv_nhwc256_r4_e049c7'

def setup_inputs(seed: int=0):
    np.random.seed(seed)
    _w = jnp.asarray

    def _rec_inputs():
        import jax
        import jax.numpy as jnp
        _gk = jax.random.key(seed)
        x = 7.22e-05 + 1 * jax.random.normal(jax.random.fold_in(_gk, 1), (2, 32, 32, 64), jnp.float32)
        return x
    x = _rec_inputs()

    def _L0_conv_setup():
        import jax, jax.numpy as jnp
        import numpy as np
        B, HIMG, WIMG, C = (2, 32, 32, 64)
        NH, HD = (8, 32)
        WH, WW = (8, 8)
        P = WH * WW
        NQK = 5
        S = 1 + HD + HD
        EPS = 1e-05

        def _spatial(intrinsic):
            ii = jnp.arange(WH)
            jj = jnp.arange(WW)
            ri = ii[:, None] - ii[None, :] + WH - 1
            rj = jj[:, None] - jj[None, :] + WW - 1
            rel = intrinsic[:, ri[:, None, :, None], rj[None, :, None, :], :]
            rel = rel.transpose(1, 2, 0, 3, 4, 5).reshape(P, NH, P, S)
            return (rel[..., 0], rel[..., 1:1 + HD], rel[..., 1 + HD:])
        key = jax.random.key(seed)
        ks = jax.random.split(key, 6)
        obtained = NH * HD * NQK
        bound = np.sqrt(6.0 / (P * 1 + P))
        return {'x': jax.random.normal(ks[0], (B, HIMG, WIMG, C), jnp.float32), 'W_prep': jax.random.normal(ks[1], (C, obtained), jnp.float32) * (1.0 / np.sqrt(C)), 'b_prep': jnp.zeros((obtained,), jnp.float32), 'intrinsic': jax.random.uniform(ks[2], (NH, 2 * WH - 1, 2 * WW - 1, S), jnp.float32, minval=-bound, maxval=bound), 'W_fin': jax.random.normal(ks[3], (NH * HD, C), jnp.float32) * (1.0 / np.sqrt(NH * HD)), 'b_fin': jnp.zeros((C,), jnp.float32)}
    _L0_conv_all = _L0_conv_setup()
    _L0_conv_in = {k: v for k, v in _L0_conv_all.items() if k in ('W_prep', 'b_prep', 'intrinsic', 'W_fin', 'b_fin')}
    del _L0_conv_all

    def _L0_ffn_setup():
        import jax, jax.numpy as jnp
        import numpy as np
        B, T, D, H, E = (16, 1024, 64, 128, 8)
        key = jax.random.key(seed)
        ks = jax.random.split(key, 5)
        x = jax.random.normal(ks[0], (B, T, D), dtype=jnp.float32)
        gate_w = jax.random.normal(ks[1], (D, E), dtype=jnp.float32) * 0.02
        gate_b = jnp.zeros((E,), dtype=jnp.float32)
        W1 = jax.random.normal(ks[2], (E, D, H), dtype=jnp.float32) * 0.02
        b1 = jnp.zeros((E, H), dtype=jnp.float32)
        W2 = jax.random.normal(ks[3], (E, H, D), dtype=jnp.float32) * 0.02
        b2 = jnp.zeros((E, D), dtype=jnp.float32)
        return {'x': x, 'gate_w': gate_w, 'gate_b': gate_b, 'W1': W1, 'b1': b1, 'W2': W2, 'b2': b2}
    _L0_ffn_all = _L0_ffn_setup()
    _L0_ffn_in = {k: v for k, v in _L0_ffn_all.items() if k in ('gate_w', 'gate_b', 'W1', 'b1', 'W2', 'b2')}
    del _L0_ffn_all

    def _L1_conv_setup():
        import jax, jax.numpy as jnp
        import numpy as np
        NLAT, NLON = (32, 64)
        CIN, COUT = (32, 32)
        MODES_LAT, MODES_LON = (32, 32)
        BATCH = 4

        def _legendre(lmax, mmax, x):
            npts = x.shape[0]
            pct = np.zeros((lmax, mmax, npts), dtype=np.float64)
            s = np.sqrt(1.0 - x * x)
            pmm = np.full(npts, np.sqrt(1.0 / (4.0 * np.pi)))
            for m in range(mmax):
                if m < lmax:
                    pct[m, m] = pmm
                    if m + 1 < lmax:
                        pct[m + 1, m] = x * np.sqrt(2.0 * m + 3.0) * pmm
                    for l in range(m + 2, lmax):
                        a = np.sqrt((4.0 * l * l - 1.0) / (l * l - m * m))
                        b = np.sqrt(((l - 1.0) ** 2 - m * m) / (4.0 * (l - 1.0) ** 2 - 1.0))
                        pct[l, m] = a * (x * pct[l - 1, m] - b * pct[l - 2, m])
                pmm = pmm * -np.sqrt((2.0 * m + 3.0) / (2.0 * m + 2.0)) * s
            return pct
        key = jax.random.key(seed)
        k1, k2 = jax.random.split(key)
        x = jax.random.normal(k1, (BATCH, CIN, NLAT, NLON), dtype=jnp.float32)
        scale = 1.0 / (CIN * COUT)
        weights = scale * jax.random.normal(k2, (CIN, COUT, MODES_LAT, MODES_LON, 2), dtype=jnp.float32)
        theta = (np.arange(NLAT) + 0.5) * np.pi / NLAT
        ct = np.cos(theta)
        w = np.pi / NLAT * np.sin(theta)
        pct = _legendre(NLAT, NLON // 2 + 1, ct)
        return {'x': x, 'weights': weights, 'pct': jnp.asarray(pct, jnp.float32), 'w': jnp.asarray(w, jnp.float32)}
    _L1_conv_all = _L1_conv_setup()
    _L1_conv_in = {k: v for k, v in _L1_conv_all.items() if k in ('weights', 'pct', 'w')}
    del _L1_conv_all

    def _L1_ffn_setup():
        import jax, jax.numpy as jnp
        import numpy as np
        N_EXPERTS = 8
        TOP_K = 2
        key = jax.random.key(seed)
        ks = jax.random.split(key, 5)
        B, T, C, E, H = (8, 512, 64, 8, 682)
        scale = 1.0 / np.sqrt(C)
        return {'x': jax.random.normal(ks[0], (B, T, C), dtype=jnp.float32), 'router_w': jax.random.normal(ks[1], (E, C), dtype=jnp.float32) * scale, 'w1': jax.random.normal(ks[2], (E, H, C), dtype=jnp.float32) * scale, 'w2': jax.random.normal(ks[3], (E, C, H), dtype=jnp.float32) * (1.0 / np.sqrt(H)), 'w3': jax.random.normal(ks[4], (E, H, C), dtype=jnp.float32) * scale}
    _L1_ffn_all = _L1_ffn_setup()
    _L1_ffn_in = {k: v for k, v in _L1_ffn_all.items() if k in ('router_w', 'w1', 'w2', 'w3')}
    del _L1_ffn_all
    return {'x': x, 'L0_conv_W_prep': _L0_conv_in['W_prep'], 'L0_conv_b_prep': _L0_conv_in['b_prep'], 'L0_conv_intrinsic': _L0_conv_in['intrinsic'], 'L0_conv_W_fin': _L0_conv_in['W_fin'], 'L0_conv_b_fin': _L0_conv_in['b_fin'], 'L0_ffn_gate_w': _L0_ffn_in['gate_w'], 'L0_ffn_gate_b': _L0_ffn_in['gate_b'], 'L0_ffn_W1': _L0_ffn_in['W1'], 'L0_ffn_b1': _L0_ffn_in['b1'], 'L0_ffn_W2': _L0_ffn_in['W2'], 'L0_ffn_b2': _L0_ffn_in['b2'], 'L1_conv_weights': _L1_conv_in['weights'], 'L1_conv_pct': _L1_conv_in['pct'], 'L1_conv_w': _L1_conv_in['w'], 'L1_ffn_router_w': _L1_ffn_in['router_w'], 'L1_ffn_w1': _L1_ffn_in['w1'], 'L1_ffn_w2': _L1_ffn_in['w2'], 'L1_ffn_w3': _L1_ffn_in['w3']}

def reference(x, L0_conv_W_prep, L0_conv_b_prep, L0_conv_intrinsic, L0_conv_W_fin, L0_conv_b_fin, L0_ffn_gate_w, L0_ffn_gate_b, L0_ffn_W1, L0_ffn_b1, L0_ffn_W2, L0_ffn_b2, L1_conv_weights, L1_conv_pct, L1_conv_w, L1_ffn_router_w, L1_ffn_w1, L1_ffn_w2, L1_ffn_w3):
    import jax
    import jax.numpy as jnp

    def _L0_conv_ref(x, W_prep, b_prep, intrinsic, W_fin, b_fin):
        import jax, jax.numpy as jnp
        import numpy as np
        B, HIMG, WIMG, C = (2, 32, 32, 64)
        NH, HD = (8, 32)
        WH, WW = (8, 8)
        P = WH * WW
        NQK = 5
        S = 1 + HD + HD
        EPS = 1e-05

        def _spatial(intrinsic):
            ii = jnp.arange(WH)
            jj = jnp.arange(WW)
            ri = ii[:, None] - ii[None, :] + WH - 1
            rj = jj[:, None] - jj[None, :] + WW - 1
            rel = intrinsic[:, ri[:, None, :, None], rj[None, :, None, :], :]
            rel = rel.transpose(1, 2, 0, 3, 4, 5).reshape(P, NH, P, S)
            return (rel[..., 0], rel[..., 1:1 + HD], rel[..., 1 + HD:])
        t = x @ W_prep + b_prep
        nwh, nww = (HIMG // WH, WIMG // WW)
        wins = t.reshape(B, nwh, WH, nww, WW, NQK, NH, HD).transpose(0, 1, 3, 2, 4, 5, 6, 7)
        wins = wins.reshape(B * nwh * nww, P, NQK, NH, HD)
        wins = wins.transpose(2, 0, 3, 1, 4)
        q_n, q, k, k_m, v = (wins[i] for i in range(NQK))
        bias, pat_n, pat_m = _spatial(intrinsic)
        score = bias[None]
        score = score + jnp.einsum('bhod,ohid->bohi', q_n, pat_n)
        score = score + jnp.einsum('bhod,bhid->bohi', q, k)
        score = score + jnp.einsum('bhid,ohid->bohi', k_m, pat_m)
        mean = jnp.mean(score, axis=-1, keepdims=True)
        std = jnp.sqrt(jnp.var(score, axis=-1, ddof=1, keepdims=True) + EPS)
        score = (score - mean) / std
        out = jnp.einsum('bohi,bhid->bohd', score, v)
        out = out.reshape(B, nwh, nww, WH, WW, NH * HD).transpose(0, 1, 3, 2, 4, 5)
        out = out.reshape(B, HIMG, WIMG, NH * HD)
        return out @ W_fin + b_fin

    def _L0_ffn_ref(x, gate_w, gate_b, W1, b1, W2, b2):
        import jax, jax.numpy as jnp
        import numpy as np
        B, T, D, H, E = (16, 1024, 64, 128, 8)
        Bb, Tt, Dd = x.shape
        Ee = gate_w.shape[1]
        xf = x.reshape(-1, Dd)
        N = xf.shape[0]
        logits = xf @ gate_w + gate_b
        probs = jax.nn.softmax(logits, axis=-1)
        top2_vals, top2_idx = jax.lax.top_k(probs, 2)
        cw = jnp.zeros((N, Ee), dtype=xf.dtype).at[jnp.arange(N)[:, None], top2_idx].add(top2_vals)

        def step(acc, params):
            w1, bb1, w2, bb2, we = params
            h = jax.nn.gelu(xf @ w1 + bb1, approximate=False)
            y = h @ w2 + bb2
            return (acc + we[:, None] * y, None)
        out, _ = jax.lax.scan(step, jnp.zeros_like(xf), (W1, b1, W2, b2, cw.T))
        return out.reshape(Bb, Tt, Dd)

    def _L1_conv_ref(x, weights, pct, w):
        import jax, jax.numpy as jnp
        import numpy as np
        NLAT, NLON = (32, 64)
        CIN, COUT = (32, 32)
        MODES_LAT, MODES_LON = (32, 32)
        BATCH = 4

        def _legendre(lmax, mmax, x):
            npts = x.shape[0]
            pct = np.zeros((lmax, mmax, npts), dtype=np.float64)
            s = np.sqrt(1.0 - x * x)
            pmm = np.full(npts, np.sqrt(1.0 / (4.0 * np.pi)))
            for m in range(mmax):
                if m < lmax:
                    pct[m, m] = pmm
                    if m + 1 < lmax:
                        pct[m + 1, m] = x * np.sqrt(2.0 * m + 3.0) * pmm
                    for l in range(m + 2, lmax):
                        a = np.sqrt((4.0 * l * l - 1.0) / (l * l - m * m))
                        b = np.sqrt(((l - 1.0) ** 2 - m * m) / (4.0 * (l - 1.0) ** 2 - 1.0))
                        pct[l, m] = a * (x * pct[l - 1, m] - b * pct[l - 2, m])
                pmm = pmm * -np.sqrt((2.0 * m + 3.0) / (2.0 * m + 2.0)) * s
            return pct
        b, cin, nlat, nlon = x.shape
        mmax = nlon // 2 + 1
        xf = jnp.fft.rfft(x, axis=-1) * (2.0 * jnp.pi / nlon)
        x_spec = jnp.einsum('lmt,bctm->bclm', pct * w, xf)
        wc = (weights[..., 0] + 1j * weights[..., 1]).astype(jnp.complex64)
        ml = min(MODES_LAT, nlat)
        mj = min(MODES_LON, mmax)
        out_block = jnp.einsum('bilm,iolm->bolm', x_spec[:, :, :ml, :mj], wc[:, :, :ml, :mj])
        out_spec = jnp.zeros((b, wc.shape[1], nlat, mmax), jnp.complex64)
        out_spec = out_spec.at[:, :, :ml, :mj].set(out_block)
        xf_out = jnp.einsum('lmt,bclm->bctm', pct, out_spec)
        out = jnp.fft.irfft(xf_out, n=nlon, axis=-1) * nlon
        return out

    def _L1_ffn_ref(x, router_w, w1, w2, w3):
        import jax, jax.numpy as jnp
        import numpy as np
        N_EXPERTS = 8
        TOP_K = 2
        B, T, C = x.shape
        flat = x.reshape(-1, C)
        logits = flat @ router_w.T
        probs = jax.nn.softmax(logits, axis=-1)
        topk_probs, topk_idx = jax.lax.top_k(probs, TOP_K)
        topk_probs = topk_probs / (jnp.sum(topk_probs, axis=-1, keepdims=True) + 1e-09)
        onehot = jax.nn.one_hot(topk_idx, N_EXPERTS, dtype=flat.dtype)
        gates = jnp.einsum('nk,nke->ne', topk_probs, onehot)
        h1 = jnp.einsum('nc,ehc->neh', flat, w1)
        h3 = jnp.einsum('nc,ehc->neh', flat, w3)
        h = jax.nn.silu(h1) * h3
        y = jnp.einsum('neh,ech->nec', h, w2)
        out = jnp.einsum('ne,nec->nc', gates, y)
        return out.reshape(B, T, C)

    def _gn(v, G=32, eps=1e-05):
        B_, H_, W_, C_ = v.shape
        g = v.reshape(B_, H_, W_, G, C_ // G)
        m = jnp.mean(g, axis=(1, 2, 4), keepdims=True)
        s = jnp.var(g, axis=(1, 2, 4), keepdims=True)
        return ((g - m) / jnp.sqrt(s + eps)).reshape(v.shape)

    def _ln_c(v, eps=1e-06):
        m = jnp.mean(v, axis=-1, keepdims=True)
        s = jnp.var(v, axis=-1, keepdims=True)
        return (v - m) / jnp.sqrt(s + eps)

    def _ln_t(v, eps=1e-05):
        m = jnp.mean(v, axis=-1, keepdims=True)
        s = jnp.var(v, axis=-1, keepdims=True)
        return (v - m) / jnp.sqrt(s + eps)

    def _to_tokens(v):
        B_, H_, W_, C_ = v.shape
        return v.reshape(B_, H_ * W_, C_)

    def _from_tokens(t, like):
        return t.reshape(like.shape)
    x = x + _L0_conv_ref(_ln_c(x), L0_conv_W_prep, L0_conv_b_prep, L0_conv_intrinsic, L0_conv_W_fin, L0_conv_b_fin)
    t = _to_tokens(x)
    t = t + _L0_ffn_ref(_ln_t(t), L0_ffn_gate_w, L0_ffn_gate_b, L0_ffn_W1, L0_ffn_b1, L0_ffn_W2, L0_ffn_b2)
    x = _from_tokens(t, x)
    x = x + _L1_conv_ref(_ln_c(x), L1_conv_weights, L1_conv_pct, L1_conv_w)
    t = _to_tokens(x)
    t = t + _L1_ffn_ref(_ln_t(t), L1_ffn_router_w, L1_ffn_w1, L1_ffn_w2, L1_ffn_w3)
    x = _from_tokens(t, x)
    return x

_drawn_inputs = setup_inputs


def setup_inputs(seed=0):
    import zlib

    import numpy as np

    out = dict(_drawn_inputs(seed))
    spreads = {'L0_conv_b_prep': (0.0, 0.1),
     'L0_conv_b_fin': (0.0, 0.8),
     'L0_ffn_gate_b': (0.0, 0.8),
     'L0_ffn_b1': (0.0, 0.8),
     'L0_ffn_b2': (0.0, 0.8)}
    factors = {'L0_ffn_gate_w': 8.0,
     'L0_ffn_W1': 8.0,
     'L0_ffn_W2': 8.0,
     'L1_conv_weights': 8.0,
     'L1_conv_pct': 8.0,
     'L1_conv_w': 8.0,
     'L1_ffn_router_w': 3.792,
     'L1_ffn_w1': 3.599,
     'L1_ffn_w2': 3.383,
     'L1_ffn_w3': 3.387}
    for name, (base, spread) in spreads.items():
        noise = np.random.default_rng([zlib.crc32(name.encode()), seed]).standard_normal(out[name].shape)
        drawn = base * np.exp(spread * noise) if base else spread * noise
        out[name] = jnp.asarray(drawn.astype(out[name].dtype))
    for name, factor in factors.items():
        out[name] = (out[name] * factor).astype(out[name].dtype)
    return out
```

```python
from contextlib import ExitStack

import concourse.bass as bass
from concourse import mybir

ALU = mybir.AluOpType
ACT = mybir.ActivationFunctionType
F32 = mybir.dt.float32
F16 = mybir.dt.float16
AX_X = mybir.AxisListType.X

P = 128
B, HIMG, WIMG, C = 2, 32, 32, 64
NTOK = B * HIMG * WIMG
NT = NTOK // P
NG = 4
NH, HD, WIN = 8, 32, 8
PW = WIN * WIN
NW = NTOK // PW
REL = 2 * WIN - 1
BANK = 512
TWO_PI = 2.0 * 3.141592653589793
EPS_C, EPS_T, EPS_A = 1e-6, 1e-5, 1e-5


def build(nc, inp, out):
    ctx = ExitStack()
    with ctx:
        def sb(name, shape, dt=F32):
            return ctx.enter_context(nc.sbuf_tensor(name, shape, dt))

        def sem(name):
            return ctx.enter_context(nc.semaphore(name))

        ARENA = sb("arena", [P, 199 * 256], F32)

        def at(off, cols, dt=F32):
            size = 4 if dt == F32 else 2
            a = ARENA[:, off // 4:(off + cols * size) // 4]
            return a if dt == F32 else a.bitcast(dt)

        K = 1024
        X = at(0, 1024).rearrange("p (j c) -> p j c", c=C)
        XH = at(4 * K, NTOK, F16)
        XL = at(8 * K, NTOK, F16)
        xrow = at(12 * K, 4096, F16).rearrange("p (j s n) -> p j s n", s=2, n=2 * C)
        xc = at(20 * K, 1024).rearrange("p (j c) -> p j c", c=C)
        sq = at(24 * K, 1024).rearrange("p (j c) -> p j c", c=C)

        XHw = at(28 * K, 2 * NTOK, F16)
        XLw = at(36 * K, 2 * NTOK, F16)
        KH = at(44 * K, 8192, F16).rearrange("p (h b u y v) -> p h b u y v", h=2, b=NW, u=8, y=2)
        KL = at(60 * K, 8192, F16).rearrange("p (h b u y v) -> p h b u y v", h=2, b=NW, u=8, y=2)
        qh, ql, nh, nl, mh, ml = [at(76 * K + 4 * K * n, 2048, F16) for n in range(6)]
        ETB = 2 * 8 * REL * 16
        ENh, ENl = [at(100 * K + 2 * ETB * n, ETB, F16).rearrange("p (a w r) -> p a w r", a=2, w=8) for n in range(2)]
        AB = at(115 * K, 4096).rearrange("p (h o b) -> p h o b", h=2, o=PW)
        Ch = at(131 * K, 4096, F16).rearrange("p (b c) -> p b c", b=NW)
        Cl = at(139 * K, 4096, F16).rearrange("p (b c) -> p b c", b=NW)
        V = at(147 * K, 4096).rearrange("p (b h n) -> p b h n", h=2, n=64)
        S_ = [at((163 + 4 * n) * K, 1024) for n in range(3)]
        Sq = [at((175 + 4 * n) * K, 1024) for n in range(2)]
        EMh, EMl = [at(163 * K + 2 * ETB * n, ETB, F16).rearrange("p (a w r) -> p a w r", a=2, w=8) for n in range(2)]
        OTh = [at(183 * K + 8 * K * g, 2048, F16) for g in range(2)]
        OTl = [at(187 * K + 8 * K * g, 2048, F16) for g in range(2)]
        wpf, wpH = at(115 * K, 1280), at(121 * K, 1280, F16)
        wff = at(125 * K, 128).rearrange("p (g c) -> p g c", g=2)
        tblf = at(126 * K, 900)
        TH, TL = at(12 * K, 900, F16), at(14 * K, 900, F16)
        O32 = [at((20 + 2 * n) * K, BANK) for n in range(2)]
        rsc = [at((24 + 2 * n) * K, BANK) for n in range(2)]
        WP = sb("WP", [P, 1280], F16)
        biasT = sb("biasT", [P, 4, PW])
        CEN = sb("cen", [P, P])
        VAR = sb("varm", [P, PW])
        wfh = sb("wfh", [P, 2, C], F16)
        wfl = sb("wfl", [P, 2, C], F16)

        WC = [at(o * K, 2048).rearrange("p (m q n) -> p m q n", m=4, q=8) for o in (28, 36, 88, 96, 44, 52, 60, 68)]
        Z3 = at(28 * K, 3072).rearrange("p (m n) -> p m n", n=96)
        GI = at(82 * K, 512).rearrange("p (r n) -> p r n", r=2)
        W1g = at(84 * K, 1024, F16)
        W2gh = at(86 * K, 512, F16)
        W2gl = at(87 * K, 512, F16)
        w1gf, w2gf, w1gH = at(104 * K, 1024), at(108 * K, 512), at(110 * K, 1024, F16)
        SX = at(108 * K, 8192).rearrange("p (m q n) -> p m q n", q=8, n=32)
        SXF = at(108 * K, 8192)
        stage = [at((112 + 3 * n) * K, 768) for n in range(4)]
        stageH = [at(124 * K + 1536 * n, 768, F16) for n in range(4)]
        PRI = [at((140 + 8 * n) * K, 2048).rearrange("p (m b t) -> p m b t", b=2, t=32) for n in range(2)]
        pctr = at(76 * K, 1024).rearrange("p (m t) -> p m t", t=32)
        pctf = at(168 * K, 1024)[0:64, :].rearrange("p (m l) -> p m l", l=32)
        b2f, b2H = at(112 * K, 512)[0:2, :], at(114 * K, 512, F16)[0:2, :]
        PCTW = at(156 * K, 2048).rearrange("p (m b l) -> p m b l", b=2, l=32)
        XF = at(164 * K, 2048).rearrange("p (m r i) -> p m r i", r=2, i=32)
        Y = at(156 * K, 2048).rearrange("p (r o m) -> p r o m", r=2, o=32)
        YT = at(164 * K, 1024).rearrange("p (g r n) -> p g r n", r=2, n=64)
        g32 = [at((156 + 2 * n) * K, 512) for n in range(2)]
        gh = [at((160 + n) * K, 512, F16) for n in range(2)]
        gl = [at((162 + n) * K, 512, F16) for n in range(2)]
        tmp = at(164 * K, 512)
        W13 = at(172 * K, 12288, F16).rearrange("p (e w n) -> p e w n", e=8, w=2)
        w2f = at(44 * K, 3072)
        W2h, W2l = at(56 * K, 3072, F16), at(62 * K, 3072, F16)
        s32 = [at((84 + 2 * n) * K, 512) for n in range(2)]
        lg, eq, sc, oh1, l2, oh2, ex, cw = [at(24 * K + 512 * n, 128).rearrange("p (j e) -> p j e", e=8)
                                            for n in range(8)]

        ident = sb("ident", [P, P], F16)
        sel = sb("sel", [P, P], F16)
        mask = sb("mask", [P, 16])
        bprep = sb("bprep", [P, 8])
        bfin = sb("bfin", [P, C])
        bv2f, bv2h = at(130 * K, 256)[0:2, :], at(125 * K + 512, 256, F16)[0:2, :]
        b2r = sb("b2r", [2, 512], F16)
        small = sb("small", [P, 64])
        g0w, g1w, g0b, b1c, idxw = [small[:, 8 * n:8 * n + 8] for n in range(5)]
        wlat, pmask, wb = small[:, 40:41], small[:, 42:46], small[:, 46:48]
        identf = sb("identf", [64, 64])
        GH = sb("gateH", [P, 16], F16)
        GW = sb("gateW", [P, 16], F16)
        FW = sb("dftw", [P, 64], F16)
        red = sb("red", [P, C])
        m1, m2, sm = [sb(n, [P, NT]) for n in ("m1", "m2", "sm")]
        bv2 = sb("bv2", [2, 256], F16)
        ones2 = sb("ones2", [2, P], F16)
        mu = sb("mu", [P, NT])
        var = sb("var", [P, NT])
        dev = sb("dev", [P, NT])

        PS = ctx.enter_context(nc.psum_tensor("ps", [P, 8 * BANK], F32))

        def bank(n, m=1):
            return PS[:, n * BANK:(n + m) * BANK]

        ld_x, ld_wp, ld_tbl, ld_small, st_out = sem("ld_x"), sem("ld_wp"), sem("ld_tbl"), sem("ld_small"), sem("st_out")
        vec = sem("vec_step")
        ln_xc, ln_sq, ln_xn, ln_hi, ln_lo, ln_tp, xs_rdy = [sem(s) for s in (
            "ln_centred", "ln_squared", "ln_normed", "ln_hi", "ln_lo", "ln_transposed", "xs_ready")]
        wp_hi, wp_rdy, tb_hi, tb_rdy, wf_hi, wf_rdy = [sem(s) for s in (
            "wprep_hi", "wprep_ready", "table_hi", "table_ready", "wfin_hi", "wfin_ready")]
        zeroed, unit_rdy, unit_hi, unit_free, k_spread = [sem(s) for s in (
            "zeroed", "unit_ready", "unit_hi", "unit_free", "k_spread")]
        st_rdy, s_added, mean_rdy, centred, squared, sv_rdy, o_read, o_hi, o_lo = [sem(s) for s in (
            "scores_ready", "scores_added", "mean_ready", "scores_centred", "scores_squared", "sv_ready",
            "o_read", "o_hi", "o_lo")]
        bfin_added, proj_rdy, x_rdy = sem("bfin_added"), sem("proj_ready"), sem("x_ready")
        bv_hi, ln_var, ln_dev, std_rdy = sem("bv_hi"), sem("ln_var"), sem("ln_dev"), sem("std_ready")
        en_hi, en_lo, em_hi, em_lo, v_free = [sem(s) for s in ("en_hi", "en_lo", "em_hi", "em_lo", "v_free")]

        LD_SMALL = 14 * 16
        XD = {1: 2, 2: 2 + 16, 3: 2 + 16 + 2}
        XD[4] = XD[3] + 16

        ld_f0, ld_wc, ld_gi, ld_pc, ld_st, ld_w2 = (sem("ld_f0"), [sem(f"ld_wc{n}") for n in range(8)], sem("ld_gi"),
                                                    sem("ld_pct"), [sem(f"ld_stage{n}") for n in range(4)], sem("ld_w2"))
        f0_hi, f0_rdy, gh_hi = sem("ffn0_weights_hi"), sem("ffn0_weights_ready"), sem("gates_hi")
        gw_rdy, st_hi, st_done, wb_rdy = sem("gate_weights_ready"), sem("stage_hi"), sem("stage_done"), sem("wb_ready")
        lg_rdy, lg_read, ex_in, ex_rdy = sem("logits_ready"), sem("logits_read"), sem("exp_in"), sem("exp_ready")
        h_rdy, g_rdy, g_hi, g_lo, y_used, y_rdy, y_read = [sem(n) for n in (
            "h_ready", "g_ready", "g_hi", "g_lo", "y_used", "y_ready", "y_read")]
        sx_zero, pri_rdy, pw_rdy = sem("sx_zero"), sem("pri_ready"), sem("pctw_ready")
        a_rdy, xf_rdy, b_rdy, sx_act, sx_dve, c_rdy, z_act, z_dve, d_rdy, yt_in, t_rdy, yt_rdy, e_rdy = [sem(n) for n in (
            "a_ready", "xf_ready", "b_ready", "sx_act", "sx_dve", "c_ready", "z_act", "z_dve", "d_ready", "y_whole",
            "t_ready", "yt_ready", "e_ready")]
        w2_hi, w2_rdy, s_rdy, h3_rdy = sem("w2_hi"), sem("w2_ready"), sem("silu_ready"), sem("h3_ready")
        hh_rdy, gg_rdy, gg_hi, gg_lo, yy_used, yy_rdy, yy_read = [sem(n) for n in (
            "hh_ready", "gg_ready", "gg_hi", "gg_lo", "yy_used", "yy_ready", "yy_read")]

        def spectrum(k):
            return XF[0:64].rearrange("p m r i -> p (m r) i")[:, :, 8 * k:8 * k + 8].rearrange("p n i -> p i n")

        def mixing(n):
            quad, g = n // 4, n % 4
            mh, r = quad // 2, quad % 2
            src = PS[32 * quad:32 * quad + 32, 0:1024].rearrange("p (m b q l) -> p m b q l", m=16, b=2, l=4)[:, :, :, :, g]
            dst = SX[32 * g:32 * g + 32, 16 * mh:16 * mh + 16, :, 4 * g + r:4 * g + 4:2]
            return dst.rearrange("p m q b -> p m b q"), src

        def modes(mb):
            return Y[0:64].rearrange("p r o m -> p (r o) m")[:, :, 8 * mb:8 * mb + 8].rearrange("p n m -> p m n")

        def bcol(kind, hg):
            return bprep[:, 2 * TYPE[kind] + hg:2 * TYPE[kind] + hg + 1]

        def wk(KX, hp, b):
            return KX[:, hp, b, :, :, :].rearrange("p u y v -> p (u y v)")

        def windowed(dst, g, j, y):
            j0 = 4 * g
            return bass.AP(dst.tensor, dst.offset + (j0 // 8) * 2048 + (j0 % 8) * 16 + 8 * y,
                           [list(dst.ap[0]), [16, 4], [P, 16], [1, 8]])

        def XW(xs, k):
            return xs[:, k * BANK:(k + 1) * BANK]

        def cols_c(CX, k):
            v = CX.rearrange("p b (u y v) -> p u y v b", u=8, y=2)
            return v[:, 2 * (k % 4):2 * (k % 4) + 2, k // 4, :, :]

        def ots(OT, hg, c):
            return OT[hg].rearrange("p (j q) -> p j q", q=P)[:, (c // 2) * 8:(c // 2) * 8 + 8,
                                                            (c % 2) * 64:(c % 2) * 64 + 64]

        ORDER = [("n", k) for k in range(4)] + [("m", k) for k in range(4)]
        for k in range(8):
            ORDER += [("a", k), ("kq"[k // 4], k % 4)]
        for k in range(8):
            ORDER += [("c", k), ("v", k)]
        UNITS = len(ORDER)
        TYPE = {"n": 0, "q": 1, "k": 2, "m": 3}

        def count(kinds, hg, n):
            return hg * sum(u in kinds for u, _ in ORDER) + sum(u in kinds for u, _ in ORDER[:n + 1])

        def last(kind):
            return max(n for n, (u, _) in enumerate(ORDER) if u == kind)

        def spread(eng, src, t, hg, c, hi):
            E = (EMh if hi else EMl) if t else (ENh if hi else ENl)
            off = (2 * t + hg) * REL * REL + 7
            view = bass.AP(src.tensor, src.offset + off, [list(src.ap[0]), [-1, 8], [REL, REL], [1, 8]])
            outer, inner = (c % 2, c // 2) if t else (c // 2, c % 2)
            dst = E[:, outer, :, :].rearrange("p w (r y v) -> p w r y v", y=2, v=8)[:, :, :, inner, :]
            if hi:
                return eng.mul(dst, view, mask[:, c:c + 1])
            return eng.tensor_scalar(dst, view, mask[:, c:c + 1], None, ALU.mult)

        def diagonal(KX, c, k):
            return KX[32 * c:32 * c + 32, c // 2, 8 * k:8 * k + 8, :, c % 2, :].rearrange("p b u v -> p (b u) v")

        block = ctx.enter_context(nc.Block())

        @block.sync
        def _(sp):
            sp.dma_start(X, inp["x"].rearrange("p (j c) -> p j c", c=C)).then_inc(ld_x, 16)
            sp.dma_start(wpf, inp["wprep"]).then_inc(ld_wp, 16)
            for dst, src in ((ident[:], "ident"), (mask[:], "mask"), (bprep[:], "bprep"), (bfin[:], "bfin"),
                             (biasT[:].rearrange("p h o -> p (h o)"), "biasT"), (CEN[:], "cen"), (VAR[:], "varm"),
                             (wff.rearrange("p g c -> p (g c)"), "wfin"), (sel[:], "sel"), (bv2f, "bv"),
                             (ones2[:], "ones"), (small[:], "small"), (identf[:], "identf"), (FW[:], "dft")):
                sp.dma_start(dst, inp[src]).then_inc(ld_small, 16)
            sp.dma_start(tblf, inp["tables"]).then_inc(ld_tbl, 16)
            sp.wait_ge(unit_rdy, 2 * UNITS)
            for dst, src in ((w1gf, "w1g"), (w2gf, "w2g"), (b2f, "b2g")):
                sp.dma_start(dst, inp[src]).then_inc(ld_f0, 16)

            def load_weights(n):
                sp.dma_start(WC[n].rearrange("p m q n -> p (m q n)"),
                             inp["wc"][:, 2048 * n:2048 * (n + 1)]).then_inc(ld_wc[n], 16)

            for n in range(4):
                load_weights(n)
            sp.wait_ge(st_rdy, 8)
            sp.dma_start(pctr.rearrange("p m t -> p (m t)"), inp["pctr"]).then_inc(ld_pc, 16)
            sp.dma_start(GI.rearrange("p r n -> p (r n)"), inp["gi"]).then_inc(ld_gi, 16)
            for n in range(4, 8):
                load_weights(n)
            sp.wait_ge(x_rdy, 2)
            sp.dma_start(pctf.rearrange("p m l -> p (m l)"), inp["pctt"]).then_inc(ld_pc, 16)
            sp.wait_ge(f0_rdy, 1)
            for n in range(16):
                if n >= 4:
                    sp.wait_ge(st_done, n - 3)
                sp.dma_start(stage[n % 4], inp["w13"][:, 768 * n:768 * (n + 1)]).then_inc(ld_st[n % 4], 16)
            sp.wait_ge(c_rdy, 4)
            sp.dma_start(w2f, inp["w2"]).then_inc(ld_w2, 16)
            sp.wait_ge(x_rdy, XD[4])
            sp.dma_start(out.rearrange("p (j c) -> p j c", c=C), X).then_inc(st_out, 16)
            sp.wait_ge(st_out, 16)

        @block.tensor
        def _(pe):
            def norm_transposes(L):
                if L == 0:
                    pe.wait_ge(ld_small, LD_SMALL)
                for g in range(NG):
                    pe.wait_ge(ln_lo, NG * L + g + 1)
                    if g >= 2:
                        pe.wait_ge(xs_rdy, NG * L + g - 1)
                    elif L:
                        pass
                    for s in range(2):
                        dst = bank(2 * (g % 2) + s).bitcast(F16)
                        for j in range(4):
                            mm = pe.transpose(dst[:, j * P:(j + 1) * P], xrow[:, 4 * g + j, s, :], ident[:])
                    mm.then_inc(ln_tp, 1)

            def attention():
                pe.wait_ge(wp_rdy, 1)
                pe.wait_ge(xs_rdy, NG)
                for hg in range(2):
                    if hg:
                        pe.wait_ge(s_added, 4)
                        pe.wait_ge(centred, 4)
                        pe.wait_ge(o_read, 4)
                    for n, (kind, k) in enumerate(ORDER):
                        N = hg * UNITS + n
                        o = bank(N % 8)
                        if n >= 8:
                            if ORDER[n - 8][0] == "v":
                                pe.wait_ge(v_free, count("v", hg, n - 8))
                            else:
                                pe.wait_ge(unit_free, count("nmqkac", hg, n - 8))
                        if kind in "nmqk":
                            col = TYPE[kind] * 256 + hg * P
                            for i, xs in enumerate((XHw, XLw)):
                                mv = xs[:, k * 1024:(k + 1) * 1024].rearrange("p (b y v) -> p b y v", y=2, v=8)[:, :, 0, :]
                                mm = pe.matmul(o, WP[:, col:col + P], mv, start=(i == 0), stop=(i == 1))
                        elif kind == "v":
                            for b4 in range(4):
                                b = 4 * k + b4
                                ob = o[:, b4 * P:(b4 + 1) * P]
                                for i, xs in enumerate((XHw, XLw)):
                                    pe.matmul(ob, xs[:, b * P:(b + 1) * P],
                                              WP[:, 1024 + hg * P:1024 + (hg + 1) * P], start=(i == 0), stop=False)
                                mm = pe.matmul(ob, ones2[:], bv2[:, hg * P:(hg + 1) * P], start=False, stop=True)
                        elif kind == "a":
                            if k == 0:
                                pe.wait_ge(unit_free, count("nmqkac", hg, last("n")))
                                pe.wait_ge(en_hi, hg + 1)
                                pe.wait_ge(en_lo, hg + 1)
                            for o16 in range(16):
                                oi, oj = divmod((k % 4) * 16 + o16, 8)
                                for i, (tab, mv) in enumerate(((ENh, nh), (ENh, nl), (ENl, nh))):
                                    mm = pe.matmul(o[:, o16 * NW:(o16 + 1) * NW],
                                                   tab[:, k // 4, oj, (7 - oi) * 16:(15 - oi) * 16],
                                                   mv[:, 8 * oi + oj::PW], start=(i == 0), stop=(i == 2))
                        else:
                            if k == 0:
                                pe.wait_ge(em_hi, hg + 1)
                                pe.wait_ge(em_lo, hg + 1)
                            for i16 in range(16):
                                ii, ij = divmod((k % 4) * 16 + i16, 8)
                                for i, (tab, mv) in enumerate(((EMh, mh), (EMh, ml), (EMl, mh))):
                                    mm = pe.matmul(o[:, i16 * NW:(i16 + 1) * NW],
                                                   tab[:, k // 4, ij, (7 - ii) * 16:(15 - ii) * 16],
                                                   mv[:, 8 * ii + ij::PW], start=(i == 0), stop=(i == 2))
                        mm.then_inc(unit_rdy, 1)

                    def scores(c):
                        cg = hg * 4 + c
                        if c == 0:
                            pe.wait_ge(unit_free, count("nmqkac", hg, UNITS - 1))
                            pe.wait_ge(v_free, count("v", hg, UNITS - 1))
                        if cg >= 2:
                            pe.wait_ge(s_added, cg - 1)
                        for b8 in range(8):
                            b = c * 8 + b8
                            for hp in range(2):
                                o = bank(2 * (cg % 2) + hp)[:, b8 * PW:(b8 + 1) * PW]
                                qs = slice(b * PW, (b + 1) * PW)
                                pe.matmul(o, wk(KH, hp, b), qh[:, qs], start=True, stop=False)
                                pe.matmul(o, wk(KH, hp, b), ql[:, qs], start=False, stop=False)
                                pe.matmul(o, wk(KL, hp, b), qh[:, qs], start=False, stop=False)
                                idn = sel[:, hp * PW:(hp + 1) * PW]
                                pe.matmul(o, Ch[:, b, :], idn, start=False, stop=False)
                                mm = pe.matmul(o, Cl[:, b, :], idn, start=False, stop=True)
                        mm.then_inc(st_rdy, 1)

                    def means(c):
                        cg = hg * 4 + c
                        pe.wait_ge(s_added, cg + 1)
                        if cg >= 1:
                            pe.wait_ge(centred, cg)
                        for hp in range(2):
                            mm = pe.matmul(bank(4 + hp), CEN[:], S_[cg % 3][:, hp * BANK:(hp + 1) * BANK],
                                           start=True, stop=True)
                        mm.then_inc(mean_rdy, 1)

                    def values(c):
                        cg = hg * 4 + c
                        pe.wait_ge(centred, cg + 1)
                        if cg >= 1:
                            pe.wait_ge(o_read, cg)
                        for b8 in range(8):
                            for hp in range(2):
                                pe.matmul(bank(6)[64 * hp:64 * hp + 64, b8 * PW:(b8 + 1) * PW],
                                          V[:, c * 8 + b8, hp, :],
                                          S_[cg % 3][:, hp * BANK + b8 * PW:hp * BANK + (b8 + 1) * PW],
                                          start=True, stop=True)
                        pe.wait_ge(squared, cg + 1)
                        for hp in range(2):
                            mm = pe.matmul(bank(7)[64 * hp:64 * hp + 64, :], VAR[:],
                                           Sq[cg % 2][:, hp * BANK:(hp + 1) * BANK], start=True, stop=True)
                        mm.then_inc(sv_rdy, 1)

                    for c in range(4 + 2):
                        if c < 4:
                            scores(c)
                        if 1 <= c < 5:
                            means(c - 1)
                        if c >= 2:
                            values(c - 2)
                pe.wait_ge(o_lo, 8)
                pe.wait_ge(wf_rdy, 1)
                for j in range(NT):
                    o = bank(j // 8)[:, (j % 8) * C:(j % 8 + 1) * C]
                    n = 0
                    for hg in range(2):
                        ts = slice(j * P, (j + 1) * P)
                        for a, w in ((OTh, wfh), (OTl, wfh), (OTh, wfl)):
                            mm = pe.matmul(o, a[hg][:, ts], w[:, hg, :], start=(n == 0), stop=(n == 5))
                            n += 1
                    if j % 8 == 7:
                        mm.then_inc(proj_rdy, 1)

            def ffn0():
                pe.wait_ge(xs_rdy, 2 * NG)
                pe.wait_ge(gw_rdy, 1)
                logits(0, bank(7))
                pe.wait_ge(f0_rdy, 1)

                def hidden(it):
                    blk, e = divmod(it, 8)
                    if it >= 2:
                        pe.wait_ge(g_rdy, it - 1)
                    for i, xs in enumerate((XH, XL)):
                        mm = pe.matmul(bank(it % 2), W1g[:, e * P:(e + 1) * P], XW(xs, blk), start=(i == 0), stop=(i == 1))
                    mm.then_inc(h_rdy, 1)

                def outputs(it):
                    blk, e = divmod(it, 8)
                    pe.wait_ge(g_lo, it + 1)
                    for jt in range(4):
                        t = 4 * blk + jt
                        o = bank(2 + t % 6)
                        if e == 0:
                            if t == 5:
                                pe.wait_ge(lg_read, 1)
                            if t >= 6:
                                pe.wait_ge(y_read, t - 5)
                            pe.matmul(o, ones2[:], b2r[:], start=True, stop=False)
                        for i, (a, w) in enumerate(((gh, W2gh), (gl, W2gh), (gh, W2gl))):
                            mm = pe.matmul(o[:, e * C:(e + 1) * C], a[it % 2][:, jt * P:(jt + 1) * P],
                                           w[:, e * C:(e + 1) * C], start=False, stop=(e == 7 and i == 2))
                    mm.then_inc(y_used, 1)

                for it in range(32 + 2):
                    if it < 32:
                        hidden(it)
                    if it >= 2:
                        outputs(it - 2)

            def logits(n, o):
                for j in range(NT):
                    for i, xs in enumerate((XH, XL)):
                        mm = pe.matmul(o[:, 8 * j:8 * j + 8], xs[:, j * P:(j + 1) * P], GW[:, 8 * n:8 * n + 8],
                                       start=(i == 0), stop=(i == 1))
                mm.then_inc(lg_rdy, 1)

            def convolution():
                pe.wait_ge(xs_rdy, 3 * NG)
                for k in range(4):
                    for i8 in range(8):
                        i = 8 * k + i8
                        col = (i % 16) * P + (i // 16) * 64
                        for n, xs in enumerate((XH, XL)):
                            mm = pe.matmul(bank(4 + k)[0:64, i8 * 64:(i8 + 1) * 64], xs[:, col:col + 64], FW[:],
                                           start=(n == 0), stop=(n == 1))
                    mm.then_inc(a_rdy, 1)
                pe.wait_ge(xf_rdy, 4)
                pe.wait_ge(pw_rdy, 1)
                for m16 in range(16):
                    for mh in range(2):
                        m = 16 * mh + m16
                        mm = pe.matmul(PS[64 * mh:64 * mh + 64, m16 * 64:(m16 + 1) * 64],
                                       XF[:, m, :, :].rearrange("p r i -> p (r i)")[0:64],
                                       PCTW[:, m, :, :].rearrange("p b l -> p (b l)")[0:64], start=True, stop=True)
                mm.then_inc(b_rdy, 1)
                pe.wait_ge(sx_act, 1)
                pe.wait_ge(sx_dve, 1)
                for mb in range(4):
                    for m8 in range(8):
                        m = 8 * mb + m8
                        if m % 4 == 0:
                            pe.wait_ge(ld_wc[m // 4], 16)
                        for q in range(2):
                            for g in range(4):
                                lq = 2 * g + q
                                base = (m * 8 + lq) * 32 - 16 * q
                                mm = pe.matmul(bank(2 + mb)[32 * g:32 * g + 32, m8 * 64:(m8 + 1) * 64],
                                               SXF[:, base:base + 32], WC[m // 4][:, m % 4, lq, :],
                                               start=(q == 0), stop=(q == 1))
                    mm.then_inc(c_rdy, 1)
                pe.wait_ge(pri_rdy, 1)
                for mb in range(4):
                    pe.wait_ge(z_act, mb + 1)
                    pe.wait_ge(z_dve, mb + 1)
                    for m8 in range(8):
                        m = 8 * mb + m8
                        o = bank((6, 7, 0, 1)[mb])[0:64, m8 * 64:(m8 + 1) * 64]
                        for n, c0 in ((0, 32), (1, 0)):
                            mm = pe.matmul(o, PRI[n][:, m, :, :].rearrange("p b t -> p (b t)"), Z3[:, m, c0:c0 + 64],
                                           start=(n == 0), stop=(n == 1))
                    mm.then_inc(d_rdy, 1)
                pe.wait_ge(yt_in, 4)
                for og in range(8):
                    for r in range(2):
                        mm = pe.transpose(PS[:, 2 * BANK + (2 * og + r) * 64:2 * BANK + (2 * og + r + 1) * 64],
                                          Y[0:64, r, 4 * og:4 * og + 4, :].rearrange("p o m -> p (o m)"), identf[:])
                    if og % 4 == 3:
                        mm.then_inc(t_rdy, 1)
                pe.wait_ge(ld_gi, 16)
                for n in range(2):
                    pe.wait_ge(yt_rdy, 2)
                    for og4 in (2 * n, 2 * n + 1):
                        for r in range(2):
                            for b in range(2):
                                for oh in range(2):
                                    q = 64 * b + 32 * oh
                                    mm = pe.matmul(bank(4 + n)[q:q + 32, (og4 % 2) * 256:(og4 % 2) * 256 + 256],
                                                   YT[:, 4 * oh + og4, r, 32 * b:32 * b + 32], GI[:, r, :],
                                                   start=(r == 0), stop=(r == 1))
                    mm.then_inc(e_rdy, 1)

            def ffn1():
                pe.wait_ge(xs_rdy, 4 * NG)
                logits(1, bank(7))

                def hidden(it):
                    blk, e, c = it // 48, it // 6 % 8, it % 6
                    for w in range(2):
                        if it >= 2:
                            pe.wait_ge((s_rdy, gg_rdy)[w], it - 1)
                        for i, xs in enumerate((XH, XL)):
                            mm = pe.matmul(bank(2 * w + it % 2), W13[:, e, w, c * P:(c + 1) * P], XW(xs, blk),
                                           start=(i == 0), stop=(i == 1))
                        mm.then_inc((hh_rdy, h3_rdy)[w], 1)

                def outputs(it):
                    blk, e, c = it // 48, it // 6 % 8, it % 6
                    pe.wait_ge(gg_lo, it + 1)
                    for jt in range(4):
                        t = 4 * blk + jt
                        o = bank(4 + jt)
                        if it % 48 == 0:
                            if t >= 4:
                                pe.wait_ge(yy_read, t - 3)
                            elif t == 3:
                                pe.wait_ge(lg_read, 2)
                        for i, (a, w) in enumerate(((gh, W2h), (gl, W2h), (gh, W2l))):
                            mm = pe.matmul(o[:, e * C:(e + 1) * C], a[it % 2][:, jt * P:(jt + 1) * P],
                                           w[:, (e * 6 + c) * C:(e * 6 + c + 1) * C],
                                           start=(c == 0 and i == 0), stop=(c == 5 and i == 2))
                    mm.then_inc(yy_used, 1)

                pe.wait_ge(st_done, 16)
                for it in range(192 + 2):
                    if it < 192:
                        hidden(it)
                    if it == 2:
                        pe.wait_ge(w2_rdy, 1)
                    if it >= 2:
                        outputs(it - 2)

            norm_transposes(0)
            attention()
            norm_transposes(1)
            ffn0()
            norm_transposes(2)
            convolution()
            norm_transposes(3)
            ffn1()

        @block.scalar
        def _(act):
            def norm(L, eps, window_order):
                for g in range(NG):
                    act.wait_ge(ln_xc, NG * L + g + 1)
                    act.activation(sq[:, 4 * g:4 * g + 4, :], xc[:, 4 * g:4 * g + 4, :], ACT.Square,
                                   scale=1.0 / 8).then_inc(ln_sq, 1)
                for g in range(NG):
                    act.wait_ge(ln_var, NG * L + g + 1)
                    act.activation(dev[:, 4 * g:4 * g + 4], var[:, 4 * g:4 * g + 4], ACT.Sqrt,
                                   bias=mask[:, eps:eps + 1]).then_inc(ln_dev, 1)
                for g in range(NG):
                    act.wait_ge(ln_xn, NG * L + g + 1)
                    src = xc[:, 4 * g:4 * g + 4, :].unsqueeze(2).broadcast_to([P, 4, 2, C])
                    act.copy(xrow[:, 4 * g:4 * g + 4, 0, :].rearrange("p j (n c) -> p j n c", n=2), src).then_inc(ln_hi, 1)
                for g in range(NG):
                    act.wait_ge(ln_tp, NG * L + g + 1)
                    for s, (dst, win) in enumerate(((XH, XHw), (XL, XLw))):
                        src = bank(2 * (g % 2) + s).bitcast(F16)[:, 0:BANK]
                        if window_order:
                            for y in range(2):
                                ins = act.copy(windowed(win, g, 0, y), src.rearrange("p (j b v) -> p j b v", j=4, v=8))
                        elif L == 2:
                            for b in range(2):
                                d = dst[:, g * BANK:(g + 1) * BANK].rearrange("p (j o b t) -> p j o b t", j=4, o=2, b=2)
                                ins = act.copy(d[:, :, :, b, :],
                                               src.rearrange("p (j b o t) -> p j b o t", j=4, b=2, o=2)[:, :, b, :, :])
                        else:
                            ins = act.copy(dst[:, g * BANK:(g + 1) * BANK], src)
                    ins.then_inc(xs_rdy, 1)

            act.wait_ge(ld_wp, 16)
            act.copy(wpH, wpf).then_inc(wp_hi, 1)
            act.wait_ge(ld_small, LD_SMALL)
            norm(0, 8, True)
            act.wait_ge(ld_tbl, 16)
            act.wait_ge(ln_tp, NG)
            act.copy(TH, tblf).then_inc(tb_hi, 1)
            act.wait_ge(tb_hi, 1)
            for c in range(4):
                ins = spread(act, TH, 0, 0, c, True)
            ins.then_inc(en_hi, 1)
            act.copy(bv2h, bv2f).then_inc(bv_hi, 1)
            act.copy(wfh[:], wff).then_inc(wf_hi, 1)
            for hg in range(2):
                for n, (kind, k) in enumerate(ORDER):
                    if (kind, k) == ("a", 4):
                        if hg:
                            act.wait_ge(sv_rdy, 4)
                        for c in range(4):
                            ins = spread(act, TH, 1, hg, c, True)
                        ins.then_inc(em_hi, 1)
                    if kind == "a":
                        continue
                    N = hg * UNITS + n
                    o = bank(N % 8)
                    act.wait_ge(unit_rdy, N + 1)
                    if kind in "nmq":
                        dst = {"n": nh, "m": mh, "q": qh}[kind]
                        ins = act.activation(XW(dst, k), o, ACT.Identity, bias=bcol(kind, hg))
                    elif kind == "k":
                        if hg == 0 and k == 0:
                            act.wait_ge(zeroed, 2)
                        for c in range(4):
                            r = slice(32 * c, 32 * c + 32)
                            ins = act.activation(diagonal(KH, c, k), o[r, :].rearrange("p (b v) -> p b v", v=8),
                                                 ACT.Identity, bias=bcol(kind, hg)[r, :])
                    elif kind == "v":
                        src = o.rearrange("p (b n) -> p b n", n=HD)
                        for y in range(2):
                            ins = act.mul(V[:, 4 * k:4 * k + 4, :, 32 * y:32 * y + 32].rearrange("p b h d -> p (b h) d"),
                                          src[:, y::2, :], mask[:, 5 + y:6 + y])
                    else:
                        ins = act.copy(cols_c(Ch, k), o.rearrange("p (u v b) -> p u v b", u=2, b=NW))
                    ins.then_inc(v_free if kind == "v" else unit_hi, 1)
                for c in range(6):
                    if c < 4 and hg == 0:
                        ins = spread(act, TH, 0, 1, c, True)
                        if c == 3:
                            ins.then_inc(en_hi, 1)
                    if c >= 2:
                        cg = hg * 4 + c - 2
                        act.wait_ge(sv_rdy, cg + 1)
                        if cg >= 2:
                            act.wait_ge(o_read, cg - 1)
                        act.activation(rsc[cg % 2], bank(7), ACT.Sqrt, bias=mask[:, 7:8]).then_inc(std_rdy, 1)
                        act.wait_ge(o_read, cg + 1)
                        act.copy(ots(OTh, hg, c - 2), O32[cg % 2].rearrange("p (j t) -> p j t", t=64)).then_inc(o_hi, 1)

            def expert_stage(n):
                act.wait_ge(ld_st[n % 4], 16 * (n // 4 + 1))
                act.copy(stageH[n % 4], stage[n % 4]).then_inc(st_hi, 1)

            def ffn0():
                act.copy(GH[:], small[:, 0:16]).then_inc(gh_hi, 1)
                act.wait_ge(ld_f0, 48)
                act.copy(w1gH, w1gf)
                act.copy(W2gh, w2gf)
                act.copy(b2H, b2f).then_inc(f0_hi, 1)

            def gates():
                act.wait_ge(ex_in, gates.n + 1)
                gates.n += 1
                act.activation(ex, ex, ACT.Exp).then_inc(ex_rdy, 1)
            gates.n = 0

            def ffn0_main():
                for it in range(32):
                    e = it % 8
                    act.wait_ge(h_rdy, it + 1)
                    if it >= 2:
                        act.wait_ge(g_lo, it - 1)
                    act.activation(g32[it % 2], bank(it % 2), ACT.Gelu, bias=b1c[:, e:e + 1]).then_inc(g_rdy, 1)
                    if it % 2 == 1:
                        expert_stage(it // 2)

            def convolution():
                act.wait_ge(wb_rdy, 1)
                act.wait_ge(ld_pc, 32)
                act.wait_ge(y_read, NT)
                for b in range(2):
                    ins = act.mul(PCTW[0:64, :, b, :], pctf, wb[0:64, b:b + 1])
                ins.then_inc(pw_rdy, 1)
                norm(2, 8, False)
                act.wait_ge(pw_rdy, 1)
                for k in (0, 2):
                    act.wait_ge(a_rdy, k + 1)
                    act.copy(spectrum(k), bank(4 + k)[0:64, :].rearrange("p (i n) -> p i n", i=8)).then_inc(xf_rdy, 1)
                act.wait_ge(b_rdy, 1)
                act.wait_ge(sx_zero, 1)
                for n in range(8):
                    ins = act.copy(*mixing(n))
                ins.then_inc(sx_act, 1)
                for mb in range(4):
                    act.wait_ge(c_rdy, mb + 1)
                    act.copy(Z3[:, 8 * mb:8 * mb + 8, 32:96],
                             bank(2 + mb).rearrange("p (m n) -> p m n", n=64)).then_inc(z_act, 1)
                act.wait_ge(xf_rdy, 4)
                for mb in (0, 2):
                    act.wait_ge(d_rdy, mb + 1)
                    act.copy(modes(mb), bank((6, 7, 0, 1)[mb])[0:64, :].rearrange("p (m n) -> p m n", n=64)).then_inc(yt_in, 1)
                act.wait_ge(t_rdy, 1)
                act.copy(YT[:, 0:4, :, :].rearrange("p g r n -> p (g r n)"), bank(2)).then_inc(yt_rdy, 1)

            def ffn1():
                act.wait_ge(ld_w2, 16)
                act.copy(W2h, w2f).then_inc(w2_hi, 1)
                norm(3, 7, False)
                gates()
                for it in range(192):
                    act.wait_ge(hh_rdy, it + 1)
                    if it >= 2:
                        act.wait_ge(gg_rdy, it - 1)
                    act.activation(s32[it % 2], bank(it % 2), ACT.Silu).then_inc(s_rdy, 1)
                    if it >= 1:
                        hi(it - 1)
                hi(191)

            def hi(it):
                act.wait_ge(gg_rdy, it + 1)
                if it >= 2:
                    act.wait_ge(yy_used, it - 1)
                act.copy(gh[it % 2], g32[it % 2]).then_inc(gg_hi, 1)

            ffn0()
            norm(1, 7, False)
            gates()
            ffn0_main()
            convolution()
            ffn1()

        @block.gpsimd
        def _(pool):
            pool.memset(at(44 * K, 4096), 0.0).then_inc(zeroed, 1)
            pool.memset(at(60 * K, 4096), 0.0).then_inc(zeroed, 1)
            pool.wait_ge(ln_xc, NG)
            pool.wait_ge(ld_small, LD_SMALL)
            pool.tensor_tensor(X, X, bfin[:].unsqueeze(1).broadcast_to([P, NT, C]), ALU.add).then_inc(bfin_added, 1)
            for hg in range(2):
                for c in range(6):
                    if 1 <= c < 5:
                        cg = hg * 4 + c - 1
                        pool.wait_ge(centred, cg + 1)
                        if cg >= 2:
                            pool.wait_ge(sv_rdy, cg - 1)
                        pool.tensor_tensor(Sq[cg % 2], S_[cg % 3], S_[cg % 3], ALU.mult).then_inc(squared, 1)
                    if c >= 2:
                        cg = hg * 4 + c - 2
                        pool.wait_ge(o_hi, cg + 1)
                        pool.tensor_tensor(ots(OTl, hg, c - 2), O32[cg % 2].rearrange("p (j t) -> p j t", t=64),
                                           ots(OTh, hg, c - 2), ALU.subtract).then_inc(o_lo, 1)

            for it in range(32):
                pool.wait_ge(g_rdy, it + 1)
                if it >= 2:
                    pool.wait_ge(y_used, it - 1)
                pool.tensor_copy(gh[it % 2], g32[it % 2]).then_inc(g_hi, 1)
            pool.wait_ge(st_done, 16)
            pool.memset(SXF, 0.0).then_inc(sx_zero, 1)
            pool.wait_ge(ld_pc, 32)
            for n in range(2):
                for b in range(2):
                    ins = pool.tensor_scalar(PRI[n][:, :, b, :], pctr, pmask[:, 2 * n + b:2 * n + b + 1], None, ALU.mult)
            ins.then_inc(pri_rdy, 1)

        @block.vector
        def _(dve):
            steps = [0]

            def link(ins):
                steps[0] += 1
                ins.then_inc(vec, 1)
                dve.wait_ge(vec, steps[0])

            def rows(a, g):
                return a[:, 4 * g:4 * g + 4, :]

            def wide(a, g):
                return a[:, 4 * g:4 * g + 4].unsqueeze(2).broadcast_to([P, 4, C])

            def norm(L):
                for g in range(NG):
                    link(dve.tensor_reduce(mu[:, 4 * g:4 * g + 4], rows(X, g), AX_X, ALU.add))
                    link(dve.tensor_scalar(mu[:, 4 * g:4 * g + 4], mu[:, 4 * g:4 * g + 4], 1.0 / C, None, ALU.mult))
                    dve.tensor_tensor(rows(xc, g), rows(X, g), wide(mu, g), ALU.subtract).then_inc(ln_xc, 1)
                for g in range(NG):
                    dve.wait_ge(ln_sq, NG * L + g + 1)
                    dve.tensor_reduce(var[:, 4 * g:4 * g + 4], rows(sq, g), AX_X, ALU.add).then_inc(ln_var, 1)
                for g in range(NG):
                    dve.wait_ge(ln_dev, NG * L + g + 1)
                    link(dve.reciprocal(dev[:, 4 * g:4 * g + 4], dev[:, 4 * g:4 * g + 4]))
                    dve.wait_ge(ln_xc, NG * L + g + 1)
                    dve.tensor_tensor(rows(xc, g), rows(xc, g), wide(dev, g), ALU.mult).then_inc(ln_xn, 1)
                for g in range(NG):
                    dve.wait_ge(ln_hi, NG * L + g + 1)
                    hi, lo = [xrow[:, 4 * g:4 * g + 4, s, :].rearrange("p j (n c) -> p j n c", n=2) for s in range(2)]
                    dve.tensor_tensor(lo, rows(xc, g).unsqueeze(2).broadcast_to([P, 4, 2, C]), hi,
                                      ALU.subtract).then_inc(ln_lo, 1)

            dve.wait_ge(ld_x, 16)
            norm(0)
            dve.wait_ge(wp_hi, 1)
            dve.wait_ge(ld_small, LD_SMALL)
            dve.scalar_tensor_tensor(WP[:], wpH, mask[:, 4:5], wpf, ALU.mult, ALU.add).then_inc(wp_rdy, 1)
            dve.wait_ge(tb_hi, 1)
            link(dve.tensor_tensor(TL, tblf, TH, ALU.subtract))
            for c in range(4):
                ins = spread(dve, TL, 0, 0, c, False)
            ins.then_inc(en_lo, 1)
            dve.wait_ge(bv_hi, 1)
            dve.scalar_tensor_tensor(bv2[:], bv2h, mask[0:2, 9:10], bv2f, ALU.mult, ALU.add)
            dve.wait_ge(wf_hi, 1)
            dve.tensor_tensor(wfl[:], wff, wfh[:], ALU.subtract).then_inc(wf_rdy, 1)

            def attention():
                for hg in range(2):
                    for n, (kind, k) in enumerate(ORDER):
                        if (kind, k) == ("a", 4):
                            if hg:
                                dve.wait_ge(sv_rdy, 4)
                            for c in range(4):
                                ins = spread(dve, TL, 1, hg, c, False)
                            ins.then_inc(em_lo, 1)
                        if kind == "v":
                            continue
                        N = hg * UNITS + n
                        o = bank(N % 8)
                        if kind == "a":
                            dve.wait_ge(unit_rdy, N + 1)
                            o0 = (k % 4) * 16
                            bb = biasT[:, 2 * hg + k // 4, o0:o0 + 16].unsqueeze(2).broadcast_to([P, 16, NW])
                            ins = dve.tensor_tensor(AB[:, k // 4, o0:o0 + 16, :], o.rearrange("p (o b) -> p o b", b=NW),
                                                    bb, ALU.add)
                        else:
                            dve.wait_ge(unit_hi, count("nmqkc", hg, n))
                        if kind in "nmq":
                            hi, lo = {"n": (nh, nl), "m": (mh, ml), "q": (qh, ql)}[kind]
                            ins = dve.scalar_tensor_tensor(XW(lo, k), o, bcol(kind, hg), XW(hi, k), ALU.add, ALU.subtract)
                        elif kind == "k":
                            for c in range(4):
                                r = slice(32 * c, 32 * c + 32)
                                ins = dve.scalar_tensor_tensor(
                                    diagonal(KL, c, k), o[r, :].rearrange("p (b v) -> p b v", v=8),
                                    bcol(kind, hg)[r, :], diagonal(KH, c, k), ALU.add, ALU.subtract)
                        elif kind == "c":
                            ins = dve.tensor_tensor(cols_c(Cl, k), o.rearrange("p (u v b) -> p u v b", u=2, b=NW),
                                                    cols_c(Ch, k), ALU.subtract)
                        ins.then_inc(unit_free, 1)
                    dve.wait_ge(unit_free, count("nmqkac", hg, UNITS - 1))

                    for c in range(6):
                        if c < 4:
                            cg = hg * 4 + c
                            dve.wait_ge(st_rdy, cg + 1)
                            if cg >= 3:
                                dve.wait_ge(sv_rdy, cg - 2)
                            a = AB[:, :, :, c * 8:c * 8 + 8].rearrange("p h o b -> p h b o")
                            for hp in range(2):
                                ins = dve.tensor_tensor(
                                    S_[cg % 3][:, hp * BANK:(hp + 1) * BANK].rearrange("p (b o) -> p b o", o=PW),
                                    bank(2 * (cg % 2) + hp).rearrange("p (b o) -> p b o", o=PW),
                                    a[:, hp, :, :], ALU.add)
                            ins.then_inc(s_added, 1)
                        if c < 4 and hg == 0:
                            ins = spread(dve, TL, 0, 1, c, False)
                            if c == 3:
                                ins.then_inc(en_lo, 1)
                        if 1 <= c < 5:
                            cg = hg * 4 + c - 1
                            dve.wait_ge(mean_rdy, cg + 1)
                            dve.tensor_tensor(S_[cg % 3], S_[cg % 3], bank(4, 2), ALU.subtract).then_inc(centred, 1)
                        if c >= 2:
                            cg = hg * 4 + c - 2
                            dve.wait_ge(std_rdy, cg + 1)
                            if cg >= 2:
                                dve.wait_ge(o_lo, cg - 1)
                            link(dve.reciprocal(rsc[cg % 2], rsc[cg % 2]))
                            v = "p (w i j) -> p w i j"
                            ins = dve.tensor_tensor(O32[cg % 2].rearrange("p (i w j) -> p w i j", i=8, w=8),
                                                    bank(6).rearrange(v, w=8, i=8), rsc[cg % 2].rearrange(v, w=8, i=8), ALU.mult)
                            ins.then_inc(o_read, 1)
                dve.wait_ge(bfin_added, 1)
                for n in range(2):
                    dve.wait_ge(proj_rdy, n + 1)
                    dve.tensor_tensor(X[:, 8 * n:8 * n + 8, :], X[:, 8 * n:8 * n + 8, :],
                                      bank(n).rearrange("p (j c) -> p j c", c=C), ALU.add).then_inc(x_rdy, 1)
                dve.wait_ge(x_rdy, 2)

            def wide8(a):
                return a.unsqueeze(2).broadcast_to([P, NT, 8])

            def top_two(n, o):
                dve.wait_ge(lg_rdy, n + 1)
                gb = (g0b.unsqueeze(1).broadcast_to([P, NT, 8]), None)[n]
                src = o[:, 0:128].rearrange("p (j e) -> p j e", e=8)
                if n == 0:
                    ins = dve.tensor_tensor(lg, src, gb, ALU.add)
                else:
                    ins = dve.tensor_copy(lg, src)
                ins.then_inc(lg_read, 1)
                dve.wait_ge(lg_read, n + 1)
                link(dve.tensor_reduce(m1[:], lg, AX_X, ALU.max))
                dve.tensor_tensor(ex, lg, wide8(m1[:]), ALU.subtract).then_inc(ex_in, 1)
                iw = idxw.unsqueeze(1).broadcast_to([P, NT, 8])

                def first_largest(a, m, oh):
                    link(dve.tensor_tensor(eq, a, wide8(m[:]), ALU.is_equal))
                    link(dve.tensor_tensor(sc, eq, iw, ALU.mult))
                    link(dve.tensor_reduce(sm[:], sc, AX_X, ALU.max))
                    link(dve.tensor_tensor(oh, sc, wide8(sm[:]), ALU.is_equal))

                first_largest(lg, m1, oh1)
                f = "p j e -> p (j e)"
                link(dve.scalar_tensor_tensor(l2.rearrange(f), oh1.rearrange(f), -3e38, lg.rearrange(f), ALU.mult, ALU.add))
                link(dve.tensor_reduce(m2[:], l2, AX_X, ALU.max))
                first_largest(l2, m2, oh2)
                link(dve.tensor_tensor(oh2, oh1, oh2, ALU.add))
                dve.wait_ge(ex_rdy, n + 1)
                link(dve.tensor_reduce(sm[:], ex, AX_X, ALU.add))
                link(dve.reciprocal(sm[:], sm[:]))
                link(dve.tensor_tensor(ex, ex, wide8(sm[:]), ALU.mult))
                link(dve.tensor_tensor(cw, ex, oh2, ALU.mult))
                if n:
                    link(dve.tensor_reduce(sm[:], cw, AX_X, ALU.add))
                    link(dve.tensor_scalar(sm[:], sm[:], 1e-9, None, ALU.add))
                    link(dve.reciprocal(sm[:], sm[:]))
                    link(dve.tensor_tensor(cw, cw, wide8(sm[:]), ALU.mult))

            def weigh(t, o, rdy, rdy_at, read):
                dve.wait_ge(rdy, rdy_at)
                c = cw[:, t, :].unsqueeze(2).broadcast_to([P, 8, C])
                ins = dve.tensor_tensor(tmp.rearrange("p (e c) -> p e c", e=8), o.rearrange("p (e c) -> p e c", e=8), c,
                                        ALU.mult).then_inc(read, 1)
                dve.wait_ge(read, t + 1)
                link(dve.tensor_reduce(red[:], tmp.rearrange("p (e c) -> p c e", e=8), AX_X, ALU.add))
                dve.tensor_tensor(X[:, t, :], X[:, t, :], red[:], ALU.add).then_inc(x_rdy, 1)

            def expert_stage(n):
                dve.wait_ge(st_hi, n + 1)
                dst = W13[:, n % 8, n // 8, :]
                dve.scalar_tensor_tensor(dst, stageH[n % 4], mask[:, 4:5], stage[n % 4], ALU.mult, ALU.add).then_inc(st_done, 1)

            def ffn0():
                dve.wait_ge(gh_hi, 1)
                dve.scalar_tensor_tensor(GW[:], GH[:], mask[:, 4:5], small[:, 0:16], ALU.mult, ALU.add).then_inc(gw_rdy, 1)
                dve.wait_ge(f0_hi, 1)
                dve.scalar_tensor_tensor(W1g, w1gH, mask[:, 4:5], w1gf, ALU.mult, ALU.add)
                dve.tensor_tensor(W2gl, w2gf, W2gh, ALU.subtract)
                dve.scalar_tensor_tensor(b2r[:], b2H, mask[0:2, 9:10], b2f, ALU.mult, ALU.add).then_inc(f0_rdy, 1)
                norm(1)
                dve.wait_ge(ln_lo, 2 * NG)
                top_two(0, bank(7))
                for it in range(32):
                    dve.wait_ge(g_hi, it + 1)
                    if it >= 2:
                        dve.wait_ge(y_used, it - 1)
                    dve.tensor_tensor(gl[it % 2], g32[it % 2], gh[it % 2], ALU.subtract).then_inc(g_lo, 1)
                    if it % 2 == 1:
                        expert_stage(it // 2)
                    if it >= 9 and it % 8 in (1, 2):
                        for t in range(4 * (it // 8 - 1) + 2 * (it % 8 - 1), 4 * (it // 8 - 1) + 2 * (it % 8)):
                            weigh(t, bank(2 + t % 6), y_used, 8 * (t // 4 + 1), y_read)
                for t in range(12, 16):
                    weigh(t, bank(2 + t % 6), y_used, 32, y_read)
                dve.wait_ge(x_rdy, XD[2])

            def convolution():
                link(dve.tensor_scalar(wb, small[:, 48:50], wlat, TWO_PI / 64, ALU.mult, ALU.mult))
                dve.tensor_copy(wb, wb).then_inc(wb_rdy, 1)
                norm(2)
                for k in (1, 3):
                    dve.wait_ge(a_rdy, k + 1)
                    dve.tensor_copy(spectrum(k), bank(4 + k)[0:64, :].rearrange("p (i n) -> p i n", i=8)).then_inc(xf_rdy, 1)
                dve.wait_ge(b_rdy, 1)
                dve.wait_ge(sx_zero, 1)
                for n in range(8, 16):
                    ins = dve.tensor_copy(*mixing(n))
                ins.then_inc(sx_dve, 1)
                for mb in range(4):
                    dve.wait_ge(z_act, mb + 1)
                    dve.tensor_scalar(Z3[:, 8 * mb:8 * mb + 8, 0:32], Z3[:, 8 * mb:8 * mb + 8, 64:96], -1.0, None,
                                      ALU.mult).then_inc(z_dve, 1)
                for mb in (1, 3):
                    dve.wait_ge(d_rdy, mb + 1)
                    dve.tensor_copy(modes(mb), bank((6, 7, 0, 1)[mb])[0:64, :].rearrange("p (m n) -> p m n", n=64)).then_inc(yt_in, 1)
                dve.wait_ge(t_rdy, 2)
                dve.tensor_copy(YT[:, 4:8, :, :].rearrange("p g r n -> p (g r n)"), bank(3)).then_inc(yt_rdy, 1)
                for n in range(2):
                    dve.wait_ge(e_rdy, n + 1)
                    dve.tensor_tensor(X[:, 8 * n:8 * n + 8, :], X[:, 8 * n:8 * n + 8, :],
                                      bank(4 + n).rearrange("p (j c) -> p j c", c=C), ALU.add).then_inc(x_rdy, 1)
                dve.wait_ge(x_rdy, XD[3])

            def ffn1():
                norm(3)
                dve.wait_ge(w2_hi, 1)
                dve.tensor_tensor(W2l, w2f, W2h, ALU.subtract).then_inc(w2_rdy, 1)
                dve.wait_ge(ln_lo, 4 * NG)
                top_two(1, bank(7))

                def low(it):
                    dve.wait_ge(gg_hi, it + 1)
                    if it >= 2:
                        dve.wait_ge(yy_used, it - 1)
                    dve.tensor_tensor(gl[it % 2], g32[it % 2], gh[it % 2], ALU.subtract).then_inc(gg_lo, 1)

                for it in range(192):
                    dve.wait_ge(s_rdy, it + 1)
                    dve.wait_ge(h3_rdy, it + 1)
                    if it >= 2:
                        dve.wait_ge(gg_lo, it - 1)
                    dve.tensor_tensor(g32[it % 2], bank(2 + it % 2), s32[it % 2], ALU.mult).then_inc(gg_rdy, 1)
                    if it:
                        low(it - 1)
                    if it >= 49 and it % 48 == 1:
                        for t in range(4 * (it // 48 - 1), 4 * (it // 48)):
                            weigh(t, bank(4 + t % 4), yy_used, 48 * (t // 4 + 1), yy_read)
                low(191)
                for t in range(12, 16):
                    weigh(t, bank(4 + t % 4), yy_used, 192, yy_read)

            attention()
            ffn0()
            convolution()
            ffn1()


def kernel(**inputs):
    import numpy as np
    import concourse.bacc as _bacc
    from concourse import mybir as _mybir
    from concourse.bass_utils import run_bass_kernel_spmd as _run

    I = {k: np.asarray(v) for k, v in inputs.items()}
    f32 = np.float32
    p = np.arange(128)
    arr = {}

    def tile_order(x):
        return x.reshape(2, 2, 16, 32, 64).transpose(0, 1, 3, 2, 4).reshape(128, 1024)

    arr["x"] = tile_order(I["x"])
    arr["wprep"] = np.concatenate([I["L0_conv_W_prep"]] * 2, 0)
    bp = I["L0_conv_b_prep"].reshape(5, 2, 128)
    arr["bprep"] = bp[:4].transpose(2, 0, 1).reshape(128, 8)
    arr["bv"] = np.stack([bp[4].reshape(256)] * 2)
    arr["ones"] = np.ones((2, 128), np.float16)
    y = p // 8 % 2
    arr["bfin"] = np.broadcast_to(I["L0_conv_b_fin"][None], (128, 64))
    intr = I["L0_conv_intrinsic"]
    tn = intr[:, ::-1, ::-1, 1:33].transpose(0, 3, 1, 2).reshape(2, 128, 225)
    tm = intr[:, :, :, 33:65].transpose(0, 3, 1, 2).reshape(2, 128, 225)
    arr["tables"] = np.stack([tn, tm], 0).transpose(2, 0, 1, 3).reshape(128, 900)
    ii = np.arange(8)
    r = ii[None, :] - ii[:, None] + 7
    bt = intr[:, r[:, None, :, None], r[None, :, None, :], 0]
    arr["biasT"] = bt.reshape(4, 2, 8, 8, 64).transpose(2, 1, 3, 0, 4).reshape(128, 256)
    o, h2 = (p // 16) * 8 + p % 8, p // 8 % 2
    arr["sel"] = (np.arange(128)[None] == (h2 * 64 + o)[:, None]).astype(np.float16)
    arr["ident"] = np.eye(128, dtype=np.float16)
    m = np.zeros((128, 16), f32)
    for c in range(4):
        m[:, c] = (p // 32 == c)
    m[:, 4] = -(p >= 64).astype(f32)
    m[:, 5], m[:, 6] = y == 0, y == 1
    m[:, 7], m[:, 8] = EPS_A, EPS_C
    m[1, 9] = -1
    arr["mask"] = m
    arr["cen"] = (y[:, None] == y[None, :]).astype(f32) / f32(64)
    arr["varm"] = (y[:, None] == np.arange(64)[None, :] // 32).astype(f32) / f32(63)
    arr["wfin"] = I["L0_conv_W_fin"].reshape(2, 128, 64).transpose(1, 0, 2).reshape(128, 128)

    arr["identf"] = np.eye(64, dtype=f32)
    W1 = I["L0_ffn_W1"].transpose(1, 0, 2).reshape(64, 1024)
    arr["w1g"] = np.concatenate([W1, W1])
    arr["w2g"] = I["L0_ffn_W2"].transpose(1, 0, 2).reshape(128, 512)
    arr["b2g"] = np.stack([I["L0_ffn_b2"].reshape(512)] * 2)
    sm = np.zeros((128, 64), f32)
    sm[:, 0:8] = np.concatenate([I["L0_ffn_gate_w"]] * 2)
    sm[:, 8:16] = np.concatenate([I["L1_ffn_router_w"].T] * 2)
    sm[:, 16:24] = I["L0_ffn_gate_b"][None]
    sm[:, 24:32] = I["L0_ffn_b1"].T
    sm[:, 32:40] = 8 - np.arange(8)
    sm[:, 40] = I["L1_conv_w"][p % 32]
    for b in range(2):
        sm[:, 42 + b] = (p // 2 % 2 == b) & (p % 2 == 0)
        sm[:, 44 + b] = (p // 2 % 2 == b) & (p % 2 == 1)
        sm[:, 48 + b] = p // 32 == b
    arr["small"] = sm
    n, mm = np.arange(64)[:, None], np.arange(32)[None]
    ang = 2 * np.pi * n * mm / 64
    F = np.stack([np.cos(ang), -np.sin(ang)], -1).reshape(64, 64).astype(f32)
    Fh = F.astype(np.float16)
    arr["dft"] = np.concatenate([Fh, (F - Fh.astype(f32)).astype(np.float16)])
    cm = np.where(np.arange(32) == 0, 1.0, 2.0)[:, None]
    gi = np.zeros((4, 32, 2, 4, 64), f32)
    for q in range(4):
        gi[q, :, 0, q] = cm * np.cos(ang.T)
        gi[q, :, 1, q] = -cm * np.sin(ang.T)
    arr["gi"] = gi.reshape(128, 512)
    pct = I["L1_conv_pct"]
    arr["pctr"] = pct[:, :32][p // 4].reshape(128, 1024)
    pt = pct[:, :32].transpose(2, 1, 0).reshape(32, 1024)
    arr["pctt"] = np.concatenate([pt, pt])
    wc = I["L1_conv_weights"].reshape(32, 32, 8, 4, 32, 2)
    arr["wc"] = wc.transpose(3, 0, 4, 2, 5, 1).reshape(128, 32 * 8 * 64)
    w13 = np.zeros((2, 64, 8, 768), f32)
    w13[0, :, :, :682] = I["L1_ffn_w1"].transpose(2, 0, 1)
    w13[1, :, :, :682] = I["L1_ffn_w3"].transpose(2, 0, 1)
    w13 = w13.transpose(1, 0, 2, 3).reshape(64, 12288)
    arr["w13"] = np.concatenate([w13, w13])
    w2 = np.zeros((8, 768, 64), f32)
    w2[:, :682] = I["L1_ffn_w2"].transpose(0, 2, 1)
    arr["w2"] = w2.reshape(8, 6, 128, 64).transpose(2, 0, 1, 3).reshape(128, 3072)

    nc = _bacc.Bacc("TRN2", target_bir_lowering=False, num_devices=1)
    inp, feeds = {}, {}
    for name, a in arr.items():
        a = np.ascontiguousarray(a)
        feeds[f"in_{name}"] = a
        inp[name] = nc.dram_tensor(f"in_{name}", a.shape, _mybir.dt.from_np(a.dtype), kind="ExternalInput").ap()
    out = nc.dram_tensor("out", (128, 1024), _mybir.dt.float32, kind="ExternalOutput").ap()
    build(nc, inp, out)
    r = _run(nc, [feeds], core_ids=[0])
    y = r.results[0]["out"]
    return y.reshape(2, 2, 32, 16, 64).transpose(0, 1, 3, 2, 4).reshape(2, 32, 32, 64)
```

```python
from contextlib import ExitStack

import concourse.bass as bass
from concourse import mybir

ALU = mybir.AluOpType
ACT = mybir.ActivationFunctionType
F32 = mybir.dt.float32
F16 = mybir.dt.float16
I32 = mybir.dt.int32
AX_X = mybir.AxisListType.X

P = 128
B, HIMG, WIMG, C = 2, 32, 32, 64
NTOK = B * HIMG * WIMG
NT = NTOK // P
NG = 4
NH, HD, WIN = 8, 32, 8
PW = WIN * WIN
NW = NTOK // PW
REL = 2 * WIN - 1
BANK = 512
TWO_PI = 2.0 * 3.141592653589793
HALF = 384
NBLK = (2 * NTOK + 8 * (P - 1)) // P
EPS_C, EPS_A = 1e-6, 1e-5


def build(nc, inp, out):
    ctx = ExitStack()
    with ctx:
        def sb(name, shape, dt=F32):
            return ctx.enter_context(nc.sbuf_tensor(name, shape, dt))

        def sem(name):
            return ctx.enter_context(nc.semaphore(name))

        ARENA = sb("arena", [P, 199 * 256], F32)

        def at(off, cols, dt=F32):
            size = 4 if dt == F32 else 2
            a = ARENA[:, off // 4:(off + cols * size) // 4]
            return a if dt == F32 else a.bitcast(dt)

        K = 1024
        X = at(0, 1024).rearrange("p (j c) -> p j c", c=C)
        XH = at(4 * K, NTOK, F16)
        XL = at(8 * K, NTOK, F16)
        xrow = at(12 * K, 4096, F16).rearrange("p (j s n) -> p j s n", s=2, n=2 * C)
        xc = at(20 * K, 1024).rearrange("p (j c) -> p j c", c=C)
        sq = at(24 * K, 1024).rearrange("p (j c) -> p j c", c=C)

        XHw = at(28 * K, 2 * NTOK, F16)
        XLw = at(36 * K, 2 * NTOK, F16)
        KH = at(44 * K, 8192, F16).rearrange("p (h b u y v) -> p h b u y v", h=2, b=NW, u=8, y=2)
        KL = at(60 * K, 8192, F16).rearrange("p (h b u y v) -> p h b u y v", h=2, b=NW, u=8, y=2)
        qh, ql, nh, nl, mh, ml = [at(76 * K + 4 * K * n, 2048, F16) for n in range(6)]
        ETB = 2 * 8 * REL * 16
        ENh, ENl = [at(100 * K + 2 * ETB * n, ETB, F16).rearrange("p (a w r) -> p a w r", a=2, w=8) for n in range(2)]
        AB = at(115 * K, 4096).rearrange("p (h o b) -> p h o b", h=2, o=PW)
        Ch = at(131 * K, 4096, F16).rearrange("p (b c) -> p b c", b=NW)
        Cl = at(139 * K, 4096, F16).rearrange("p (b c) -> p b c", b=NW)
        V = at(147 * K, 4096).rearrange("p (b h n) -> p b h n", h=2, n=64)
        S_ = [at((163 + 4 * n) * K, 1024) for n in range(3)]
        Sq = [at((175 + 4 * n) * K, 1024) for n in range(2)]
        EMh, EMl = [at(163 * K + 2 * ETB * n, ETB, F16).rearrange("p (a w r) -> p a w r", a=2, w=8) for n in range(2)]
        OTh = [at(183 * K + 8 * K * g, 2048, F16) for g in range(2)]
        OTl = [at(187 * K + 8 * K * g, 2048, F16) for g in range(2)]
        wpf, wpH = at(115 * K, 1280), at(121 * K, 1280, F16)
        wff = at(125 * K, 128).rearrange("p (g c) -> p g c", g=2)
        tblf = at(126 * K, 900)
        TH, TL = at(12 * K, 900, F16), at(14 * K, 900, F16)
        O32 = [at((20 + 2 * n) * K, BANK) for n in range(2)]
        rsc = [at((24 + 2 * n) * K, BANK) for n in range(2)]
        WP = sb("WP", [P, 1280], F16)
        biasT = sb("biasT", [P, 4, PW])
        CEN = sb("cen", [P, P])
        VAR = sb("varm", [P, PW])
        wfh = sb("wfh", [P, 2, C], F16)
        wfl = sb("wfl", [P, 2, C], F16)

        WC = [at(o * K, 2048).rearrange("p (m q n) -> p m q n", m=4, q=8) for o in (28, 36, 88, 96, 44, 52, 60, 68)]
        Z3 = at(28 * K, 3072).rearrange("p (m n) -> p m n", n=96)
        GI = at(82 * K, 512).rearrange("p (r n) -> p r n", r=2)
        W1g = at(84 * K, 1024, F16)
        W2gh = at(86 * K, 512, F16)
        W2gl = at(87 * K, 512, F16)
        w1gf, w2gf, w1gH = at(104 * K, 1024), at(108 * K, 512), at(110 * K, 1024, F16)
        SX = at(108 * K, 8192).rearrange("p (m q n) -> p m q n", q=8, n=32)
        SXF = at(108 * K, 8192)
        stage = [at((112 + 3 * n) * K, 768) for n in range(4)]
        stageH = [at(124 * K + 1536 * n, 768, F16) for n in range(4)]
        PRI = [at((140 + 8 * n) * K, 2048).rearrange("p (m b t) -> p m b t", b=2, t=32) for n in range(2)]
        pctr = at(76 * K, 1024).rearrange("p (m t) -> p m t", t=32)
        pctf = at(168 * K, 1024)[0:64, :].rearrange("p (m l) -> p m l", l=32)
        b2f, b2H = at(112 * K, 512)[0:2, :], at(114 * K, 512, F16)[0:2, :]
        PCTW = at(156 * K, 2048).rearrange("p (m b l) -> p m b l", b=2, l=32)
        XF = at(164 * K, 2048).rearrange("p (m r i) -> p m r i", r=2, i=32)
        Y = at(156 * K, 2048).rearrange("p (r o m) -> p r o m", r=2, o=32)
        YT = at(164 * K, 1024).rearrange("p (g r n) -> p g r n", r=2, n=64)
        g32 = [at((156 + 2 * n) * K, 512) for n in range(2)]
        gh = [at((160 + n) * K, 512, F16) for n in range(2)]
        gl = [at((162 + n) * K, 512, F16) for n in range(2)]
        tmp = at(164 * K, 512)
        W13 = at(172 * K, 12288, F16).rearrange("p (e w n) -> p e w n", e=8, w=2)
        w2f = at(44 * K, 3072)
        W2 = at(56 * K, 6144, F16).rearrange("p (e c s n) -> p e c s n", e=8, c=6, s=2)
        w2v = w2f.rearrange("p (e c n) -> p (e c) n", e=8, c=6)
        W2hi, W2lo = [W2[:, :, :, n, :].rearrange("p e c n -> p (e c) n") for n in range(2)]

        oh12 = at(26 * K, 256).rearrange("p (k n) -> p k n", k=2)
        xg = [at(28 * K + 512 * n, 256, F16) for n in range(4)]
        xb = [at(30 * K + 512 * n, 256, F16) for n in range(2)]
        s32 = [at(31 * K + 1536 * n, HALF) for n in range(2)]
        f32 = [at(34 * K + 1536 * n, HALF) for n in range(2)]
        fh = [at(37 * K + 768 * n, HALF, F16) for n in range(4)]
        fl = [at(40 * K + 768 * n, HALF, F16) for n in range(4)]
        ys = [at(43 * K + 256 * n, C) for n in range(4)]
        RT, RT16 = at(108 * K, 288), at(109 * K + 256, 256, F16)
        iota, k128 = RT[:, 0:P], RT[:, 128:144].unsqueeze(1).broadcast_to([P, 8, 16])
        before = RT[:, 144:208].rearrange("p (e f) -> p e f", e=8)
        row_id = RT[:, 208:240]
        tri, ones = RT16[:, 0:P], RT16[:, P:2 * P]
        picked = at(110 * K, (NT + 1) * 8, F16)
        rank = at(111 * K, (NT + 1) * 8)
        above = at(112 * K, 128).rearrange("p (e k) -> p e k", e=8)
        nblk, first, end = [at(113 * K + 32 * n, 8) for n in range(3)]
        partial = at(113 * K + 256, 64).rearrange("p (e f) -> p e f", e=8)
        prod = at(114 * K, 256)
        slot, gate2, gate_rest, blk_f, pos_f = [at(115 * K + 128 * n, 32) for n in range(5)]
        slot_i, blk_i, pos_i = [at(116 * K + 128 * n, 32).bitcast(I32) for n in range(3)]
        gate2h = at(116 * K + 384, 32, F16)
        OBX = at(117 * K, 32 * 3 * NBLK, F16).rearrange("p (c v b) -> p c v b", v=3, b=NBLK)
        OB = at(125 * K, 32 * NBLK, F16).rearrange("p (c b) -> p c b", b=NBLK)
        OR = at(128 * K, 32 * P, F16).rearrange("p (c r) -> p c r", r=P)
        NW8 = -(-NBLK // 8)
        past = at(136 * K, 8 * 8 * NW8)[0:1, :].rearrange("p (b e) -> p b e", e=8)
        exp_f = at(138 * K, 8 * NW8)[0:1, :]
        digit = RT[0:1, 241:241 + 8 * NW8]
        word_f = at(138 * K + 256, NW8)[0:1, :]
        word_i = at(138 * K + 384, NW8)[0:1, :].bitcast(I32)
        row_i = at(138 * K + 512, NBLK).bitcast(I32)
        gate = at(138 * K + 768, NBLK)
        pad_row = at(139 * K, NBLK)
        own_row = RT[:, 240:241]
        lg, eq, sc, l2, oh1, oh2, ex, cw = [at(24 * K + 512 * n, 128).rearrange("p (j e) -> p j e", e=8)
                                            for n in range(8)]

        ident = sb("ident", [P, P], F16)
        sel = sb("sel", [P, P], F16)
        mask = sb("mask", [P, 16])
        bprep = sb("bprep", [P, 8])
        bfin = sb("bfin", [P, C])
        bv2f, bv2h = at(130 * K, 256)[0:2, :], at(125 * K + 512, 256, F16)[0:2, :]
        b2r = sb("b2r", [2, 512], F16)
        small = sb("small", [P, 64])
        g0w, g1w, g0b, b1c, idxw = [small[:, 8 * n:8 * n + 8] for n in range(5)]
        wlat, pmask, wb = small[:, 40:41], small[:, 42:46], small[:, 46:48]
        identf = sb("identf", [64, 64])
        GH = sb("gateH", [P, 16], F16)
        GW = sb("gateW", [P, 16], F16)
        FW = sb("dftw", [P, 64], F16)
        red = sb("red", [P, C])
        m1, m2, sm = [sb(n, [P, NT]) for n in ("m1", "m2", "sm")]
        bv2 = sb("bv2", [2, 256], F16)
        ones2 = sb("ones2", [2, P], F16)
        mu = sb("mu", [P, NT])
        var = sb("var", [P, NT])
        dev = sb("dev", [P, NT])

        PS = ctx.enter_context(nc.psum_tensor("ps", [P, 8 * BANK], F32))

        def bank(n, m=1):
            return PS[:, n * BANK:(n + m) * BANK]

        ld_x, ld_wp, ld_tbl, ld_small, st_out = sem("ld_x"), sem("ld_wp"), sem("ld_tbl"), sem("ld_small"), sem("st_out")
        vec = sem("vec_step")
        ln_xc, ln_sq, ln_xn, ln_hi, ln_lo, ln_tp, xs_rdy = [sem(s) for s in (
            "ln_centred", "ln_squared", "ln_normed", "ln_hi", "ln_lo", "ln_transposed", "xs_ready")]
        wp_hi, wp_rdy, tb_hi, tb_rdy, wf_hi, wf_rdy = [sem(s) for s in (
            "wprep_hi", "wprep_ready", "table_hi", "table_ready", "wfin_hi", "wfin_ready")]
        zeroed, unit_rdy, unit_hi, unit_free, k_spread = [sem(s) for s in (
            "zeroed", "unit_ready", "unit_hi", "unit_free", "k_spread")]
        st_rdy, s_added, mean_rdy, centred, squared, sv_rdy, o_read, o_hi, o_lo = [sem(s) for s in (
            "scores_ready", "scores_added", "mean_ready", "scores_centred", "scores_squared", "sv_ready",
            "o_read", "o_hi", "o_lo")]
        bfin_added, proj_rdy, x_rdy = sem("bfin_added"), sem("proj_ready"), sem("x_ready")
        bv_hi, ln_var, ln_dev, std_rdy = sem("bv_hi"), sem("ln_var"), sem("ln_dev"), sem("std_ready")
        en_hi, en_lo, em_hi, em_lo, v_free = [sem(s) for s in ("en_hi", "en_lo", "em_hi", "em_lo", "v_free")]

        LD_SMALL = 14 * 16
        XD = {1: 2, 2: 2 + 16, 3: 2 + 16 + 2}

        ld_f0, ld_wc, ld_gi, ld_pc, ld_st, ld_w2 = (sem("ld_f0"), [sem(f"ld_wc{n}") for n in range(8)], sem("ld_gi"),
                                                    sem("ld_pct"), [sem(f"ld_stage{n}") for n in range(4)], sem("ld_w2"))
        f0_hi, f0_rdy, gh_hi = sem("ffn0_weights_hi"), sem("ffn0_weights_ready"), sem("gates_hi")
        gw_rdy, st_hi, st_done, wb_rdy = sem("gate_weights_ready"), sem("stage_hi"), sem("stage_done"), sem("wb_ready")
        lg_rdy, lg_read, ex_in, ex_rdy = sem("logits_ready"), sem("logits_read"), sem("exp_in"), sem("exp_ready")
        h_rdy, g_rdy, g_hi, g_lo, y_used, y_rdy, y_read = [sem(n) for n in (
            "h_ready", "g_ready", "g_hi", "g_lo", "y_used", "y_ready", "y_read")]
        sx_zero, pri_rdy, pw_rdy = sem("sx_zero"), sem("pri_ready"), sem("pctw_ready")
        a_rdy, xf_rdy, b_rdy, sx_act, sx_dve, c_rdy, z_act, z_dve, d_rdy, yt_in, t_rdy, yt_rdy, e_rdy = [sem(n) for n in (
            "a_ready", "xf_ready", "b_ready", "sx_act", "sx_dve", "c_ready", "z_act", "z_dve", "d_ready", "y_whole",
            "t_ready", "yt_ready", "e_ready")]
        ys_hi = sem("ys_hi")
        w2_hi, w2_rdy, s_rdy = sem("w2_hi"), sem("w2_ready"), sem("silu_ready")
        hh_rdy, gg_rdy, gg_hi, gg_lo, yy_used, ys_rdy = [sem(n) for n in (
            "hh_ready", "gg_ready", "gg_hi", "gg_lo", "yy_used", "ys_ready")]
        ld_rt, st_init, st_rows, gathered = sem("ld_routing"), sem("st_init"), sem("st_rows"), [sem(f"gathered{n}") for n in range(4)]
        added = [sem("added_even"), sem("added_odd")]
        pick_rdy, rank_rdy, exp_rdy, map_in, map_rdy, row_rdy, gate_rdy, tp_rdy, xb_rdy = [sem(n) for n in (
            "picks_ready", "ranks_ready", "experts_ready", "map_in", "map_ready", "rows_ready", "gate_ready",
            "tp_ready", "xb_ready")]

        def spectrum(k):
            return XF[0:64].rearrange("p m r i -> p (m r) i")[:, :, 8 * k:8 * k + 8].rearrange("p n i -> p i n")

        def mixing(n):
            quad, g = n // 4, n % 4
            mh, r = quad // 2, quad % 2
            src = PS[32 * quad:32 * quad + 32, 0:1024].rearrange("p (m b q l) -> p m b q l", m=16, b=2, l=4)[:, :, :, :, g]
            dst = SX[32 * g:32 * g + 32, 16 * mh:16 * mh + 16, :, 4 * g + r:4 * g + 4:2]
            return dst.rearrange("p m q b -> p m b q"), src

        def modes(mb):
            return Y[0:64].rearrange("p r o m -> p (r o) m")[:, :, 8 * mb:8 * mb + 8].rearrange("p n m -> p m n")

        def bcol(kind, hg):
            return bprep[:, 2 * TYPE[kind] + hg:2 * TYPE[kind] + hg + 1]

        def wk(KX, hp, b):
            return KX[:, hp, b, :, :, :].rearrange("p u y v -> p (u y v)")

        def windowed(dst, g, j, y):
            j0 = 4 * g
            return bass.AP(dst.tensor, dst.offset + (j0 // 8) * 2048 + (j0 % 8) * 16 + 8 * y,
                           [list(dst.ap[0]), [16, 4], [P, 16], [1, 8]])

        def XW(xs, k):
            return xs[:, k * BANK:(k + 1) * BANK]

        def cols_c(CX, k):
            v = CX.rearrange("p b (u y v) -> p u y v b", u=8, y=2)
            return v[:, 2 * (k % 4):2 * (k % 4) + 2, k // 4, :, :]

        def ots(OT, hg, c):
            return OT[hg].rearrange("p (j q) -> p j q", q=P)[:, (c // 2) * 8:(c // 2) * 8 + 8,
                                                            (c % 2) * 64:(c % 2) * 64 + 64]

        ORDER = [("n", k) for k in range(4)] + [("m", k) for k in range(4)]
        for k in range(8):
            ORDER += [("a", k), ("kq"[k // 4], k % 4)]
        for k in range(8):
            ORDER += [("c", k), ("v", k)]
        UNITS = len(ORDER)
        TYPE = {"n": 0, "q": 1, "k": 2, "m": 3}

        def count(kinds, hg, n):
            return hg * sum(u in kinds for u, _ in ORDER) + sum(u in kinds for u, _ in ORDER[:n + 1])

        def last(kind):
            return max(n for n, (u, _) in enumerate(ORDER) if u == kind)

        def spread(eng, src, t, hg, c, hi):
            E = (EMh if hi else EMl) if t else (ENh if hi else ENl)
            off = (2 * t + hg) * REL * REL + 7
            view = bass.AP(src.tensor, src.offset + off, [list(src.ap[0]), [-1, 8], [REL, REL], [1, 8]])
            outer, inner = (c % 2, c // 2) if t else (c // 2, c % 2)
            dst = E[:, outer, :, :].rearrange("p w (r y v) -> p w r y v", y=2, v=8)[:, :, :, inner, :]
            if hi:
                return eng.mul(dst, view, mask[:, c:c + 1])
            return eng.tensor_scalar(dst, view, mask[:, c:c + 1], None, ALU.mult)

        def diagonal(KX, c, k):
            return KX[32 * c:32 * c + 32, c // 2, 8 * k:8 * k + 8, :, c % 2, :].rearrange("p b u v -> p (b u) v")

        rows_x = nc.dram_tensor("rows_x", (P + NTOK, 256), F16).ap()
        sum_odd = nc.dram_tensor("sum_odd", (P + NTOK, C), F32).ap()

        block = ctx.enter_context(nc.Block())

        @block.sync
        def _(sp):
            sp.dma_start(X, inp["x"].rearrange("p (j c) -> p j c", c=C)).then_inc(ld_x, 16)
            sp.dma_start(wpf, inp["wprep"]).then_inc(ld_wp, 16)
            for dst, src in ((ident[:], "ident"), (mask[:], "mask"), (bprep[:], "bprep"), (bfin[:], "bfin"),
                             (biasT[:].rearrange("p h o -> p (h o)"), "biasT"), (CEN[:], "cen"), (VAR[:], "varm"),
                             (wff.rearrange("p g c -> p (g c)"), "wfin"), (sel[:], "sel"), (bv2f, "bv"),
                             (ones2[:], "ones"), (small[:], "small"), (identf[:], "identf"), (FW[:], "dft")):
                sp.dma_start(dst, inp[src]).then_inc(ld_small, 16)
            sp.dma_start(tblf, inp["tables"]).then_inc(ld_tbl, 16)
            sp.wait_ge(unit_rdy, 2 * UNITS)
            for dst, src in ((w1gf, "w1g"), (w2gf, "w2g"), (b2f, "b2g")):
                sp.dma_start(dst, inp[src]).then_inc(ld_f0, 16)

            def load_weights(n):
                sp.dma_start(WC[n].rearrange("p m q n -> p (m q n)"),
                             inp["wc"][:, 2048 * n:2048 * (n + 1)]).then_inc(ld_wc[n], 16)

            for n in range(4):
                load_weights(n)
            sp.wait_ge(st_rdy, 8)
            sp.dma_start(pctr.rearrange("p m t -> p (m t)"), inp["pctr"]).then_inc(ld_pc, 16)
            sp.dma_start(GI.rearrange("p r n -> p (r n)"), inp["gi"]).then_inc(ld_gi, 16)
            for n in range(4, 8):
                load_weights(n)
            sp.wait_ge(x_rdy, 2)
            sp.dma_start(pctf.rearrange("p m l -> p (m l)"), inp["pctt"]).then_inc(ld_pc, 16)
            sp.wait_ge(f0_rdy, 1)
            for n in range(16):
                if n >= 4:
                    sp.wait_ge(st_done, n - 3)
                sp.dma_start(stage[n % 4], inp["w13"][:, 768 * n:768 * (n + 1)]).then_inc(ld_st[n % 4], 16)
            sp.wait_ge(c_rdy, 4)
            sp.dma_start(w2f, inp["w2"]).then_inc(ld_w2, 16)
            sp.dma_start(RT, inp["routing"]).then_inc(ld_rt, 16)
            sp.dma_start(RT16, inp["routing16"]).then_inc(ld_rt, 16)
            sp.dma_start(rows_x[0:P, :], inp["zeros"].bitcast(F16)[0:P, 0:256]).then_inc(st_rows, 16)
            sp.dma_start(out[0:P, :], inp["zeros"][0:P, 0:C]).then_inc(st_init, 16)
            sp.dma_start(sum_odd.rearrange("r c -> (r c)"), inp["zeros"].rearrange("r c -> (r c)")).then_inc(st_init, 16)
            sp.wait_ge(x_rdy, XD[3])
            sp.dma_start(out[P:, :].rearrange("(p j) c -> p j c", p=P), X).then_inc(st_init, 16)
            sp.wait_ge(ln_lo, 4 * NG)
            sp.dma_start(rows_x[P:, :].rearrange("(p j) n -> p j n", p=P),
                         xrow.rearrange("p j s n -> p j (s n)")).then_inc(st_rows, 16)

        @block.tensor
        def _(pe):
            def norm_transposes(L):
                if L == 0:
                    pe.wait_ge(ld_small, LD_SMALL)
                for g in range(NG):
                    pe.wait_ge(ln_lo, NG * L + g + 1)
                    if g >= 2:
                        pe.wait_ge(xs_rdy, NG * L + g - 1)
                    elif L:
                        pass
                    for s in range(2):
                        dst = bank(2 * (g % 2) + s).bitcast(F16)
                        for j in range(4):
                            mm = pe.transpose(dst[:, j * P:(j + 1) * P], xrow[:, 4 * g + j, s, :], ident[:])
                    mm.then_inc(ln_tp, 1)

            def attention():
                pe.wait_ge(wp_rdy, 1)
                pe.wait_ge(xs_rdy, NG)
                for hg in range(2):
                    if hg:
                        pe.wait_ge(s_added, 4)
                        pe.wait_ge(centred, 4)
                        pe.wait_ge(o_read, 4)
                    for n, (kind, k) in enumerate(ORDER):
                        N = hg * UNITS + n
                        o = bank(N % 8)
                        if n >= 8:
                            if ORDER[n - 8][0] == "v":
                                pe.wait_ge(v_free, count("v", hg, n - 8))
                            else:
                                pe.wait_ge(unit_free, count("nmqkac", hg, n - 8))
                        if kind in "nmqk":
                            col = TYPE[kind] * 256 + hg * P
                            for i, xs in enumerate((XHw, XLw)):
                                mv = xs[:, k * 1024:(k + 1) * 1024].rearrange("p (b y v) -> p b y v", y=2, v=8)[:, :, 0, :]
                                mm = pe.matmul(o, WP[:, col:col + P], mv, start=(i == 0), stop=(i == 1))
                        elif kind == "v":
                            for b4 in range(4):
                                b = 4 * k + b4
                                ob = o[:, b4 * P:(b4 + 1) * P]
                                for i, xs in enumerate((XHw, XLw)):
                                    pe.matmul(ob, xs[:, b * P:(b + 1) * P],
                                              WP[:, 1024 + hg * P:1024 + (hg + 1) * P], start=(i == 0), stop=False)
                                mm = pe.matmul(ob, ones2[:], bv2[:, hg * P:(hg + 1) * P], start=False, stop=True)
                        elif kind == "a":
                            if k == 0:
                                pe.wait_ge(unit_free, count("nmqkac", hg, last("n")))
                                pe.wait_ge(en_hi, hg + 1)
                                pe.wait_ge(en_lo, hg + 1)
                            for o16 in range(16):
                                oi, oj = divmod((k % 4) * 16 + o16, 8)
                                for i, (tab, mv) in enumerate(((ENh, nh), (ENh, nl), (ENl, nh))):
                                    mm = pe.matmul(o[:, o16 * NW:(o16 + 1) * NW],
                                                   tab[:, k // 4, oj, (7 - oi) * 16:(15 - oi) * 16],
                                                   mv[:, 8 * oi + oj::PW], start=(i == 0), stop=(i == 2))
                        else:
                            if k == 0:
                                pe.wait_ge(em_hi, hg + 1)
                                pe.wait_ge(em_lo, hg + 1)
                            for i16 in range(16):
                                ii, ij = divmod((k % 4) * 16 + i16, 8)
                                for i, (tab, mv) in enumerate(((EMh, mh), (EMh, ml), (EMl, mh))):
                                    mm = pe.matmul(o[:, i16 * NW:(i16 + 1) * NW],
                                                   tab[:, k // 4, ij, (7 - ii) * 16:(15 - ii) * 16],
                                                   mv[:, 8 * ii + ij::PW], start=(i == 0), stop=(i == 2))
                        mm.then_inc(unit_rdy, 1)

                    def scores(c):
                        cg = hg * 4 + c
                        if c == 0:
                            pe.wait_ge(unit_free, count("nmqkac", hg, UNITS - 1))
                            pe.wait_ge(v_free, count("v", hg, UNITS - 1))
                        if cg >= 2:
                            pe.wait_ge(s_added, cg - 1)
                        for b8 in range(8):
                            b = c * 8 + b8
                            for hp in range(2):
                                o = bank(2 * (cg % 2) + hp)[:, b8 * PW:(b8 + 1) * PW]
                                qs = slice(b * PW, (b + 1) * PW)
                                pe.matmul(o, wk(KH, hp, b), qh[:, qs], start=True, stop=False)
                                pe.matmul(o, wk(KH, hp, b), ql[:, qs], start=False, stop=False)
                                pe.matmul(o, wk(KL, hp, b), qh[:, qs], start=False, stop=False)
                                idn = sel[:, hp * PW:(hp + 1) * PW]
                                pe.matmul(o, Ch[:, b, :], idn, start=False, stop=False)
                                mm = pe.matmul(o, Cl[:, b, :], idn, start=False, stop=True)
                        mm.then_inc(st_rdy, 1)

                    def means(c):
                        cg = hg * 4 + c
                        pe.wait_ge(s_added, cg + 1)
                        if cg >= 1:
                            pe.wait_ge(centred, cg)
                        for hp in range(2):
                            mm = pe.matmul(bank(4 + hp), CEN[:], S_[cg % 3][:, hp * BANK:(hp + 1) * BANK],
                                           start=True, stop=True)
                        mm.then_inc(mean_rdy, 1)

                    def values(c):
                        cg = hg * 4 + c
                        pe.wait_ge(centred, cg + 1)
                        if cg >= 1:
                            pe.wait_ge(o_read, cg)
                        for b8 in range(8):
                            for hp in range(2):
                                pe.matmul(bank(6)[64 * hp:64 * hp + 64, b8 * PW:(b8 + 1) * PW],
                                          V[:, c * 8 + b8, hp, :],
                                          S_[cg % 3][:, hp * BANK + b8 * PW:hp * BANK + (b8 + 1) * PW],
                                          start=True, stop=True)
                        pe.wait_ge(squared, cg + 1)
                        for hp in range(2):
                            mm = pe.matmul(bank(7)[64 * hp:64 * hp + 64, :], VAR[:],
                                           Sq[cg % 2][:, hp * BANK:(hp + 1) * BANK], start=True, stop=True)
                        mm.then_inc(sv_rdy, 1)

                    for c in range(4 + 2):
                        if c < 4:
                            scores(c)
                        if 1 <= c < 5:
                            means(c - 1)
                        if c >= 2:
                            values(c - 2)
                pe.wait_ge(o_lo, 8)
                pe.wait_ge(wf_rdy, 1)
                for j in range(NT):
                    o = bank(j // 8)[:, (j % 8) * C:(j % 8 + 1) * C]
                    n = 0
                    for hg in range(2):
                        ts = slice(j * P, (j + 1) * P)
                        for a, w in ((OTh, wfh), (OTl, wfh), (OTh, wfl)):
                            mm = pe.matmul(o, a[hg][:, ts], w[:, hg, :], start=(n == 0), stop=(n == 5))
                            n += 1
                    if j % 8 == 7:
                        mm.then_inc(proj_rdy, 1)

            def ffn0():
                pe.wait_ge(xs_rdy, 2 * NG)
                pe.wait_ge(gw_rdy, 1)
                logits(0, bank(7))
                pe.wait_ge(f0_rdy, 1)

                def hidden(it):
                    blk, e = divmod(it, 8)
                    if it >= 2:
                        pe.wait_ge(g_rdy, it - 1)
                    for i, xs in enumerate((XH, XL)):
                        mm = pe.matmul(bank(it % 2), W1g[:, e * P:(e + 1) * P], XW(xs, blk), start=(i == 0), stop=(i == 1))
                    mm.then_inc(h_rdy, 1)

                def outputs(it):
                    blk, e = divmod(it, 8)
                    pe.wait_ge(g_lo, it + 1)
                    for jt in range(4):
                        t = 4 * blk + jt
                        o = bank(2 + t % 6)
                        if e == 0:
                            if t == 5:
                                pe.wait_ge(lg_read, 1)
                            if t >= 6:
                                pe.wait_ge(y_read, t - 5)
                            pe.matmul(o, ones2[:], b2r[:], start=True, stop=False)
                        for i, (a, w) in enumerate(((gh, W2gh), (gl, W2gh), (gh, W2gl))):
                            mm = pe.matmul(o[:, e * C:(e + 1) * C], a[it % 2][:, jt * P:(jt + 1) * P],
                                           w[:, e * C:(e + 1) * C], start=False, stop=(e == 7 and i == 2))
                    mm.then_inc(y_used, 1)

                for it in range(32 + 2):
                    if it < 32:
                        hidden(it)
                    if it >= 2:
                        outputs(it - 2)

            def logits(n, o):
                for j in range(NT):
                    for i, xs in enumerate((XH, XL)):
                        mm = pe.matmul(o[:, 8 * j:8 * j + 8], xs[:, j * P:(j + 1) * P], GW[:, 8 * n:8 * n + 8],
                                       start=(i == 0), stop=(i == 1))
                mm.then_inc(lg_rdy, 1)

            def convolution():
                pe.wait_ge(xs_rdy, 3 * NG)
                for k in range(4):
                    for i8 in range(8):
                        i = 8 * k + i8
                        col = (i % 16) * P + (i // 16) * 64
                        for n, xs in enumerate((XH, XL)):
                            mm = pe.matmul(bank(4 + k)[0:64, i8 * 64:(i8 + 1) * 64], xs[:, col:col + 64], FW[:],
                                           start=(n == 0), stop=(n == 1))
                    mm.then_inc(a_rdy, 1)
                pe.wait_ge(xf_rdy, 4)
                pe.wait_ge(pw_rdy, 1)
                for m16 in range(16):
                    for mh in range(2):
                        m = 16 * mh + m16
                        mm = pe.matmul(PS[64 * mh:64 * mh + 64, m16 * 64:(m16 + 1) * 64],
                                       XF[:, m, :, :].rearrange("p r i -> p (r i)")[0:64],
                                       PCTW[:, m, :, :].rearrange("p b l -> p (b l)")[0:64], start=True, stop=True)
                mm.then_inc(b_rdy, 1)
                pe.wait_ge(sx_act, 1)
                pe.wait_ge(sx_dve, 1)
                for mb in range(4):
                    for m8 in range(8):
                        m = 8 * mb + m8
                        if m % 4 == 0:
                            pe.wait_ge(ld_wc[m // 4], 16)
                        for q in range(2):
                            for g in range(4):
                                lq = 2 * g + q
                                base = (m * 8 + lq) * 32 - 16 * q
                                mm = pe.matmul(bank(2 + mb)[32 * g:32 * g + 32, m8 * 64:(m8 + 1) * 64],
                                               SXF[:, base:base + 32], WC[m // 4][:, m % 4, lq, :],
                                               start=(q == 0), stop=(q == 1))
                    mm.then_inc(c_rdy, 1)
                pe.wait_ge(pri_rdy, 1)
                for mb in range(4):
                    pe.wait_ge(z_act, mb + 1)
                    pe.wait_ge(z_dve, mb + 1)
                    for m8 in range(8):
                        m = 8 * mb + m8
                        o = bank((6, 7, 0, 1)[mb])[0:64, m8 * 64:(m8 + 1) * 64]
                        for n, c0 in ((0, 32), (1, 0)):
                            mm = pe.matmul(o, PRI[n][:, m, :, :].rearrange("p b t -> p (b t)"), Z3[:, m, c0:c0 + 64],
                                           start=(n == 0), stop=(n == 1))
                    mm.then_inc(d_rdy, 1)
                pe.wait_ge(yt_in, 4)
                for og in range(8):
                    for r in range(2):
                        mm = pe.transpose(PS[:, 2 * BANK + (2 * og + r) * 64:2 * BANK + (2 * og + r + 1) * 64],
                                          Y[0:64, r, 4 * og:4 * og + 4, :].rearrange("p o m -> p (o m)"), identf[:])
                    if og % 4 == 3:
                        mm.then_inc(t_rdy, 1)
                pe.wait_ge(ld_gi, 16)
                for n in range(2):
                    pe.wait_ge(yt_rdy, 2)
                    for og4 in (2 * n, 2 * n + 1):
                        for r in range(2):
                            for b in range(2):
                                for oh in range(2):
                                    q = 64 * b + 32 * oh
                                    mm = pe.matmul(bank(4 + n)[q:q + 32, (og4 % 2) * 256:(og4 % 2) * 256 + 256],
                                                   YT[:, 4 * oh + og4, r, 32 * b:32 * b + 32], GI[:, r, :],
                                                   start=(r == 0), stop=(r == 1))
                    mm.then_inc(e_rdy, 1)

            def ffn1():
                pe.wait_ge(xs_rdy, 4 * NG)
                logits(1, bank(7))

                pe.wait_ge(pick_rdy, 1)
                pe.wait_ge(ld_rt, 32)
                pe.matmul(bank(6)[:, 0:(NT + 1) * 8], tri, picked, start=True, stop=False)
                for j in range(NT):
                    n = NT - j
                    mm = pe.matmul(bank(6)[:, 8 * (j + 1):8 * (NT + 1)].rearrange("p (j e) -> p j e", e=8), ones,
                                   picked[:, 8 * j:8 * j + 8].unsqueeze(1).broadcast_to([P, n, 8]), start=False,
                                   stop=(j == NT - 1))
                mm.then_inc(rank_rdy, 1)
                pe.wait_ge(map_in, 1)
                for c in range(32):
                    mm = pe.matmul(bank(7)[:, 0:3 * NBLK], OR[:, c, :], OBX[:, c, :, :].rearrange("p v b -> p (v b)"),
                                   start=(c == 0), stop=(c == 31))
                mm.then_inc(map_rdy, 1)
                pe.wait_ge(exp_rdy, 1)
                pe.wait_ge(w2_rdy, 1)
                pe.wait_ge(st_done, 16)

                expert, word = {}, [0]

                def transposes(b):
                    pe.wait_ge(gathered[b % 4], 16 * (b // 4 + 1))
                    if b >= 2:
                        pe.wait_ge(xb_rdy, b - 1)
                    dst = bank(4 + b % 2).bitcast(F16)
                    for s in range(2):
                        mm = pe.transpose(dst[:, s * P:(s + 1) * P], xg[b % 4][:, s * P:(s + 1) * P], ident[:])
                    mm.then_inc(tp_rdy, 1)
                    if b % 8 == 0:
                        word[0] = pe.value_load(word_i[:, b // 8:b // 8 + 1], min_val=0, max_val=8 ** 8 - 1)
                    expert[b] = word[0] // 8 ** (b % 8) % 8

                def hidden(b, half):
                    if half == 0:
                        pe.wait_ge(xb_rdy, b + 1)
                    if b:
                        pe.wait_ge(gg_rdy, 2 * b + half - 1)
                    for w in range(2):
                        for c in range(3):
                            wt = W13[:, bass.ds(expert[b], 1), w, (3 * half + c) * P:(3 * half + c + 1) * P]
                            for i in range(2):
                                mm = pe.matmul(bank(2 * w + half)[:, c * P:(c + 1) * P], wt.rearrange("p a n -> p (a n)"),
                                               xb[b % 2][:, i * P:(i + 1) * P], start=(i == 0), stop=(i == 1))
                    mm.then_inc(hh_rdy, 1)

                def outputs(b, half):
                    pe.wait_ge(gg_lo, 2 * b + half + 1)
                    if half == 0 and b >= 2:
                        pe.wait_ge(ys_rdy, b - 1)
                    n, o = 2 * (b % 2) + half, bank(6 + b % 2)
                    for c in range(3):
                        wt = W2[:, bass.ds(expert[b], 1), 3 * half + c, :, :].rearrange("p a s n -> p (a s n)")
                        cs = slice(c * P, (c + 1) * P)
                        pe.matmul(o[:, 0:2 * C], fh[n][:, cs], wt, start=(half == 0 and c == 0), stop=False)
                        mm = pe.matmul(o[:, 0:C], fl[n][:, cs], wt[:, 0:C], start=False, stop=(half == 1 and c == 2))
                    mm.then_inc(yy_used, 1)

                transposes(0)
                for b in range(NBLK + 2):
                    if b + 1 < NBLK:
                        transposes(b + 1)
                    if b < NBLK:
                        hidden(b, 0)
                    if b >= 2:
                        outputs(b - 2, 1)
                    if b < NBLK:
                        hidden(b, 1)
                    if 1 <= b <= NBLK:
                        outputs(b - 1, 0)

            norm_transposes(0)
            attention()
            norm_transposes(1)
            ffn0()
            norm_transposes(2)
            convolution()
            norm_transposes(3)
            ffn1()

        @block.scalar
        def _(act):
            def norm(L, eps, window_order):
                for g in range(NG):
                    act.wait_ge(ln_xc, NG * L + g + 1)
                    act.activation(sq[:, 4 * g:4 * g + 4, :], xc[:, 4 * g:4 * g + 4, :], ACT.Square,
                                   scale=1.0 / 8).then_inc(ln_sq, 1)
                for g in range(NG):
                    act.wait_ge(ln_var, NG * L + g + 1)
                    act.activation(dev[:, 4 * g:4 * g + 4], var[:, 4 * g:4 * g + 4], ACT.Sqrt,
                                   bias=mask[:, eps:eps + 1]).then_inc(ln_dev, 1)
                for g in range(NG):
                    act.wait_ge(ln_xn, NG * L + g + 1)
                    src = xc[:, 4 * g:4 * g + 4, :].unsqueeze(2).broadcast_to([P, 4, 2, C])
                    act.copy(xrow[:, 4 * g:4 * g + 4, 0, :].rearrange("p j (n c) -> p j n c", n=2), src).then_inc(ln_hi, 1)
                for g in range(NG):
                    act.wait_ge(ln_tp, NG * L + g + 1)
                    for s, (dst, win) in enumerate(((XH, XHw), (XL, XLw))):
                        src = bank(2 * (g % 2) + s).bitcast(F16)[:, 0:BANK]
                        if window_order:
                            for y in range(2):
                                ins = act.copy(windowed(win, g, 0, y), src.rearrange("p (j b v) -> p j b v", j=4, v=8))
                        elif L == 2:
                            for b in range(2):
                                d = dst[:, g * BANK:(g + 1) * BANK].rearrange("p (j o b t) -> p j o b t", j=4, o=2, b=2)
                                ins = act.copy(d[:, :, :, b, :],
                                               src.rearrange("p (j b o t) -> p j b o t", j=4, b=2, o=2)[:, :, b, :, :])
                        else:
                            ins = act.copy(dst[:, g * BANK:(g + 1) * BANK], src)
                    ins.then_inc(xs_rdy, 1)

            act.wait_ge(ld_wp, 16)
            act.copy(wpH, wpf).then_inc(wp_hi, 1)
            act.wait_ge(ld_small, LD_SMALL)
            norm(0, 8, True)
            act.wait_ge(ld_tbl, 16)
            act.wait_ge(ln_tp, NG)
            act.copy(TH, tblf).then_inc(tb_hi, 1)
            act.wait_ge(tb_hi, 1)
            for c in range(4):
                ins = spread(act, TH, 0, 0, c, True)
            ins.then_inc(en_hi, 1)
            act.copy(bv2h, bv2f).then_inc(bv_hi, 1)
            act.copy(wfh[:], wff).then_inc(wf_hi, 1)
            for hg in range(2):
                for n, (kind, k) in enumerate(ORDER):
                    if (kind, k) == ("a", 4):
                        if hg:
                            act.wait_ge(sv_rdy, 4)
                        for c in range(4):
                            ins = spread(act, TH, 1, hg, c, True)
                        ins.then_inc(em_hi, 1)
                    if kind == "a":
                        continue
                    N = hg * UNITS + n
                    o = bank(N % 8)
                    act.wait_ge(unit_rdy, N + 1)
                    if kind in "nmq":
                        dst = {"n": nh, "m": mh, "q": qh}[kind]
                        ins = act.activation(XW(dst, k), o, ACT.Identity, bias=bcol(kind, hg))
                    elif kind == "k":
                        if hg == 0 and k == 0:
                            act.wait_ge(zeroed, 2)
                        for c in range(4):
                            r = slice(32 * c, 32 * c + 32)
                            ins = act.activation(diagonal(KH, c, k), o[r, :].rearrange("p (b v) -> p b v", v=8),
                                                 ACT.Identity, bias=bcol(kind, hg)[r, :])
                    elif kind == "v":
                        src = o.rearrange("p (b n) -> p b n", n=HD)
                        for y in range(2):
                            ins = act.mul(V[:, 4 * k:4 * k + 4, :, 32 * y:32 * y + 32].rearrange("p b h d -> p (b h) d"),
                                          src[:, y::2, :], mask[:, 5 + y:6 + y])
                    else:
                        ins = act.copy(cols_c(Ch, k), o.rearrange("p (u v b) -> p u v b", u=2, b=NW))
                    ins.then_inc(v_free if kind == "v" else unit_hi, 1)
                for c in range(6):
                    if c < 4 and hg == 0:
                        ins = spread(act, TH, 0, 1, c, True)
                        if c == 3:
                            ins.then_inc(en_hi, 1)
                    if c >= 2:
                        cg = hg * 4 + c - 2
                        act.wait_ge(sv_rdy, cg + 1)
                        if cg >= 2:
                            act.wait_ge(o_read, cg - 1)
                        act.activation(rsc[cg % 2], bank(7), ACT.Sqrt, bias=mask[:, 7:8]).then_inc(std_rdy, 1)
                        act.wait_ge(o_read, cg + 1)
                        act.copy(ots(OTh, hg, c - 2), O32[cg % 2].rearrange("p (j t) -> p j t", t=64)).then_inc(o_hi, 1)

            def expert_stage(n):
                act.wait_ge(ld_st[n % 4], 16 * (n // 4 + 1))
                act.copy(stageH[n % 4], stage[n % 4]).then_inc(st_hi, 1)

            def ffn0():
                act.copy(GH[:], small[:, 0:16]).then_inc(gh_hi, 1)
                act.wait_ge(ld_f0, 48)
                act.copy(w1gH, w1gf)
                act.copy(W2gh, w2gf)
                act.copy(b2H, b2f).then_inc(f0_hi, 1)

            def gates():
                act.wait_ge(ex_in, gates.n + 1)
                gates.n += 1
                act.activation(ex, ex, ACT.Exp).then_inc(ex_rdy, 1)
            gates.n = 0

            def ffn0_main():
                for it in range(32):
                    e = it % 8
                    act.wait_ge(h_rdy, it + 1)
                    if it >= 2:
                        act.wait_ge(g_lo, it - 1)
                    act.activation(g32[it % 2], bank(it % 2), ACT.Gelu, bias=b1c[:, e:e + 1]).then_inc(g_rdy, 1)
                    if it % 2 == 1:
                        expert_stage(it // 2)

            def convolution():
                act.wait_ge(wb_rdy, 1)
                act.wait_ge(ld_pc, 32)
                act.wait_ge(y_read, NT)
                for b in range(2):
                    ins = act.mul(PCTW[0:64, :, b, :], pctf, wb[0:64, b:b + 1])
                ins.then_inc(pw_rdy, 1)
                norm(2, 8, False)
                act.wait_ge(pw_rdy, 1)
                for k in (0, 2):
                    act.wait_ge(a_rdy, k + 1)
                    act.copy(spectrum(k), bank(4 + k)[0:64, :].rearrange("p (i n) -> p i n", i=8)).then_inc(xf_rdy, 1)
                act.wait_ge(b_rdy, 1)
                act.wait_ge(sx_zero, 1)
                for n in range(8):
                    ins = act.copy(*mixing(n))
                ins.then_inc(sx_act, 1)
                for mb in range(4):
                    act.wait_ge(c_rdy, mb + 1)
                    act.copy(Z3[:, 8 * mb:8 * mb + 8, 32:96],
                             bank(2 + mb).rearrange("p (m n) -> p m n", n=64)).then_inc(z_act, 1)
                act.wait_ge(xf_rdy, 4)
                for mb in (0, 2):
                    act.wait_ge(d_rdy, mb + 1)
                    act.copy(modes(mb), bank((6, 7, 0, 1)[mb])[0:64, :].rearrange("p (m n) -> p m n", n=64)).then_inc(yt_in, 1)
                act.wait_ge(t_rdy, 1)
                act.copy(YT[:, 0:4, :, :].rearrange("p g r n -> p (g r n)"), bank(2)).then_inc(yt_rdy, 1)

            def ffn1():
                act.wait_ge(ld_w2, 16)
                act.copy(W2hi, w2v).then_inc(w2_hi, 1)
                norm(3, 7, False)
                gates()

                def high(b, odd, half):
                    act.wait_ge(gg_rdy, 2 * b + half + 1)
                    if not (isinstance(b, int) and b < 2):
                        act.wait_ge(yy_used, 2 * b + half - 3)
                    act.copy(fh[2 * odd + half], f32[half]).then_inc(gg_hi, 1)

                def outputs(b, u4, turn):
                    act.wait_ge(yy_used, 2 * b + 2)
                    if not (isinstance(b, int) and b < 4):
                        act.wait_ge(added[u4 % 2], 16 * (2 * turn + u4 // 2 - 1))
                    act.mul(ys[u4], bank(6 + u4 % 2)[:, 0:C], gate[:, bass.ds(b, 1)]).then_inc(ys_hi, 1)

                def step(b, u4, turn):
                    for half in range(2):
                        act.wait_ge(hh_rdy, 2 * b + half + 1)
                        if not (isinstance(b, int) and b == 0):
                            act.wait_ge(gg_rdy, 2 * b + half - 1)
                        act.activation(s32[half], bank(half)[:, 0:HALF], ACT.Silu).then_inc(s_rdy, 1)
                        if half:
                            high(b, u4 % 2, 0)
                        elif not (isinstance(b, int) and b == 0):
                            high(b - 1, (u4 + 1) % 2, 1)
                    if not (isinstance(b, int) and b < 2):
                        outputs(b - 2, (u4 + 2) % 4, turn if u4 >= 2 else turn - 1)

                act.wait_ge(gate_rdy, 1)
                for b in range(8):
                    step(b, b % 4, b // 4)
                with act.Fori(2, NBLK // 4) as i:
                    for u in range(4):
                        step(4 * i + u, u, i)
                for b in range(NBLK // 4 * 4, NBLK):
                    step(b, b % 4, b // 4)
                high(NBLK - 1, (NBLK - 1) % 2, 1)
                for b in (NBLK - 2, NBLK - 1):
                    outputs(b, b % 4, b // 4)

            ffn0()
            norm(1, 7, False)
            gates()
            ffn0_main()
            convolution()
            ffn1()

        @block.gpsimd
        def _(pool):
            pool.memset(at(44 * K, 4096), 0.0).then_inc(zeroed, 1)
            pool.memset(at(60 * K, 4096), 0.0).then_inc(zeroed, 1)
            pool.wait_ge(ln_xc, NG)
            pool.wait_ge(ld_small, LD_SMALL)
            pool.tensor_tensor(X, X, bfin[:].unsqueeze(1).broadcast_to([P, NT, C]), ALU.add).then_inc(bfin_added, 1)
            for hg in range(2):
                for c in range(6):
                    if 1 <= c < 5:
                        cg = hg * 4 + c - 1
                        pool.wait_ge(centred, cg + 1)
                        if cg >= 2:
                            pool.wait_ge(sv_rdy, cg - 1)
                        pool.tensor_tensor(Sq[cg % 2], S_[cg % 3], S_[cg % 3], ALU.mult).then_inc(squared, 1)
                    if c >= 2:
                        cg = hg * 4 + c - 2
                        pool.wait_ge(o_hi, cg + 1)
                        pool.tensor_tensor(ots(OTl, hg, c - 2), O32[cg % 2].rearrange("p (j t) -> p j t", t=64),
                                           ots(OTh, hg, c - 2), ALU.subtract).then_inc(o_lo, 1)

            for it in range(32):
                pool.wait_ge(g_rdy, it + 1)
                if it >= 2:
                    pool.wait_ge(y_used, it - 1)
                pool.tensor_copy(gh[it % 2], g32[it % 2]).then_inc(g_hi, 1)
            pool.wait_ge(st_done, 16)
            pool.memset(SXF, 0.0).then_inc(sx_zero, 1)
            pool.wait_ge(ld_pc, 32)
            for n in range(2):
                for b in range(2):
                    ins = pool.tensor_scalar(PRI[n][:, :, b, :], pctr, pmask[:, 2 * n + b:2 * n + b + 1], None, ALU.mult)
            ins.then_inc(pri_rdy, 1)

            pool.wait_ge(row_rdy, 1)
            pool.wait_ge(st_rows, 32)
            pool.wait_ge(st_init, 48)

            def gather(b):
                if b >= 4:
                    pool.wait_ge(tp_rdy, b - 3)
                pool.indirect_dma_start(xg[b % 4], None, rows_x, bass.IndirectOffsetOnAxis(ap=row_i[:, b:b + 1], axis=0)
                                        ).then_inc(gathered[b % 4], 16)

            for b in range(6):
                gather(b)
            for b in range(NBLK):
                if b + 6 < NBLK:
                    gather(b + 6)
                pool.wait_ge(ys_rdy, b + 1)
                if b >= 2:
                    pool.wait_ge(added[b % 2], 16 * (b // 2))
                pool.indirect_dma_start((out, sum_odd)[b % 2], bass.IndirectOffsetOnAxis(ap=row_i[:, b:b + 1], axis=0),
                                        ys[b % 4], None, compute_op=ALU.add).then_inc(added[b % 2], 16)
            for n in range(2):
                pool.wait_ge(added[n], 16 * ((NBLK + 1 - n) // 2))
            pool.dma_start(out[P:, :], sum_odd[P:, :], accum_op=ALU.add, max_dma_last_dim=4096).then_inc(st_out, 16)
            pool.wait_ge(st_out, 16)

        @block.vector
        def _(dve):
            steps = [0]

            def link(ins):
                steps[0] += 1
                ins.then_inc(vec, 1)
                dve.wait_ge(vec, steps[0])

            def rows(a, g):
                return a[:, 4 * g:4 * g + 4, :]

            def wide(a, g):
                return a[:, 4 * g:4 * g + 4].unsqueeze(2).broadcast_to([P, 4, C])

            def norm(L):
                for g in range(NG):
                    link(dve.tensor_reduce(mu[:, 4 * g:4 * g + 4], rows(X, g), AX_X, ALU.add))
                    link(dve.tensor_scalar(mu[:, 4 * g:4 * g + 4], mu[:, 4 * g:4 * g + 4], 1.0 / C, None, ALU.mult))
                    dve.tensor_tensor(rows(xc, g), rows(X, g), wide(mu, g), ALU.subtract).then_inc(ln_xc, 1)
                for g in range(NG):
                    dve.wait_ge(ln_sq, NG * L + g + 1)
                    dve.tensor_reduce(var[:, 4 * g:4 * g + 4], rows(sq, g), AX_X, ALU.add).then_inc(ln_var, 1)
                for g in range(NG):
                    dve.wait_ge(ln_dev, NG * L + g + 1)
                    link(dve.reciprocal(dev[:, 4 * g:4 * g + 4], dev[:, 4 * g:4 * g + 4]))
                    dve.wait_ge(ln_xc, NG * L + g + 1)
                    dve.tensor_tensor(rows(xc, g), rows(xc, g), wide(dev, g), ALU.mult).then_inc(ln_xn, 1)
                for g in range(NG):
                    dve.wait_ge(ln_hi, NG * L + g + 1)
                    hi, lo = [xrow[:, 4 * g:4 * g + 4, s, :].rearrange("p j (n c) -> p j n c", n=2) for s in range(2)]
                    dve.tensor_tensor(lo, rows(xc, g).unsqueeze(2).broadcast_to([P, 4, 2, C]), hi,
                                      ALU.subtract).then_inc(ln_lo, 1)

            dve.wait_ge(ld_x, 16)
            norm(0)
            dve.wait_ge(wp_hi, 1)
            dve.wait_ge(ld_small, LD_SMALL)
            dve.scalar_tensor_tensor(WP[:], wpH, mask[:, 4:5], wpf, ALU.mult, ALU.add).then_inc(wp_rdy, 1)
            dve.wait_ge(tb_hi, 1)
            link(dve.tensor_tensor(TL, tblf, TH, ALU.subtract))
            for c in range(4):
                ins = spread(dve, TL, 0, 0, c, False)
            ins.then_inc(en_lo, 1)
            dve.wait_ge(bv_hi, 1)
            dve.scalar_tensor_tensor(bv2[:], bv2h, mask[0:2, 9:10], bv2f, ALU.mult, ALU.add)
            dve.wait_ge(wf_hi, 1)
            dve.tensor_tensor(wfl[:], wff, wfh[:], ALU.subtract).then_inc(wf_rdy, 1)

            def attention():
                for hg in range(2):
                    for n, (kind, k) in enumerate(ORDER):
                        if (kind, k) == ("a", 4):
                            if hg:
                                dve.wait_ge(sv_rdy, 4)
                            for c in range(4):
                                ins = spread(dve, TL, 1, hg, c, False)
                            ins.then_inc(em_lo, 1)
                        if kind == "v":
                            continue
                        N = hg * UNITS + n
                        o = bank(N % 8)
                        if kind == "a":
                            dve.wait_ge(unit_rdy, N + 1)
                            o0 = (k % 4) * 16
                            bb = biasT[:, 2 * hg + k // 4, o0:o0 + 16].unsqueeze(2).broadcast_to([P, 16, NW])
                            ins = dve.tensor_tensor(AB[:, k // 4, o0:o0 + 16, :], o.rearrange("p (o b) -> p o b", b=NW),
                                                    bb, ALU.add)
                        else:
                            dve.wait_ge(unit_hi, count("nmqkc", hg, n))
                        if kind in "nmq":
                            hi, lo = {"n": (nh, nl), "m": (mh, ml), "q": (qh, ql)}[kind]
                            ins = dve.scalar_tensor_tensor(XW(lo, k), o, bcol(kind, hg), XW(hi, k), ALU.add, ALU.subtract)
                        elif kind == "k":
                            for c in range(4):
                                r = slice(32 * c, 32 * c + 32)
                                ins = dve.scalar_tensor_tensor(
                                    diagonal(KL, c, k), o[r, :].rearrange("p (b v) -> p b v", v=8),
                                    bcol(kind, hg)[r, :], diagonal(KH, c, k), ALU.add, ALU.subtract)
                        elif kind == "c":
                            ins = dve.tensor_tensor(cols_c(Cl, k), o.rearrange("p (u v b) -> p u v b", u=2, b=NW),
                                                    cols_c(Ch, k), ALU.subtract)
                        ins.then_inc(unit_free, 1)
                    dve.wait_ge(unit_free, count("nmqkac", hg, UNITS - 1))

                    for c in range(6):
                        if c < 4:
                            cg = hg * 4 + c
                            dve.wait_ge(st_rdy, cg + 1)
                            if cg >= 3:
                                dve.wait_ge(sv_rdy, cg - 2)
                            a = AB[:, :, :, c * 8:c * 8 + 8].rearrange("p h o b -> p h b o")
                            for hp in range(2):
                                ins = dve.tensor_tensor(
                                    S_[cg % 3][:, hp * BANK:(hp + 1) * BANK].rearrange("p (b o) -> p b o", o=PW),
                                    bank(2 * (cg % 2) + hp).rearrange("p (b o) -> p b o", o=PW),
                                    a[:, hp, :, :], ALU.add)
                            ins.then_inc(s_added, 1)
                        if c < 4 and hg == 0:
                            ins = spread(dve, TL, 0, 1, c, False)
                            if c == 3:
                                ins.then_inc(en_lo, 1)
                        if 1 <= c < 5:
                            cg = hg * 4 + c - 1
                            dve.wait_ge(mean_rdy, cg + 1)
                            dve.tensor_tensor(S_[cg % 3], S_[cg % 3], bank(4, 2), ALU.subtract).then_inc(centred, 1)
                        if c >= 2:
                            cg = hg * 4 + c - 2
                            dve.wait_ge(std_rdy, cg + 1)
                            if cg >= 2:
                                dve.wait_ge(o_lo, cg - 1)
                            link(dve.reciprocal(rsc[cg % 2], rsc[cg % 2]))
                            v = "p (w i j) -> p w i j"
                            ins = dve.tensor_tensor(O32[cg % 2].rearrange("p (i w j) -> p w i j", i=8, w=8),
                                                    bank(6).rearrange(v, w=8, i=8), rsc[cg % 2].rearrange(v, w=8, i=8), ALU.mult)
                            ins.then_inc(o_read, 1)
                dve.wait_ge(bfin_added, 1)
                for n in range(2):
                    dve.wait_ge(proj_rdy, n + 1)
                    dve.tensor_tensor(X[:, 8 * n:8 * n + 8, :], X[:, 8 * n:8 * n + 8, :],
                                      bank(n).rearrange("p (j c) -> p j c", c=C), ALU.add).then_inc(x_rdy, 1)
                dve.wait_ge(x_rdy, 2)

            def wide8(a):
                return a.unsqueeze(2).broadcast_to([P, NT, 8])

            def top_two(n, o):
                dve.wait_ge(lg_rdy, n + 1)
                gb = (g0b.unsqueeze(1).broadcast_to([P, NT, 8]), None)[n]
                src = o[:, 0:128].rearrange("p (j e) -> p j e", e=8)
                if n == 0:
                    ins = dve.tensor_tensor(lg, src, gb, ALU.add)
                else:
                    ins = dve.tensor_copy(lg, src)
                ins.then_inc(lg_read, 1)
                dve.wait_ge(lg_read, n + 1)
                link(dve.tensor_reduce(m1[:], lg, AX_X, ALU.max))
                dve.tensor_tensor(ex, lg, wide8(m1[:]), ALU.subtract).then_inc(ex_in, 1)
                iw = idxw.unsqueeze(1).broadcast_to([P, NT, 8])

                def first_largest(a, m, oh):
                    link(dve.tensor_tensor(eq, a, wide8(m[:]), ALU.is_equal))
                    link(dve.tensor_tensor(sc, eq, iw, ALU.mult))
                    link(dve.tensor_reduce(sm[:], sc, AX_X, ALU.max))
                    link(dve.tensor_tensor(oh, sc, wide8(sm[:]), ALU.is_equal))

                first_largest(lg, m1, oh1)
                f = "p j e -> p (j e)"
                link(dve.scalar_tensor_tensor(l2.rearrange(f), oh1.rearrange(f), -3e38, lg.rearrange(f), ALU.mult, ALU.add))
                link(dve.tensor_reduce(m2[:], l2, AX_X, ALU.max))
                first_largest(l2, m2, oh2)
                link(dve.tensor_tensor(eq, oh1, oh2, ALU.add))
                dve.wait_ge(ex_rdy, n + 1)
                link(dve.tensor_reduce(sm[:], ex, AX_X, ALU.add))
                link(dve.reciprocal(sm[:], sm[:]))
                link(dve.tensor_tensor(ex, ex, wide8(sm[:]), ALU.mult))
                link(dve.tensor_tensor(cw, ex, eq, ALU.mult))
                if n:
                    link(dve.tensor_reduce(sm[:], cw, AX_X, ALU.add))
                    link(dve.tensor_scalar(sm[:], sm[:], 1e-9, None, ALU.add))
                    link(dve.reciprocal(sm[:], sm[:]))
                    link(dve.tensor_tensor(cw, cw, wide8(sm[:]), ALU.mult))

            def weigh(t, o, rdy, rdy_at, read):
                dve.wait_ge(rdy, rdy_at)
                c = cw[:, t, :].unsqueeze(2).broadcast_to([P, 8, C])
                ins = dve.tensor_tensor(tmp.rearrange("p (e c) -> p e c", e=8), o.rearrange("p (e c) -> p e c", e=8), c,
                                        ALU.mult).then_inc(read, 1)
                dve.wait_ge(read, t + 1)
                link(dve.tensor_reduce(red[:], tmp.rearrange("p (e c) -> p c e", e=8), AX_X, ALU.add))
                dve.tensor_tensor(X[:, t, :], X[:, t, :], red[:], ALU.add).then_inc(x_rdy, 1)

            def expert_stage(n):
                dve.wait_ge(st_hi, n + 1)
                dst = W13[:, n % 8, n // 8, :]
                dve.scalar_tensor_tensor(dst, stageH[n % 4], mask[:, 4:5], stage[n % 4], ALU.mult, ALU.add).then_inc(st_done, 1)

            def ffn0():
                dve.wait_ge(gh_hi, 1)
                dve.scalar_tensor_tensor(GW[:], GH[:], mask[:, 4:5], small[:, 0:16], ALU.mult, ALU.add).then_inc(gw_rdy, 1)
                dve.wait_ge(f0_hi, 1)
                dve.scalar_tensor_tensor(W1g, w1gH, mask[:, 4:5], w1gf, ALU.mult, ALU.add)
                dve.tensor_tensor(W2gl, w2gf, W2gh, ALU.subtract)
                dve.scalar_tensor_tensor(b2r[:], b2H, mask[0:2, 9:10], b2f, ALU.mult, ALU.add).then_inc(f0_rdy, 1)
                norm(1)
                dve.wait_ge(ln_lo, 2 * NG)
                top_two(0, bank(7))
                for it in range(32):
                    dve.wait_ge(g_hi, it + 1)
                    if it >= 2:
                        dve.wait_ge(y_used, it - 1)
                    dve.tensor_tensor(gl[it % 2], g32[it % 2], gh[it % 2], ALU.subtract).then_inc(g_lo, 1)
                    if it % 2 == 1:
                        expert_stage(it // 2)
                    if it >= 9 and it % 8 in (1, 2):
                        for t in range(4 * (it // 8 - 1) + 2 * (it % 8 - 1), 4 * (it // 8 - 1) + 2 * (it % 8)):
                            weigh(t, bank(2 + t % 6), y_used, 8 * (t // 4 + 1), y_read)
                for t in range(12, 16):
                    weigh(t, bank(2 + t % 6), y_used, 32, y_read)
                dve.wait_ge(x_rdy, XD[2])

            def convolution():
                link(dve.tensor_scalar(wb, small[:, 48:50], wlat, TWO_PI / 64, ALU.mult, ALU.mult))
                dve.tensor_copy(wb, wb).then_inc(wb_rdy, 1)
                norm(2)
                for k in (1, 3):
                    dve.wait_ge(a_rdy, k + 1)
                    dve.tensor_copy(spectrum(k), bank(4 + k)[0:64, :].rearrange("p (i n) -> p i n", i=8)).then_inc(xf_rdy, 1)
                dve.wait_ge(b_rdy, 1)
                dve.wait_ge(sx_zero, 1)
                for n in range(8, 16):
                    ins = dve.tensor_copy(*mixing(n))
                ins.then_inc(sx_dve, 1)
                for mb in range(4):
                    dve.wait_ge(z_act, mb + 1)
                    dve.tensor_scalar(Z3[:, 8 * mb:8 * mb + 8, 0:32], Z3[:, 8 * mb:8 * mb + 8, 64:96], -1.0, None,
                                      ALU.mult).then_inc(z_dve, 1)
                for mb in (1, 3):
                    dve.wait_ge(d_rdy, mb + 1)
                    dve.tensor_copy(modes(mb), bank((6, 7, 0, 1)[mb])[0:64, :].rearrange("p (m n) -> p m n", n=64)).then_inc(yt_in, 1)
                dve.wait_ge(t_rdy, 2)
                dve.tensor_copy(YT[:, 4:8, :, :].rearrange("p g r n -> p (g r n)"), bank(3)).then_inc(yt_rdy, 1)
                for n in range(2):
                    dve.wait_ge(e_rdy, n + 1)
                    dve.tensor_tensor(X[:, 8 * n:8 * n + 8, :], X[:, 8 * n:8 * n + 8, :],
                                      bank(4 + n).rearrange("p (j c) -> p j c", c=C), ALU.add).then_inc(x_rdy, 1)
                dve.wait_ge(x_rdy, XD[3])

            def ffn1():
                norm(3)
                dve.wait_ge(w2_hi, 1)
                dve.tensor_tensor(W2lo, w2v, W2hi, ALU.subtract).then_inc(w2_rdy, 1)
                dve.wait_ge(ln_lo, 4 * NG)
                top_two(1, bank(7))

                dve.wait_ge(ld_rt, 32)
                dve.memset(picked[:, 8 * NT:], 0.0)
                dve.tensor_copy(picked[:, 0:8 * NT], eq.rearrange("p j e -> p (j e)")).then_inc(pick_rdy, 1)
                c32 = lambda a: a.rearrange("p (c e) -> p c e", e=8)
                link(dve.tensor_tensor(prod.rearrange("p (k n) -> p k n", k=2), oh12,
                                       cw.rearrange("p j e -> p (j e)").unsqueeze(1).broadcast_to([P, 2, P]), ALU.mult))
                link(dve.tensor_reduce(gate2, c32(prod), AX_X, ALU.add))
                link(dve.tensor_copy(gate2h, gate2))
                link(dve.tensor_tensor(gate_rest, gate2, gate2h, ALU.subtract))
                link(dve.tensor_scalar(gate_rest, gate_rest, 2048.0, None, ALU.mult))
                dve.wait_ge(rank_rdy, 1)
                link(dve.tensor_copy(rank, bank(6)[:, 0:(NT + 1) * 8]))
                link(dve.tensor_tensor(above, rank[:, 8 * NT:].unsqueeze(2).broadcast_to([P, 8, 16]), k128, ALU.is_gt))
                link(dve.tensor_reduce(nblk, above, AX_X, ALU.add))
                link(dve.tensor_tensor(partial, before, nblk.unsqueeze(1).broadcast_to([P, 8, 8]), ALU.mult))
                link(dve.tensor_reduce(first, partial, AX_X, ALU.add))
                r3 = rank[:, 0:8 * NT].rearrange("p (j e) -> p j e", e=8)
                link(dve.scalar_tensor_tensor(r3, first.unsqueeze(1).broadcast_to([P, NT, 8]), float(P), r3, ALU.mult, ALU.add))
                link(dve.tensor_tensor(prod.rearrange("p (k n) -> p k n", k=2), oh12,
                                       rank[:, 0:8 * NT].unsqueeze(1).broadcast_to([P, 2, P]), ALU.mult))
                link(dve.tensor_reduce(slot, c32(prod), AX_X, ALU.add))
                link(dve.tensor_copy(slot_i, slot))
                dve.tensor_scalar(blk_i, slot_i, 7, None, ALU.arith_shift_right)
                link(dve.tensor_scalar(pos_i, slot_i, P - 1, None, ALU.bitwise_and))
                dve.tensor_copy(blk_f, blk_i)
                link(dve.tensor_copy(pos_f, pos_i))
                shape = [P, 32, NBLK]
                link(dve.tensor_tensor(OB, iota[:, 0:NBLK].unsqueeze(1).broadcast_to(shape),
                                       blk_f.unsqueeze(2).broadcast_to(shape), ALU.is_equal))
                for v, a in enumerate((row_id, gate2h, gate_rest)):
                    dve.tensor_tensor(OBX[:, :, v, :], OB, a.unsqueeze(2).broadcast_to(shape), ALU.mult)
                for c in range(32):
                    ins = dve.tensor_scalar(OR[:, c, :], iota, pos_f[:, c:c + 1], None, ALU.is_equal)
                ins.then_inc(map_in, 1)
                link(dve.tensor_tensor(end, first, nblk, ALU.add))
                link(dve.tensor_tensor(past, iota[0:1, 0:8 * NW8].unsqueeze(2).broadcast_to([1, 8 * NW8, 8]),
                                       end[0:1, :].unsqueeze(1).broadcast_to([1, 8 * NW8, 8]), ALU.is_ge))
                link(dve.tensor_reduce(exp_f, past, AX_X, ALU.add))
                link(dve.tensor_scalar(exp_f, exp_f, 7.0, None, ALU.min))
                link(dve.tensor_tensor(exp_f, exp_f, digit, ALU.mult))
                link(dve.tensor_reduce(word_f, exp_f.rearrange("p (w b) -> p w b", b=8), AX_X, ALU.add))
                dve.tensor_copy(word_i, word_f).then_inc(exp_rdy, 1)
                dve.wait_ge(map_rdy, 1)
                link(dve.tensor_scalar(pad_row, bank(7)[:, 0:NBLK], 0.0, own_row, ALU.is_equal, ALU.mult))
                dve.scalar_tensor_tensor(row_i, pad_row, float(P - 1), bank(7)[:, 0:NBLK], ALU.add, ALU.add).then_inc(row_rdy, 1)
                link(dve.tensor_copy(gate, bank(7)[:, NBLK:2 * NBLK]))
                dve.scalar_tensor_tensor(gate, bank(7)[:, 2 * NBLK:3 * NBLK], 1.0 / 2048, gate, ALU.mult,
                                         ALU.add).then_inc(gate_rdy, 1)

                def columns(b, odd):
                    dve.wait_ge(tp_rdy, b + 1)
                    if not (isinstance(b, int) and b < 2):
                        dve.wait_ge(hh_rdy, 2 * b - 2)
                    dve.tensor_copy(xb[odd], bank(4 + odd).bitcast(F16)[:, 0:256]).then_inc(xb_rdy, 1)

                def low(b, odd, half):
                    dve.wait_ge(gg_hi, 2 * b + half + 1)
                    if not (isinstance(b, int) and b < 2):
                        dve.wait_ge(yy_used, 2 * b + half - 3)
                    n = 2 * odd + half
                    dve.tensor_tensor(fl[n], f32[half], fh[n], ALU.subtract).then_inc(gg_lo, 1)

                def outputs(b, u4):
                    dve.wait_ge(ys_hi, b + 1)
                    dve.scalar_tensor_tensor(ys[u4], bank(6 + u4 % 2)[:, C:2 * C], gate[:, bass.ds(b, 1)], ys[u4],
                                             ALU.mult, ALU.add).then_inc(ys_rdy, 1)

                def step(b, u4, is_last=False):
                    odd = u4 % 2
                    if not (isinstance(b, int) and b < 3):
                        outputs(b - 3, (u4 + 1) % 4)
                    if not is_last:
                        columns(b + 1, 1 - odd)
                    for half in range(2):
                        dve.wait_ge(s_rdy, 2 * b + half + 1)
                        if not (isinstance(b, int) and b == 0):
                            dve.wait_ge(gg_lo, 2 * b + half - 1)
                        dve.tensor_tensor(f32[half], bank(2 + half)[:, 0:HALF], s32[half], ALU.mult).then_inc(gg_rdy, 1)
                        if half:
                            low(b, odd, 0)
                        elif not (isinstance(b, int) and b == 0):
                            low(b - 1, 1 - odd, 1)

                columns(0, 0)
                for b in range(4):
                    step(b, b)
                with dve.Fori(1, NBLK // 4) as i:
                    for u in range(4):
                        step(4 * i + u, u)
                for b in range(NBLK // 4 * 4, NBLK):
                    step(b, b % 4, is_last=(b == NBLK - 1))
                low(NBLK - 1, (NBLK - 1) % 2, 1)
                for b in (NBLK - 3, NBLK - 2, NBLK - 1):
                    outputs(b, b % 4)

            attention()
            ffn0()
            convolution()
            ffn1()


def kernel(**inputs):
    import numpy as np
    import concourse.bacc as _bacc
    from concourse import mybir as _mybir
    from concourse.bass_utils import run_bass_kernel_spmd as _run

    I = {k: np.asarray(v) for k, v in inputs.items()}
    f32 = np.float32
    p = np.arange(128)
    arr = {}

    def tile_order(x):
        return x.reshape(2, 2, 16, 32, 64).transpose(0, 1, 3, 2, 4).reshape(128, 1024)

    arr["x"] = tile_order(I["x"])
    arr["wprep"] = np.concatenate([I["L0_conv_W_prep"]] * 2, 0)
    bp = I["L0_conv_b_prep"].reshape(5, 2, 128)
    arr["bprep"] = bp[:4].transpose(2, 0, 1).reshape(128, 8)
    arr["bv"] = np.stack([bp[4].reshape(256)] * 2)
    arr["ones"] = np.ones((2, 128), np.float16)
    y = p // 8 % 2
    arr["bfin"] = np.broadcast_to(I["L0_conv_b_fin"][None], (128, 64))
    intr = I["L0_conv_intrinsic"]
    tn = intr[:, ::-1, ::-1, 1:33].transpose(0, 3, 1, 2).reshape(2, 128, 225)
    tm = intr[:, :, :, 33:65].transpose(0, 3, 1, 2).reshape(2, 128, 225)
    arr["tables"] = np.stack([tn, tm], 0).transpose(2, 0, 1, 3).reshape(128, 900)
    ii = np.arange(8)
    r = ii[None, :] - ii[:, None] + 7
    bt = intr[:, r[:, None, :, None], r[None, :, None, :], 0]
    arr["biasT"] = bt.reshape(4, 2, 8, 8, 64).transpose(2, 1, 3, 0, 4).reshape(128, 256)
    o, h2 = (p // 16) * 8 + p % 8, p // 8 % 2
    arr["sel"] = (np.arange(128)[None] == (h2 * 64 + o)[:, None]).astype(np.float16)
    arr["ident"] = np.eye(128, dtype=np.float16)
    m = np.zeros((128, 16), f32)
    for c in range(4):
        m[:, c] = (p // 32 == c)
    m[:, 4] = -(p >= 64).astype(f32)
    m[:, 5], m[:, 6] = y == 0, y == 1
    m[:, 7], m[:, 8] = EPS_A, EPS_C
    m[1, 9] = -1
    arr["mask"] = m
    arr["cen"] = (y[:, None] == y[None, :]).astype(f32) / f32(64)
    arr["varm"] = (y[:, None] == np.arange(64)[None, :] // 32).astype(f32) / f32(63)
    arr["wfin"] = I["L0_conv_W_fin"].reshape(2, 128, 64).transpose(1, 0, 2).reshape(128, 128)

    arr["identf"] = np.eye(64, dtype=f32)
    W1 = I["L0_ffn_W1"].transpose(1, 0, 2).reshape(64, 1024)
    arr["w1g"] = np.concatenate([W1, W1])
    arr["w2g"] = I["L0_ffn_W2"].transpose(1, 0, 2).reshape(128, 512)
    arr["b2g"] = np.stack([I["L0_ffn_b2"].reshape(512)] * 2)
    sm = np.zeros((128, 64), f32)
    sm[:, 0:8] = np.concatenate([I["L0_ffn_gate_w"]] * 2)
    sm[:, 8:16] = np.concatenate([I["L1_ffn_router_w"].T] * 2)
    sm[:, 16:24] = I["L0_ffn_gate_b"][None]
    sm[:, 24:32] = I["L0_ffn_b1"].T
    sm[:, 32:40] = 8 - np.arange(8)
    sm[:, 40] = I["L1_conv_w"][p % 32]
    for b in range(2):
        sm[:, 42 + b] = (p // 2 % 2 == b) & (p % 2 == 0)
        sm[:, 44 + b] = (p // 2 % 2 == b) & (p % 2 == 1)
        sm[:, 48 + b] = p // 32 == b
    arr["small"] = sm
    n, mm = np.arange(64)[:, None], np.arange(32)[None]
    ang = 2 * np.pi * n * mm / 64
    F = np.stack([np.cos(ang), -np.sin(ang)], -1).reshape(64, 64).astype(f32)
    Fh = F.astype(np.float16)
    arr["dft"] = np.concatenate([Fh, (F - Fh.astype(f32)).astype(np.float16)])
    cm = np.where(np.arange(32) == 0, 1.0, 2.0)[:, None]
    gi = np.zeros((4, 32, 2, 4, 64), f32)
    for q in range(4):
        gi[q, :, 0, q] = cm * np.cos(ang.T)
        gi[q, :, 1, q] = -cm * np.sin(ang.T)
    arr["gi"] = gi.reshape(128, 512)
    pct = I["L1_conv_pct"]
    arr["pctr"] = pct[:, :32][p // 4].reshape(128, 1024)
    pt = pct[:, :32].transpose(2, 1, 0).reshape(32, 1024)
    arr["pctt"] = np.concatenate([pt, pt])
    wc = I["L1_conv_weights"].reshape(32, 32, 8, 4, 32, 2)
    arr["wc"] = wc.transpose(3, 0, 4, 2, 5, 1).reshape(128, 32 * 8 * 64)
    w13 = np.zeros((2, 64, 8, 768), f32)
    w13[0, :, :, :682] = I["L1_ffn_w1"].transpose(2, 0, 1)
    w13[1, :, :, :682] = I["L1_ffn_w3"].transpose(2, 0, 1)
    w13 = w13.transpose(1, 0, 2, 3).reshape(64, 12288)
    arr["w13"] = np.concatenate([w13, w13])
    w2 = np.zeros((8, 768, 64), f32)
    w2[:, :682] = I["L1_ffn_w2"].transpose(0, 2, 1)
    arr["w2"] = w2.reshape(8, 6, 128, 64).transpose(2, 0, 1, 3).reshape(128, 3072)

    rt = np.zeros((128, 288), f32)
    rt[:, 0:128] = np.arange(128)
    rt[:, 128:144] = 128 * np.arange(16)
    rt[:, 144:208] = (np.arange(8)[None, :] < np.arange(8)[:, None]).reshape(64)
    rt[:, 240] = p - 127
    rt[:, 208:240] = 1 + 16 * p[:, None] + np.arange(32)[None] % 16
    rt[:, 241:281] = 8 ** (np.arange(40) % 8)
    arr["routing"] = rt
    arr["routing16"] = np.concatenate([p[:, None] < p[None, :], np.ones((128, 128), bool)], 1).astype(np.float16)
    arr["zeros"] = np.zeros((1088, 128), f32)

    nc = _bacc.Bacc("TRN2", target_bir_lowering=False, num_devices=1)
    inp, feeds = {}, {}
    for name, a in arr.items():
        a = np.ascontiguousarray(a)
        feeds[f"in_{name}"] = a
        inp[name] = nc.dram_tensor(f"in_{name}", a.shape, _mybir.dt.from_np(a.dtype), kind="ExternalInput").ap()
    out = nc.dram_tensor("out", (128 + 2048, 64), _mybir.dt.float32, kind="ExternalOutput").ap()
    build(nc, inp, out)
    r = _run(nc, [feeds], core_ids=[0])
    y = r.results[0]["out"][128:]
    return y.reshape(2, 2, 32, 16, 64).transpose(0, 1, 3, 2, 4).reshape(2, 32, 32, 64)
```

```python
from contextlib import ExitStack

import concourse.bass as bass
from concourse import mybir

ALU = mybir.AluOpType
ACT = mybir.ActivationFunctionType
F32 = mybir.dt.float32
F16 = mybir.dt.float16
I32 = mybir.dt.int32
AX_X = mybir.AxisListType.X

P = 128
B, HIMG, WIMG, C = 2, 32, 32, 64
NTOK = B * HIMG * WIMG
NT = NTOK // P
NG = 4
HD, WIN = 32, 8
PW = WIN * WIN
NW = NTOK // PW
REL = 2 * WIN - 1
BANK = 512
TWO_PI = 2.0 * 3.141592653589793
HALF = 384
NBLK = (2 * NTOK + 8 * (P - 1)) // P
EPS_C, EPS_A = 1e-6, 1e-5


def build(nc, inp, out):
    ctx = ExitStack()
    with ctx:
        def sb(name, shape, dt=F32):
            return ctx.enter_context(nc.sbuf_tensor(name, shape, dt))

        def sem(name):
            return ctx.enter_context(nc.semaphore(name))

        ARENA = sb("arena", [P, 199 * 256], F32)

        def at(off, cols, dt=F32):
            size = 4 if dt == F32 else 2
            a = ARENA[:, off // 4:(off + cols * size) // 4]
            return a if dt == F32 else a.bitcast(dt)

        K = 1024
        X = at(0, 1024).rearrange("p (j c) -> p j c", c=C)
        XH = at(4 * K, NTOK, F16)
        XL = at(8 * K, NTOK, F16)
        xrow = at(12 * K, 4096, F16).rearrange("p (j s n) -> p j s n", s=2, n=2 * C)
        xc = at(20 * K, 1024).rearrange("p (j c) -> p j c", c=C)
        sq = at(24 * K, 1024).rearrange("p (j c) -> p j c", c=C)

        XHw = at(28 * K, 2 * NTOK, F16)
        XLw = at(36 * K, 2 * NTOK, F16)
        KH = at(44 * K, 8192, F16).rearrange("p (h b u y v) -> p h b u y v", h=2, b=NW, u=8, y=2)
        KL = at(60 * K, 8192, F16).rearrange("p (h b u y v) -> p h b u y v", h=2, b=NW, u=8, y=2)
        qh, ql, nh, nl, mh, ml = [at(76 * K + 4 * K * n, 2048, F16) for n in range(6)]
        ETB = 2 * 8 * REL * 16
        ENh, ENl = [at(100 * K + 2 * ETB * n, ETB, F16).rearrange("p (a w r) -> p a w r", a=2, w=8) for n in range(2)]
        AB = at(115 * K, 4096).rearrange("p (h o b) -> p h o b", h=2, o=PW)
        Ch = at(131 * K, 4096, F16).rearrange("p (b c) -> p b c", b=NW)
        Cl = at(139 * K, 4096, F16).rearrange("p (b c) -> p b c", b=NW)
        V = at(147 * K, 4096).rearrange("p (b h n) -> p b h n", h=2, n=64)
        S_ = [at((163 + 4 * n) * K, 1024) for n in range(3)]
        Sq = [at((175 + 4 * n) * K, 1024) for n in range(2)]
        EMh, EMl = [at(163 * K + 2 * ETB * n, ETB, F16).rearrange("p (a w r) -> p a w r", a=2, w=8) for n in range(2)]
        OTh = [at(183 * K + 8 * K * g, 2048, F16) for g in range(2)]
        OTl = [at(187 * K + 8 * K * g, 2048, F16) for g in range(2)]
        wpf = at(115 * K, 1280)
        wff = at(125 * K, 128).rearrange("p (g c) -> p g c", g=2)
        tblf = at(126 * K, 900)
        TH, TL = at(12 * K, 900, F16), at(14 * K, 900, F16)
        O32 = [at((20 + 2 * n) * K, BANK) for n in range(2)]
        rsc = [at((24 + 2 * n) * K, BANK) for n in range(2)]
        WP = sb("WP", [P, 1280], F16)
        biasT = sb("biasT", [P, 4, PW])
        CEN = sb("cen", [P, P])
        VAR = sb("varm", [P, PW])
        wfh = sb("wfh", [P, 2, C], F16)
        wfl = sb("wfl", [P, 2, C], F16)

        WC = [at(o * K, 2048).rearrange("p (m q n) -> p m q n", m=4, q=8) for o in (28, 36, 88, 96, 44, 52, 60, 68)]
        Z3 = at(28 * K, 3072).rearrange("p (m n) -> p m n", n=96)
        GI = at(82 * K, 512).rearrange("p (r n) -> p r n", r=2)
        W1g = at(84 * K, 1024, F16)
        W2gh = at(86 * K, 512, F16)
        W2gl = at(87 * K, 512, F16)
        w1gf, w2gf = at(104 * K, 1024), at(108 * K, 512)
        SX = at(108 * K, 8192).rearrange("p (m q n) -> p m q n", q=8, n=32)
        SXF = at(108 * K, 8192)
        stage = [at((112 + 3 * n) * K, 768) for n in range(4)]
        PRI = [at((140 + 8 * n) * K, 2048).rearrange("p (m b t) -> p m b t", b=2, t=32) for n in range(2)]
        pctr = at(76 * K, 1024).rearrange("p (m t) -> p m t", t=32)
        pctf = at(168 * K, 1024)[0:64, :].rearrange("p (m l) -> p m l", l=32)
        b2f, b2H = at(112 * K, 512)[0:2, :], at(114 * K, 512, F16)[0:2, :]
        PCTW = at(156 * K, 2048).rearrange("p (m b l) -> p m b l", b=2, l=32)
        XF = at(164 * K, 2048).rearrange("p (m r i) -> p m r i", r=2, i=32)
        Y = at(156 * K, 2048).rearrange("p (r o m) -> p r o m", r=2, o=32)
        YT = at(164 * K, 1024).rearrange("p (g r n) -> p g r n", r=2, n=64)
        g32 = [at((156 + 2 * n) * K, 512) for n in range(2)]
        gh = [at((160 + n) * K, 512, F16) for n in range(2)]
        gl = [at((162 + n) * K, 512, F16) for n in range(2)]
        red = at(105 * K, 2 * C).rearrange("p (n c) -> p n c", n=2)
        weighed = [at((164 + 2 * n) * K, 512) for n in range(2)]
        W13 = at(172 * K, 12288, F16).rearrange("p (e w n) -> p e w n", e=8, w=2)
        w2f = at(44 * K, 3072)
        W2 = at(56 * K, 6144, F16).rearrange("p (e c s n) -> p e c s n", e=8, c=6, s=2)
        w2v = w2f.rearrange("p (e c n) -> p (e c) n", e=8, c=6)
        W2hi, W2lo = [W2[:, :, :, n, :].rearrange("p e c n -> p (e c) n") for n in range(2)]

        oh12 = at(26 * K, 256).rearrange("p (k n) -> p k n", k=2)
        xg = [at(28 * K + 512 * n, 256, F16) for n in range(4)]
        xb = [at(30 * K + 512 * n, 256, F16) for n in range(2)]
        s32 = [at(31 * K + 1536 * n, HALF) for n in range(2)]
        f32 = [at(34 * K + 1536 * n, HALF) for n in range(2)]
        fh = [at(37 * K + 768 * n, HALF, F16) for n in range(4)]
        fl = [at(40 * K + 768 * n, HALF, F16) for n in range(4)]
        ys = [at(43 * K + 256 * n, C) for n in range(4)]
        RT, RT16 = at(108 * K, 288), at(104 * K, 288, F16)
        iota, k128 = RT[:, 0:P], RT[:, 128:144].unsqueeze(1).broadcast_to([P, 8, 16])
        before = RT[:, 144:208].rearrange("p (e f) -> p e f", e=8)
        tri, ones = RT16[:, 0:P], RT16[:, P:2 * P]
        row_id = RT16[:, 2 * P:2 * P + 32]
        picked = at(110 * K, (NT + 1) * 8, F16)
        rank = at(111 * K, (NT + 1) * 8)
        above = at(112 * K, 128).rearrange("p (e k) -> p e k", e=8)
        nblk, first, end = [at(113 * K + 32 * n, 8) for n in range(3)]
        partial = at(113 * K + 256, 64).rearrange("p (e f) -> p e f", e=8)
        prod = at(114 * K, 256)
        slot, gate2, gate_rest = [at(115 * K + 128 * n, 32) for n in range(3)]
        slot_i, blk_i, pos_i = [at(116 * K + 128 * n, 32).bitcast(I32) for n in range(3)]
        gate2h, gate2l, blk_h, pos_h = [at(116 * K + 384 + 64 * n, 32, F16) for n in range(4)]
        OBX = at(117 * K, 32 * 3 * NBLK, F16).rearrange("p (v b c) -> p v b c", v=3, b=NBLK)
        OB = at(125 * K, 32 * NBLK, F16).rearrange("p (b c) -> p b c", b=NBLK)
        OR = at(128 * K, 32 * P, F16).rearrange("p (r c) -> p r c", r=P)
        numbers = at(88 * K, 32 * P, F16).rearrange("p (r c) -> p r c", r=P)
        NW8 = -(-NBLK // 8)
        past = at(136 * K, 8 * 8 * NW8)[0:1, :].rearrange("p (b e) -> p b e", e=8)
        exp_f = at(138 * K, 8 * NW8)[0:1, :]
        digit = RT[0:1, 241:241 + 8 * NW8]
        word_f = at(138 * K + 256, NW8)[0:1, :]
        word_i = at(138 * K + 384, NW8)[0:1, :].bitcast(I32)
        row_i = at(138 * K + 512, NBLK).bitcast(I32)
        gate = at(138 * K + 768, NBLK)
        pad_row = at(139 * K, NBLK)
        own_row = RT[:, 240:241]
        lg, eq, sc, l2, oh1, oh2, ex, cw = [at(24 * K + 512 * n, 128).rearrange("p (j e) -> p j e", e=8)
                                            for n in range(8)]

        ident = sb("ident", [P, P], F16)
        sel = sb("sel", [P, P], F16)
        mask = sb("mask", [P, 16])
        bprep = sb("bprep", [P, 8])
        bfin = sb("bfin", [P, C])
        bv2f, bv2h = at(130 * K, 256)[0:2, :], at(125 * K + 512, 256, F16)[0:2, :]
        b2r = sb("b2r", [2, 512], F16)
        small = sb("small", [P, 64])
        g0b, b1c, idxw = [small[:, 8 * n:8 * n + 8] for n in (2, 3, 4)]
        wlat, pmask, wb = small[:, 40:41], small[:, 42:46], small[:, 46:48]
        identf = sb("identf", [64, 64])
        scratch = sb("scratch", [P, 1])
        GH = sb("gateH", [P, 16], F16)
        GW = sb("gateW", [P, 16], F16)
        FW = sb("dftw", [P, 64], F16)
        m1, m2, sm = [sb(n, [P, NT]) for n in ("m1", "m2", "sm")]
        bv2 = sb("bv2", [2, 256], F16)
        ones2 = sb("ones2", [2, P], F16)
        mu = sb("mu", [P, NT])
        var = sb("var", [P, NT])
        dev = sb("dev", [P, NT])

        PS = ctx.enter_context(nc.psum_tensor("ps", [P, 8 * BANK], F32))

        def bank(n, m=1):
            return PS[:, n * BANK:(n + m) * BANK]

        ld_x, ld_wp, ld_tbl, ld_small, st_out = sem("ld_x"), sem("ld_wp"), sem("ld_tbl"), sem("ld_small"), sem("st_out")
        vec, scratch_rdy = sem("vec_step"), sem("scratch_ready")
        ln_xc, ln_sq, ln_xn, ln_hi, ln_lo, ln_tp, xs_hi, xs_lo = [sem(s) for s in (
            "ln_centred", "ln_squared", "ln_normed", "ln_hi", "ln_lo", "ln_transposed", "xs_hi", "xs_lo")]
        wp_hi, wp_rdy, tb_hi, wf_hi, wf_rdy = [sem(s) for s in (
            "wprep_hi", "wprep_ready", "table_hi", "wfin_hi", "wfin_ready")]
        zeroed, unit_rdy, unit_hi, unit_free = [sem(s) for s in ("zeroed", "unit_ready", "unit_hi", "unit_free")]
        st_rdy, s_added, mean_rdy, centred, squared, var_rdy, val_rdy, o_read, o_hi, o_lo = [sem(s) for s in (
            "scores_ready", "scores_added", "mean_ready", "scores_centred", "scores_squared", "var_ready", "values_ready",
            "o_read", "o_hi", "o_lo")]
        bfin_added, proj_rdy, x_rdy = sem("bfin_added"), sem("proj_ready"), sem("x_ready")
        bv_hi, ln_var, ln_dev, std_rdy, scale_rdy = [sem(s) for s in ("bv_hi", "ln_var", "ln_dev", "std_ready", "scale_ready")]
        en1_hi, en_rdy, em_rdy, v_free = [sem(s) for s in ("en1_hi", "en_rdy", "em_rdy", "v_free")]

        LD_SMALL = 14 * 16
        XD = {1: 2, 2: 2 + 16, 3: 2 + 16 + 2}

        ld_f0, ld_wc, ld_gi, ld_pc, ld_st, ld_w2 = (sem("ld_f0"), [sem(f"ld_wc{n}") for n in range(8)], sem("ld_gi"),
                                                    sem("ld_pct"), [sem(f"ld_stage{n}") for n in range(4)], sem("ld_w2"))
        f0_hi, f0_lo, f0_rdy, gh_hi = [sem(s) for s in ("ffn0_weights_hi", "ffn0_weights_lo", "ffn0_bias_ready", "gates_hi")]
        gw_rdy, st_hi, st_done, wb_rdy = sem("gate_weights_ready"), sem("stage_hi"), sem("stage_done"), sem("wb_ready")
        lg_rdy, lg_read, ex_in, ex_rdy = sem("logits_ready"), sem("logits_read"), sem("exp_in"), sem("exp_ready")
        h_rdy, g_rdy, g_hi, g_lo, y_used, y_read = [sem(n) for n in (
            "h_ready", "g_ready", "g_hi", "g_lo", "y_used", "y_read")]
        y_summed = sem("y_summed")
        sx_zero, pri_rdy, pw_rdy = sem("sx_zero"), sem("pri_ready"), sem("pctw_ready")
        a_rdy, xf_rdy, b_rdy, sx_act, sx_dve, c_rdy, z_act, z_dve, d_rdy, yt_in, t_rdy, yt_rdy, e_rdy = [sem(n) for n in (
            "a_ready", "xf_ready", "b_ready", "sx_act", "sx_dve", "c_ready", "z_act", "z_dve", "d_ready", "y_whole",
            "t_ready", "yt_ready", "e_ready")]
        ys_hi = sem("ys_hi")
        w2_hi, w2_rdy, s_rdy = sem("w2_hi"), sem("w2_ready"), sem("silu_ready")
        hh_rdy, gg_rdy, gg_hi, gg_lo, yy_used, ys_rdy = [sem(n) for n in (
            "hh_ready", "gg_ready", "gg_hi", "gg_lo", "yy_used", "ys_ready")]
        ld_rt, st_init, st_rows, gathered = sem("ld_routing"), sem("st_init"), sem("st_rows"), [sem(f"gathered{n}") for n in range(4)]
        added = [sem("added_even"), sem("added_odd")]
        pick_rdy, rank_rdy, exp_rdy, map_in, map_rdy, row_rdy, gate_rdy, tp_rdy, xb_rdy = [sem(n) for n in (
            "picks_ready", "ranks_ready", "experts_ready", "map_in", "map_ready", "rows_ready", "gate_ready",
            "tp_ready", "xb_ready")]

        def spectrum(k):
            return XF[0:64].rearrange("p m r i -> p (m r) i")[:, :, 8 * k:8 * k + 8].rearrange("p n i -> p i n")

        def mixing(n):
            quad, g = n // 4, n % 4
            mh, r = quad // 2, quad % 2
            src = PS[32 * quad:32 * quad + 32, 0:1024].rearrange("p (m b q l) -> p m b q l", m=16, b=2, l=4)[:, :, :, :, g]
            dst = SX[32 * g:32 * g + 32, 16 * mh:16 * mh + 16, :, 4 * g + r:4 * g + 4:2]
            return dst.rearrange("p m q b -> p m b q"), src

        def modes(mb):
            return Y[0:64].rearrange("p r o m -> p (r o) m")[:, :, 8 * mb:8 * mb + 8].rearrange("p n m -> p m n")

        def bcol(kind, hg):
            return bprep[:, 2 * TYPE[kind] + hg:2 * TYPE[kind] + hg + 1]

        def wk(KX, hp, b):
            return KX[:, hp, b, :, :, :].rearrange("p u y v -> p (u y v)")

        def windowed(dst, g, j, y):
            j0 = 4 * g
            return bass.AP(dst.tensor, dst.offset + (j0 // 8) * 2048 + (j0 % 8) * 16 + 8 * y,
                           [list(dst.ap[0]), [16, 4], [P, 16], [1, 8]])

        def columns(copy, L, g, s):
            src = bank(2 * (g % 2) + s).bitcast(F16)[:, 0:BANK]
            if L == 0:
                for y in range(2):
                    ins = copy(windowed((XHw, XLw)[s], g, 0, y), src.rearrange("p (j b v) -> p j b v", j=4, v=8))
                return ins
            dst = (XH, XL)[s][:, g * BANK:(g + 1) * BANK]
            if L != 2:
                return copy(dst, src)
            for b in range(2):
                ins = copy(dst.rearrange("p (j o b t) -> p j o b t", j=4, o=2, b=2)[:, :, :, b, :],
                           src.rearrange("p (j b o t) -> p j b o t", j=4, b=2, o=2)[:, :, b, :, :])
            return ins

        def XW(xs, k):
            return xs[:, k * BANK:(k + 1) * BANK]

        def cols_c(CX, k):
            v = CX.rearrange("p b (u y v) -> p u y v b", u=8, y=2)
            return v[:, 2 * (k % 4):2 * (k % 4) + 2, k // 4, :, :]

        def ots(OT, hg, c):
            return OT[hg].rearrange("p (j q) -> p j q", q=P)[:, (c // 2) * 8:(c // 2) * 8 + 8,
                                                            (c % 2) * 64:(c % 2) * 64 + 64]

        ORDER = [("n", k) for k in range(4)] + [("m", k) for k in range(4)]
        for k in range(16):
            ORDER += [("ac"[k // 8], k % 8), (("k", k // 4), ("v", k // 2), ("q", k // 4), ("v", k // 2))[k % 4]]
        UNITS = len(ORDER)
        EARLY = 4
        TYPE = {"n": 0, "q": 1, "k": 2, "m": 3}

        def count(kinds, hg, n):
            return hg * sum(u in kinds for u, _ in ORDER) + sum(u in kinds for u, _ in ORDER[:n + 1])

        def last(kind):
            return max(n for n, (u, _) in enumerate(ORDER) if u == kind)

        def spread(src, t, hg, c, hi):
            E = (EMh if hi else EMl) if t else (ENh if hi else ENl)
            off = (2 * t + hg) * REL * REL + 7
            view = bass.AP(src.tensor, src.offset + off, [list(src.ap[0]), [-1, 8], [REL, REL], [1, 8]])
            outer, inner = (c % 2, c // 2) if t else (c // 2, c % 2)
            dst = E[:, outer, :, :].rearrange("p w (r y v) -> p w r y v", y=2, v=8)[:, :, :, inner, :]
            return dst, view, mask[:, c:c + 1]

        def diagonal(KX, c, k):
            return KX[32 * c:32 * c + 32, c // 2, 8 * k:8 * k + 8, :, c % 2, :].rearrange("p b u v -> p (b u) v")

        rows_x = nc.dram_tensor("rows_x", (P + NTOK, 256), F16).ap()
        sum_odd = nc.dram_tensor("sum_odd", (P + NTOK, C), F32).ap()

        block = ctx.enter_context(nc.Block())

        @block.sync
        def _(sp):
            sp.dma_start(X, inp["x"].rearrange("p (j c) -> p j c", c=C)).then_inc(ld_x, 16)
            sp.dma_start(wpf, inp["wprep"]).then_inc(ld_wp, 16)
            for dst, src in ((ident[:], "ident"), (mask[:], "mask"), (bprep[:], "bprep"), (bfin[:], "bfin"),
                             (biasT[:].rearrange("p h o -> p (h o)"), "biasT"), (CEN[:], "cen"), (VAR[:], "varm"),
                             (wff.rearrange("p g c -> p (g c)"), "wfin"), (sel[:], "sel"), (bv2f, "bv"),
                             (ones2[:], "ones"), (small[:], "small"), (identf[:], "identf"), (FW[:], "dft")):
                sp.dma_start(dst, inp[src]).then_inc(ld_small, 16)
            sp.dma_start(tblf, inp["tables"]).then_inc(ld_tbl, 16)
            sp.wait_ge(unit_rdy, 2 * UNITS)
            for dst, src in ((w1gf, "w1g"), (w2gf, "w2g"), (b2f, "b2g")):
                sp.dma_start(dst, inp[src]).then_inc(ld_f0, 16)

            def load_weights(n):
                sp.dma_start(WC[n].rearrange("p m q n -> p (m q n)"),
                             inp["wc"][:, 2048 * n:2048 * (n + 1)]).then_inc(ld_wc[n], 16)

            for n in range(4):
                load_weights(n)
            sp.wait_ge(st_rdy, 8)
            sp.dma_start(pctr.rearrange("p m t -> p (m t)"), inp["pctr"]).then_inc(ld_pc, 16)
            sp.dma_start(GI.rearrange("p r n -> p (r n)"), inp["gi"]).then_inc(ld_gi, 16)
            for n in range(4, 8):
                load_weights(n)
            sp.wait_ge(x_rdy, 2)
            sp.dma_start(pctf.rearrange("p m l -> p (m l)"), inp["pctt"]).then_inc(ld_pc, 16)
            sp.wait_ge(f0_rdy, 1)
            for n in range(16):
                if n >= 4:
                    sp.wait_ge(st_done, n - 3)
                sp.dma_start(stage[n % 4], inp["w13"][:, 768 * n:768 * (n + 1)]).then_inc(ld_st[n % 4], 16)
            sp.wait_ge(c_rdy, 4)
            sp.dma_start(w2f, inp["w2"]).then_inc(ld_w2, 16)
            sp.dma_start(RT, inp["routing"]).then_inc(ld_rt, 16)
            sp.dma_start(RT16, inp["routing16"]).then_inc(ld_rt, 16)
            sp.dma_start(numbers.rearrange("p r c -> p (r c)"), inp["numbers"]).then_inc(ld_rt, 16)
            sp.dma_start(rows_x[0:P, :], inp["zeros"].bitcast(F16)[0:P, 0:256]).then_inc(st_rows, 16)
            sp.dma_start(out[0:P, :], inp["zeros"][0:P, 0:C]).then_inc(st_init, 16)
            sp.dma_start(sum_odd.rearrange("r c -> (r c)"), inp["zeros"].rearrange("r c -> (r c)")).then_inc(st_init, 16)
            sp.wait_ge(x_rdy, XD[3])
            sp.dma_start(out[P:, :].rearrange("(p j) c -> p j c", p=P), X).then_inc(st_init, 16)
            sp.wait_ge(ln_lo, 4 * NG)
            sp.dma_start(rows_x[P:, :].rearrange("(p j) n -> p j n", p=P),
                         xrow.rearrange("p j s n -> p j (s n)")).then_inc(st_rows, 16)

        @block.tensor
        def _(pe):
            def norm_transposes(L):
                if L == 0:
                    pe.wait_ge(ld_small, LD_SMALL)
                for g in range(NG):
                    pe.wait_ge(ln_lo, NG * L + g + 1)
                    if g >= 2:
                        pe.wait_ge(xs_hi, NG * L + g - 1)
                        pe.wait_ge(xs_lo, NG * L + g - 1)
                    for s in range(2):
                        dst = bank(2 * (g % 2) + s).bitcast(F16)
                        for j in range(4):
                            mm = pe.transpose(dst[:, j * P:(j + 1) * P], xrow[:, 4 * g + j, s, :], ident[:])
                    mm.then_inc(ln_tp, 1)

            def attention():
                pe.wait_ge(wp_rdy, 1)
                pe.wait_ge(xs_hi, NG)
                pe.wait_ge(xs_lo, NG)

                def unit(hg, n):
                    kind, k = ORDER[n]
                    if hg and n == 0:
                        pe.wait_ge(s_added, 4)
                    if hg and n == 4:
                        pe.wait_ge(centred, 4)
                    if hg and n == 6:
                        pe.wait_ge(o_read, 4)
                        pe.wait_ge(std_rdy, 4)
                    N = hg * UNITS + n
                    o = bank(N % 8)
                    if n >= 8:
                        if ORDER[n - 8][0] == "v":
                            pe.wait_ge(v_free, count("v", hg, n - 8))
                        else:
                            pe.wait_ge(unit_free, count("nmqkac", hg, n - 8))
                    if kind in "nmqk":
                        col = TYPE[kind] * 256 + hg * P
                        for i, xs in enumerate((XHw, XLw)):
                            mv = xs[:, k * 1024:(k + 1) * 1024].rearrange("p (b y v) -> p b y v", y=2, v=8)[:, :, 0, :]
                            mm = pe.matmul(o, WP[:, col:col + P], mv, start=(i == 0), stop=(i == 1))
                    elif kind == "v":
                        for b4 in range(4):
                            b = 4 * k + b4
                            ob = o[:, b4 * P:(b4 + 1) * P]
                            for i, xs in enumerate((XHw, XLw)):
                                pe.matmul(ob, xs[:, b * P:(b + 1) * P],
                                          WP[:, 1024 + hg * P:1024 + (hg + 1) * P], start=(i == 0), stop=False)
                            mm = pe.matmul(ob, ones2[:], bv2[:, hg * P:(hg + 1) * P], start=False, stop=True)
                    elif kind == "a":
                        if k == 0:
                            pe.wait_ge(unit_free, count("nmqkac", hg, last("n")))
                            if hg:
                                pe.wait_ge(en1_hi, 1)
                            pe.wait_ge(en_rdy, hg + 1)
                        for o16 in range(16):
                            oi, oj = divmod((k % 4) * 16 + o16, 8)
                            for i, (tab, mv) in enumerate(((ENh, nh), (ENh, nl), (ENl, nh))):
                                mm = pe.matmul(o[:, o16 * NW:(o16 + 1) * NW],
                                               tab[:, k // 4, oj, (7 - oi) * 16:(15 - oi) * 16],
                                               mv[:, 8 * oi + oj::PW], start=(i == 0), stop=(i == 2))
                    else:
                        if k == 0:
                            pe.wait_ge(em_rdy, hg + 1)
                        for i16 in range(16):
                            ii, ij = divmod((k % 4) * 16 + i16, 8)
                            for i, (tab, mv) in enumerate(((EMh, mh), (EMh, ml), (EMl, mh))):
                                mm = pe.matmul(o[:, i16 * NW:(i16 + 1) * NW],
                                               tab[:, k // 4, ij, (7 - ii) * 16:(15 - ii) * 16],
                                               mv[:, 8 * ii + ij::PW], start=(i == 0), stop=(i == 2))
                    mm.then_inc(unit_rdy, 1)

                for hg in range(2):
                    for n in range(EARLY * hg, UNITS):
                        unit(hg, n)

                    def scores(c):
                        cg = hg * 4 + c
                        if c == 0:
                            pe.wait_ge(unit_free, count("nmqkac", hg, UNITS - 1))
                            pe.wait_ge(v_free, count("v", hg, UNITS - 1))
                        if cg >= 2:
                            pe.wait_ge(s_added, cg - 1)
                        for b8 in range(8):
                            b = c * 8 + b8
                            for hp in range(2):
                                o = bank(2 * (cg % 2) + hp)[:, b8 * PW:(b8 + 1) * PW]
                                qs = slice(b * PW, (b + 1) * PW)
                                pe.matmul(o, wk(KH, hp, b), qh[:, qs], start=True, stop=False)
                                pe.matmul(o, wk(KH, hp, b), ql[:, qs], start=False, stop=False)
                                pe.matmul(o, wk(KL, hp, b), qh[:, qs], start=False, stop=False)
                                idn = sel[:, hp * PW:(hp + 1) * PW]
                                pe.matmul(o, Ch[:, b, :], idn, start=False, stop=False)
                                mm = pe.matmul(o, Cl[:, b, :], idn, start=False, stop=True)
                        mm.then_inc(st_rdy, 1)

                    def means(c):
                        cg = hg * 4 + c
                        pe.wait_ge(s_added, cg + 1)
                        if cg >= 1:
                            pe.wait_ge(centred, cg)
                        for hp in range(2):
                            mm = pe.matmul(bank(4 + hp), CEN[:], S_[cg % 3][:, hp * BANK:(hp + 1) * BANK],
                                           start=True, stop=True)
                        mm.then_inc(mean_rdy, 1)

                    def variances(c):
                        cg = hg * 4 + c
                        pe.wait_ge(squared, cg + 1)
                        if cg >= 1:
                            pe.wait_ge(std_rdy, cg)
                        for hp in range(2):
                            mm = pe.matmul(bank(7)[64 * hp:64 * hp + 64, :], VAR[:],
                                           Sq[cg % 2][:, hp * BANK:(hp + 1) * BANK], start=True, stop=True)
                        mm.then_inc(var_rdy, 1)

                    def values(c):
                        cg = hg * 4 + c
                        pe.wait_ge(centred, cg + 1)
                        if cg >= 1:
                            pe.wait_ge(o_read, cg)
                        for b8 in range(8):
                            for hp in range(2):
                                mm = pe.matmul(bank(6)[64 * hp:64 * hp + 64, b8 * PW:(b8 + 1) * PW],
                                          V[:, c * 8 + b8, hp, :],
                                          S_[cg % 3][:, hp * BANK + b8 * PW:hp * BANK + (b8 + 1) * PW],
                                          start=True, stop=True)
                        mm.then_inc(val_rdy, 1)

                    for c in range(4 + 2):
                        if c < 4:
                            scores(c)
                        if (hg, c) == (0, 5):
                            for n in range(EARLY):
                                unit(1, n)
                        if c >= 2:
                            variances(c - 2)
                        if 1 <= c < 5:
                            means(c - 1)
                        if c >= 2:
                            values(c - 2)
                pe.wait_ge(o_lo, 8)
                pe.wait_ge(wf_rdy, 1)
                for j in range(NT):
                    o = bank(j // 8)[:, (j % 8) * C:(j % 8 + 1) * C]
                    n = 0
                    for hg in range(2):
                        ts = slice(j * P, (j + 1) * P)
                        for a, w in ((OTh, wfh), (OTl, wfh), (OTh, wfl)):
                            mm = pe.matmul(o, a[hg][:, ts], w[:, hg, :], start=(n == 0), stop=(n == 5))
                            n += 1
                    if j % 8 == 7:
                        mm.then_inc(proj_rdy, 1)

            def ffn0():
                pe.wait_ge(xs_hi, 2 * NG)
                pe.wait_ge(xs_lo, 2 * NG)
                pe.wait_ge(gw_rdy, 1)
                logits(0, bank(7))
                pe.wait_ge(f0_rdy, 1)
                pe.wait_ge(f0_lo, 2)

                def hidden(it):
                    blk, e = divmod(it, 8)
                    if it >= 2:
                        pe.wait_ge(g_rdy, it - 1)
                    for i, xs in enumerate((XH, XL)):
                        mm = pe.matmul(bank(it % 2), W1g[:, e * P:(e + 1) * P], XW(xs, blk), start=(i == 0), stop=(i == 1))
                    mm.then_inc(h_rdy, 1)

                def outputs(it):
                    blk, e = divmod(it, 8)
                    pe.wait_ge(g_lo, it + 1)
                    for jt in range(4):
                        t = 4 * blk + jt
                        o = bank(2 + t % 6)
                        if e == 0:
                            if t == 5:
                                pe.wait_ge(lg_read, 1)
                            if t >= 6:
                                pe.wait_ge(y_read, t - 5)
                            pe.matmul(o, ones2[:], b2r[:], start=True, stop=False)
                        for i, (a, w) in enumerate(((gh, W2gh), (gl, W2gh), (gh, W2gl))):
                            mm = pe.matmul(o[:, e * C:(e + 1) * C], a[it % 2][:, jt * P:(jt + 1) * P],
                                           w[:, e * C:(e + 1) * C], start=False, stop=(e == 7 and i == 2))
                    mm.then_inc(y_used, 1)

                for it in range(32 + 2):
                    if it < 32:
                        hidden(it)
                    if it >= 2:
                        outputs(it - 2)

            def logits(n, o):
                for j in range(NT):
                    for i, xs in enumerate((XH, XL)):
                        mm = pe.matmul(o[:, 8 * j:8 * j + 8], xs[:, j * P:(j + 1) * P], GW[:, 8 * n:8 * n + 8],
                                       start=(i == 0), stop=(i == 1))
                mm.then_inc(lg_rdy, 1)

            def convolution():
                pe.wait_ge(xs_hi, 3 * NG)
                pe.wait_ge(xs_lo, 3 * NG)
                for k in range(4):
                    for i8 in range(8):
                        i = 8 * k + i8
                        col = (i % 16) * P + (i // 16) * 64
                        for n, xs in enumerate((XH, XL)):
                            mm = pe.matmul(bank(4 + k)[0:64, i8 * 64:(i8 + 1) * 64], xs[:, col:col + 64], FW[:],
                                           start=(n == 0), stop=(n == 1))
                    mm.then_inc(a_rdy, 1)
                pe.wait_ge(xf_rdy, 4)
                pe.wait_ge(pw_rdy, 1)
                for m16 in range(16):
                    for mh in range(2):
                        m = 16 * mh + m16
                        mm = pe.matmul(PS[64 * mh:64 * mh + 64, m16 * 64:(m16 + 1) * 64],
                                       XF[:, m, :, :].rearrange("p r i -> p (r i)")[0:64],
                                       PCTW[:, m, :, :].rearrange("p b l -> p (b l)")[0:64], start=True, stop=True)
                mm.then_inc(b_rdy, 1)
                pe.wait_ge(sx_act, 1)
                pe.wait_ge(sx_dve, 1)
                for mb in range(4):
                    for m8 in range(8):
                        m = 8 * mb + m8
                        if m % 4 == 0:
                            pe.wait_ge(ld_wc[m // 4], 16)
                        for q in range(2):
                            for g in range(4):
                                lq = 2 * g + q
                                base = (m * 8 + lq) * 32 - 16 * q
                                mm = pe.matmul(bank(2 + mb)[32 * g:32 * g + 32, m8 * 64:(m8 + 1) * 64],
                                               SXF[:, base:base + 32], WC[m // 4][:, m % 4, lq, :],
                                               start=(q == 0), stop=(q == 1))
                    mm.then_inc(c_rdy, 1)
                pe.wait_ge(pri_rdy, 1)
                for mb in range(4):
                    pe.wait_ge(z_act, mb + 1)
                    pe.wait_ge(z_dve, mb + 1)
                    for m8 in range(8):
                        m = 8 * mb + m8
                        o = bank((6, 7, 0, 1)[mb])[0:64, m8 * 64:(m8 + 1) * 64]
                        for n, c0 in ((0, 32), (1, 0)):
                            mm = pe.matmul(o, PRI[n][:, m, :, :].rearrange("p b t -> p (b t)"), Z3[:, m, c0:c0 + 64],
                                           start=(n == 0), stop=(n == 1))
                    mm.then_inc(d_rdy, 1)
                pe.wait_ge(yt_in, 4)
                for og in range(8):
                    for r in range(2):
                        mm = pe.transpose(PS[:, 2 * BANK + (2 * og + r) * 64:2 * BANK + (2 * og + r + 1) * 64],
                                          Y[0:64, r, 4 * og:4 * og + 4, :].rearrange("p o m -> p (o m)"), identf[:])
                    if og % 4 == 3:
                        mm.then_inc(t_rdy, 1)
                pe.wait_ge(ld_gi, 16)
                for n in range(2):
                    pe.wait_ge(yt_rdy, 2)
                    for og4 in (2 * n, 2 * n + 1):
                        for r in range(2):
                            for b in range(2):
                                for oh in range(2):
                                    q = 64 * b + 32 * oh
                                    mm = pe.matmul(bank(4 + n)[q:q + 32, (og4 % 2) * 256:(og4 % 2) * 256 + 256],
                                                   YT[:, 4 * oh + og4, r, 32 * b:32 * b + 32], GI[:, r, :],
                                                   start=(r == 0), stop=(r == 1))
                    mm.then_inc(e_rdy, 1)

            def ffn1():
                pe.wait_ge(xs_hi, 4 * NG)
                pe.wait_ge(xs_lo, 4 * NG)
                logits(1, bank(7))

                pe.wait_ge(pick_rdy, 1)
                pe.wait_ge(ld_rt, 48)
                pe.matmul(bank(6)[:, 0:(NT + 1) * 8], tri, picked, start=True, stop=False)
                for j in range(NT):
                    n = NT - j
                    mm = pe.matmul(bank(6)[:, 8 * (j + 1):8 * (NT + 1)].rearrange("p (j e) -> p j e", e=8), ones,
                                   picked[:, 8 * j:8 * j + 8].unsqueeze(1).broadcast_to([P, n, 8]), start=False,
                                   stop=(j == NT - 1))
                mm.then_inc(rank_rdy, 1)
                pe.wait_ge(map_in, 1)
                for c in range(32):
                    mm = pe.matmul(bank(7)[:, 0:3 * NBLK], OR[:, :, c], OBX[:, :, :, c].rearrange("p v b -> p (v b)"),
                                   start=(c == 0), stop=(c == 31))
                mm.then_inc(map_rdy, 1)
                pe.wait_ge(exp_rdy, 1)
                pe.wait_ge(w2_rdy, 1)
                pe.wait_ge(st_done, 16)

                expert, word = {}, [0]

                def transposes(b):
                    pe.wait_ge(gathered[b % 4], 16 * (b // 4 + 1))
                    if b >= 2:
                        pe.wait_ge(xb_rdy, b - 1)
                    dst = bank(4 + b % 2).bitcast(F16)
                    for s in range(2):
                        mm = pe.transpose(dst[:, s * P:(s + 1) * P], xg[b % 4][:, s * P:(s + 1) * P], ident[:])
                    mm.then_inc(tp_rdy, 1)
                    if b % 8 == 0:
                        word[0] = pe.value_load(word_i[:, b // 8:b // 8 + 1], min_val=0, max_val=8 ** 8 - 1)
                    expert[b] = word[0] // 8 ** (b % 8) % 8

                def hidden(b, half):
                    if half == 0:
                        pe.wait_ge(xb_rdy, b + 1)
                    if b:
                        pe.wait_ge(gg_rdy, 2 * b + half - 1)
                    for w in range(2):
                        for c in range(3):
                            wt = W13[:, bass.ds(expert[b], 1), w, (3 * half + c) * P:(3 * half + c + 1) * P]
                            for i in range(2):
                                mm = pe.matmul(bank(2 * w + half)[:, c * P:(c + 1) * P], wt.rearrange("p a n -> p (a n)"),
                                               xb[b % 2][:, i * P:(i + 1) * P], start=(i == 0), stop=(i == 1))
                    mm.then_inc(hh_rdy, 1)

                def outputs(b, half):
                    pe.wait_ge(gg_lo, 2 * b + half + 1)
                    if half == 0 and b >= 2:
                        pe.wait_ge(ys_rdy, b - 1)
                    n, o = 2 * (b % 2) + half, bank(6 + b % 2)
                    for c in range(3):
                        wt = W2[:, bass.ds(expert[b], 1), 3 * half + c, :, :].rearrange("p a s n -> p (a s n)")
                        cs = slice(c * P, (c + 1) * P)
                        pe.matmul(o[:, 0:2 * C], fh[n][:, cs], wt, start=(half == 0 and c == 0), stop=False)
                        mm = pe.matmul(o[:, 0:C], fl[n][:, cs], wt[:, 0:C], start=False, stop=(half == 1 and c == 2))
                    mm.then_inc(yy_used, 1)

                transposes(0)
                for b in range(NBLK + 2):
                    if b + 1 < NBLK:
                        transposes(b + 1)
                    if b < NBLK:
                        hidden(b, 0)
                    if b >= 2:
                        outputs(b - 2, 1)
                    if b < NBLK:
                        hidden(b, 1)
                    if 1 <= b <= NBLK:
                        outputs(b - 1, 0)

            norm_transposes(0)
            attention()
            norm_transposes(1)
            ffn0()
            norm_transposes(2)
            convolution()
            norm_transposes(3)
            ffn1()

        @block.scalar
        def _(act):
            def norm(L, eps):
                act.activation(scratch[:], scratch[:], ACT.Sqrt)
                for g in range(NG):
                    act.wait_ge(ln_xc, NG * L + g + 1)
                    act.activation(sq[:, 4 * g:4 * g + 4, :], xc[:, 4 * g:4 * g + 4, :], ACT.Square,
                                   scale=1.0 / 8).then_inc(ln_sq, 1)
                for g in range(NG):
                    act.wait_ge(ln_var, NG * L + g + 1)
                    act.activation(dev[:, 4 * g:4 * g + 4], var[:, 4 * g:4 * g + 4], ACT.Sqrt,
                                   bias=mask[:, eps:eps + 1]).then_inc(ln_dev, 1)
                for g in range(NG):
                    act.wait_ge(ln_xn, NG * L + g + 1)
                    src = xc[:, 4 * g:4 * g + 4, :].unsqueeze(2).broadcast_to([P, 4, 2, C])
                    act.copy(xrow[:, 4 * g:4 * g + 4, 0, :].rearrange("p j (n c) -> p j n c", n=2), src).then_inc(ln_hi, 1)
                for g in range(NG):
                    act.wait_ge(ln_tp, NG * L + g + 1)
                    columns(act.copy, L, g, 0).then_inc(xs_hi, 1)

            act.wait_ge(scratch_rdy, 1)
            act.wait_ge(ld_wp, 16)
            act.copy(WP[:], wpf).then_inc(wp_hi, 1)
            act.wait_ge(ld_small, LD_SMALL)
            norm(0, 8)
            act.wait_ge(ld_tbl, 16)
            act.wait_ge(ln_tp, NG)
            act.copy(TH, tblf).then_inc(tb_hi, 1)
            act.copy(bv2h, bv2f).then_inc(bv_hi, 1)
            act.copy(wfh[:], wff).then_inc(wf_hi, 1)

            def unit(hg, n):
                kind, k = ORDER[n]
                if kind == "a":
                    return
                N = hg * UNITS + n
                o = bank(N % 8)
                act.wait_ge(unit_rdy, N + 1)
                if kind in "nmq":
                    dst = {"n": nh, "m": mh, "q": qh}[kind]
                    ins = act.activation(XW(dst, k), o, ACT.Identity, bias=bcol(kind, hg))
                elif kind == "k":
                    if hg == 0 and k == 0:
                        act.wait_ge(zeroed, 2)
                    for c in range(4):
                        r = slice(32 * c, 32 * c + 32)
                        ins = act.activation(diagonal(KH, c, k), o[r, :].rearrange("p (b v) -> p b v", v=8),
                                             ACT.Identity, bias=bcol(kind, hg)[r, :])
                elif kind == "v":
                    src = o.rearrange("p (b n) -> p b n", n=HD)
                    for y in range(2):
                        ins = act.mul(V[:, 4 * k:4 * k + 4, :, 32 * y:32 * y + 32].rearrange("p b h d -> p (b h) d"),
                                      src[:, y::2, :], mask[:, 5 + y:6 + y])
                else:
                    ins = act.copy(cols_c(Ch, k), o.rearrange("p (u v b) -> p u v b", u=2, b=NW))
                ins.then_inc(v_free if kind == "v" else unit_hi, 1)

            for hg in range(2):
                for n in range(EARLY * hg, UNITS):
                    unit(hg, n)
                for c in range(6):
                    if c >= 2:
                        cg = hg * 4 + c - 2
                        act.wait_ge(var_rdy, cg + 1)
                        if cg >= 2:
                            act.wait_ge(o_read, cg - 1)
                        act.activation(rsc[cg % 2], bank(7), ACT.Sqrt, bias=mask[:, 7:8]).then_inc(std_rdy, 1)
                    if (hg, c) == (0, 5):
                        for n in range(EARLY):
                            unit(1, n)
                    if c < 4 and hg == 0:
                        ins = act.mul(*spread(TH, 0, 1, c, True))
                        if c == 3:
                            ins.then_inc(en1_hi, 1)
                    if 1 <= c < 5:
                        cg = hg * 4 + c - 1
                        act.wait_ge(centred, cg + 1)
                        if cg >= 2:
                            act.wait_ge(var_rdy, cg - 1)
                        act.activation(Sq[cg % 2], S_[cg % 3], ACT.Square).then_inc(squared, 1)
                    if c >= 2:
                        cg = hg * 4 + c - 2
                        act.wait_ge(o_read, cg + 1)
                        act.copy(ots(OTh, hg, c - 2), O32[cg % 2].rearrange("p (j t) -> p j t", t=64)).then_inc(o_hi, 1)

            def expert_stage(n):
                act.wait_ge(ld_st[n % 4], 16 * (n // 4 + 1))
                act.copy(W13[:, n % 8, n // 8, :], stage[n % 4]).then_inc(st_hi, 1)

            def ffn0():
                act.copy(GH[:], small[:, 0:16]).then_inc(gh_hi, 1)
                act.wait_ge(ld_f0, 48)
                act.copy(W1g, w1gf)
                act.copy(W2gh, w2gf)
                act.copy(b2H, b2f).then_inc(f0_hi, 1)

            def gates():
                act.wait_ge(ex_in, gates.n + 1)
                gates.n += 1
                act.activation(ex, ex, ACT.Exp).then_inc(ex_rdy, 1)
            gates.n = 0

            def ffn0_main():
                for it in range(32):
                    e = it % 8
                    act.wait_ge(h_rdy, it + 1)
                    if it >= 2:
                        act.wait_ge(g_lo, it - 1)
                    act.activation(g32[it % 2], bank(it % 2), ACT.Gelu, bias=b1c[:, e:e + 1]).then_inc(g_rdy, 1)
                    if it % 2 == 0:
                        expert_stage(it // 2)
                    act.wait_ge(g_rdy, it + 1)
                    if it >= 2:
                        act.wait_ge(y_used, it - 1)
                    act.copy(gh[it % 2], g32[it % 2]).then_inc(g_hi, 1)

            def convolution():
                act.wait_ge(y_read, NT)
                norm(2, 8)
                act.wait_ge(wb_rdy, 1)
                act.wait_ge(ld_pc, 32)
                act.wait_ge(y_read, NT)
                for b in range(2):
                    ins = act.mul(PCTW[0:64, :, b, :], pctf, wb[0:64, b:b + 1])
                ins.then_inc(pw_rdy, 1)
                act.wait_ge(pw_rdy, 1)
                for k in (0, 2):
                    act.wait_ge(a_rdy, k + 1)
                    act.copy(spectrum(k), bank(4 + k)[0:64, :].rearrange("p (i n) -> p i n", i=8)).then_inc(xf_rdy, 1)
                act.wait_ge(b_rdy, 1)
                act.wait_ge(sx_zero, 1)
                for n in range(8):
                    ins = act.copy(*mixing(n))
                ins.then_inc(sx_act, 1)
                for mb in range(4):
                    act.wait_ge(c_rdy, mb + 1)
                    act.copy(Z3[:, 8 * mb:8 * mb + 8, 32:96],
                             bank(2 + mb).rearrange("p (m n) -> p m n", n=64)).then_inc(z_act, 1)
                act.wait_ge(xf_rdy, 4)
                for mb in (0, 2):
                    act.wait_ge(d_rdy, mb + 1)
                    act.copy(modes(mb), bank((6, 7, 0, 1)[mb])[0:64, :].rearrange("p (m n) -> p m n", n=64)).then_inc(yt_in, 1)
                act.wait_ge(t_rdy, 1)
                act.copy(YT[:, 0:4, :, :].rearrange("p g r n -> p (g r n)"), bank(2)).then_inc(yt_rdy, 1)

            def ffn1():
                act.wait_ge(ld_w2, 16)
                act.copy(W2hi, w2v).then_inc(w2_hi, 1)
                norm(3, 7)
                gates()

                def high(b, odd, half):
                    act.wait_ge(gg_rdy, 2 * b + half + 1)
                    if not (isinstance(b, int) and b < 2):
                        act.wait_ge(yy_used, 2 * b + half - 3)
                    act.copy(fh[2 * odd + half], f32[half]).then_inc(gg_hi, 1)

                def outputs(b, u4, turn):
                    act.wait_ge(yy_used, 2 * b + 2)
                    if not (isinstance(b, int) and b < 4):
                        act.wait_ge(added[u4 % 2], 16 * (2 * turn + u4 // 2 - 1))
                    act.mul(ys[u4], bank(6 + u4 % 2)[:, 0:C], gate[:, bass.ds(b, 1)]).then_inc(ys_hi, 1)

                def step(b, u4, turn):
                    for half in range(2):
                        act.wait_ge(hh_rdy, 2 * b + half + 1)
                        if not (isinstance(b, int) and b == 0):
                            act.wait_ge(gg_rdy, 2 * b + half - 1)
                        act.activation(s32[half], bank(half)[:, 0:HALF], ACT.Silu).then_inc(s_rdy, 1)
                        if half:
                            high(b, u4 % 2, 0)
                        elif not (isinstance(b, int) and b == 0):
                            high(b - 1, (u4 + 1) % 2, 1)
                    if not (isinstance(b, int) and b < 2):
                        outputs(b - 2, (u4 + 2) % 4, turn if u4 >= 2 else turn - 1)

                act.activation(scratch[:], scratch[:], ACT.Silu)
                act.wait_ge(gate_rdy, 1)
                for b in range(8):
                    step(b, b % 4, b // 4)
                with act.Fori(2, NBLK // 4) as i:
                    for u in range(4):
                        step(4 * i + u, u, i)
                for b in range(NBLK // 4 * 4, NBLK):
                    step(b, b % 4, b // 4)
                high(NBLK - 1, (NBLK - 1) % 2, 1)
                for b in (NBLK - 2, NBLK - 1):
                    outputs(b, b % 4, b // 4)

            ffn0()
            norm(1, 7)
            gates()
            ffn0_main()
            convolution()
            ffn1()

        @block.gpsimd
        def _(pool):
            pool.memset(scratch[:], 0.0).then_inc(scratch_rdy, 1)
            pool.memset(at(44 * K, 4096), 0.0).then_inc(zeroed, 1)
            pool.memset(at(60 * K, 4096), 0.0).then_inc(zeroed, 1)
            pool.wait_ge(zeroed, 2)
            pool.wait_ge(wp_hi, 1)
            pool.tensor_tensor(WP[64:P, :], wpf[64:P, :], WP[64:P, :], ALU.subtract).then_inc(wp_rdy, 1)
            pool.wait_ge(wp_rdy, 1)
            pool.wait_ge(ln_xc, NG)
            pool.wait_ge(ld_small, LD_SMALL)
            pool.tensor_tensor(X, X, bfin[:].unsqueeze(1).broadcast_to([P, NT, C]), ALU.add).then_inc(bfin_added, 1)
            for hg in range(2):
                for c in range(6):
                    if c >= 2:
                        cg = hg * 4 + c - 2
                        pool.wait_ge(o_hi, cg + 1)
                        pool.tensor_tensor(ots(OTl, hg, c - 2), O32[cg % 2].rearrange("p (j t) -> p j t", t=64),
                                           ots(OTh, hg, c - 2), ALU.subtract).then_inc(o_lo, 1)

            pool.wait_ge(f0_hi, 1)
            pool.tensor_tensor(W2gl, w2gf, W2gh, ALU.subtract).then_inc(f0_lo, 1)
            pool.wait_ge(f0_lo, 1)
            pool.tensor_tensor(W1g[64:P], w1gf[64:P], W1g[64:P], ALU.subtract).then_inc(f0_lo, 1)
            for n in range(16):
                pool.wait_ge(st_hi, n + 1)
                half = W13[64:P, n % 8, n // 8, :]
                pool.tensor_tensor(half, stage[n % 4][64:P], half, ALU.subtract).then_inc(st_done, 1)
            pool.wait_ge(st_done, 16)
            pool.memset(SXF, 0.0).then_inc(sx_zero, 1)
            pool.wait_ge(ld_pc, 32)
            for n in range(2):
                for b in range(2):
                    ins = pool.tensor_scalar(PRI[n][:, :, b, :], pctr, pmask[:, 2 * n + b:2 * n + b + 1], None, ALU.mult)
            ins.then_inc(pri_rdy, 1)

            pool.wait_ge(w2_hi, 1)
            pool.tensor_tensor(W2lo, w2v, W2hi, ALU.subtract).then_inc(w2_rdy, 1)

            pool.wait_ge(row_rdy, 1)
            pool.wait_ge(st_rows, 32)
            pool.wait_ge(st_init, 48)

            def gather(b):
                if b >= 4:
                    pool.wait_ge(tp_rdy, b - 3)
                pool.indirect_dma_start(xg[b % 4], None, rows_x, bass.IndirectOffsetOnAxis(ap=row_i[:, b:b + 1], axis=0)
                                        ).then_inc(gathered[b % 4], 16)

            for b in range(6):
                gather(b)
            for b in range(NBLK):
                if b + 6 < NBLK:
                    gather(b + 6)
                pool.wait_ge(ys_rdy, b + 1)
                if b >= 2:
                    pool.wait_ge(added[b % 2], 16 * (b // 2))
                pool.indirect_dma_start((out, sum_odd)[b % 2], bass.IndirectOffsetOnAxis(ap=row_i[:, b:b + 1], axis=0),
                                        ys[b % 4], None, compute_op=ALU.add).then_inc(added[b % 2], 16)
            for n in range(2):
                pool.wait_ge(added[n], 16 * ((NBLK + 1 - n) // 2))
            pool.dma_start(out[P:, :], sum_odd[P:, :], accum_op=ALU.add, max_dma_last_dim=4096).then_inc(st_out, 16)
            pool.wait_ge(st_out, 16)

        @block.vector
        def _(dve):
            steps = [0]

            def link(ins):
                steps[0] += 1
                ins.then_inc(vec, 1)
                dve.wait_ge(vec, steps[0])

            def rows(a, g):
                return a[:, 4 * g:4 * g + 4, :]

            def wide(a, g):
                return a[:, 4 * g:4 * g + 4].unsqueeze(2).broadcast_to([P, 4, C])

            def centre(L, groups):
                for g in groups:
                    link(dve.tensor_reduce(mu[:, 4 * g:4 * g + 4], rows(X, g), AX_X, ALU.add))
                    link(dve.tensor_scalar(mu[:, 4 * g:4 * g + 4], mu[:, 4 * g:4 * g + 4], 1.0 / C, None, ALU.mult))
                    dve.tensor_tensor(rows(xc, g), rows(X, g), wide(mu, g), ALU.subtract).then_inc(ln_xc, 1)

            def norm(L, centred_before=0):
                centre(L, range(centred_before, NG))
                for g in range(NG):
                    dve.wait_ge(ln_sq, NG * L + g + 1)
                    dve.tensor_reduce(var[:, 4 * g:4 * g + 4], rows(sq, g), AX_X, ALU.add).then_inc(ln_var, 1)
                for g in range(NG):
                    dve.wait_ge(ln_dev, NG * L + g + 1)
                    link(dve.reciprocal(dev[:, 4 * g:4 * g + 4], dev[:, 4 * g:4 * g + 4]))
                    dve.wait_ge(ln_xc, NG * L + g + 1)
                    dve.tensor_tensor(rows(xc, g), rows(xc, g), wide(dev, g), ALU.mult).then_inc(ln_xn, 1)
                for g in range(NG):
                    dve.wait_ge(ln_hi, NG * L + g + 1)
                    hi, lo = [xrow[:, 4 * g:4 * g + 4, s, :].rearrange("p j (n c) -> p j n c", n=2) for s in range(2)]
                    dve.tensor_tensor(lo, rows(xc, g).unsqueeze(2).broadcast_to([P, 4, 2, C]), hi,
                                      ALU.subtract).then_inc(ln_lo, 1)

            def columns_lo(L):
                for g in range(NG):
                    dve.wait_ge(ln_tp, NG * L + g + 1)
                    columns(dve.tensor_copy, L, g, 1).then_inc(xs_lo, 1)

            dve.wait_ge(ld_x, 16)
            norm(0)
            dve.wait_ge(ld_small, LD_SMALL)
            columns_lo(0)
            dve.wait_ge(tb_hi, 1)
            link(dve.tensor_tensor(TL, tblf, TH, ALU.subtract))
            for c in range(4):
                dve.tensor_scalar(*spread(TH, 0, 0, c, True), None, ALU.mult)
                ins = dve.tensor_scalar(*spread(TL, 0, 0, c, False), None, ALU.mult)
            ins.then_inc(en_rdy, 1)
            dve.wait_ge(bv_hi, 1)
            dve.scalar_tensor_tensor(bv2[:], bv2h, mask[0:2, 9:10], bv2f, ALU.mult, ALU.add)
            dve.wait_ge(wf_hi, 1)
            dve.tensor_tensor(wfl[:], wff, wfh[:], ALU.subtract).then_inc(wf_rdy, 1)

            def attention():
                for hg in range(2):
                    for n, (kind, k) in enumerate(ORDER):
                        if (kind, k) == ("a", 4):
                            if hg:
                                dve.wait_ge(val_rdy, 4)
                            for c in range(4):
                                dve.tensor_scalar(*spread(TH, 1, hg, c, True), None, ALU.mult)
                                ins = dve.tensor_scalar(*spread(TL, 1, hg, c, False), None, ALU.mult)
                            ins.then_inc(em_rdy, 1)
                        if kind == "v":
                            continue
                        N = hg * UNITS + n
                        o = bank(N % 8)
                        if kind == "a":
                            dve.wait_ge(unit_rdy, N + 1)
                            o0 = (k % 4) * 16
                            bb = biasT[:, 2 * hg + k // 4, o0:o0 + 16].unsqueeze(2).broadcast_to([P, 16, NW])
                            ins = dve.tensor_tensor(AB[:, k // 4, o0:o0 + 16, :], o.rearrange("p (o b) -> p o b", b=NW),
                                                    bb, ALU.add)
                        else:
                            dve.wait_ge(unit_hi, count("nmqkc", hg, n))
                        if kind in "nmq":
                            hi, lo = {"n": (nh, nl), "m": (mh, ml), "q": (qh, ql)}[kind]
                            ins = dve.scalar_tensor_tensor(XW(lo, k), o, bcol(kind, hg), XW(hi, k), ALU.add, ALU.subtract)
                        elif kind == "k":
                            for c in range(4):
                                r = slice(32 * c, 32 * c + 32)
                                ins = dve.scalar_tensor_tensor(
                                    diagonal(KL, c, k), o[r, :].rearrange("p (b v) -> p b v", v=8),
                                    bcol(kind, hg)[r, :], diagonal(KH, c, k), ALU.add, ALU.subtract)
                        elif kind == "c":
                            ins = dve.tensor_tensor(cols_c(Cl, k), o.rearrange("p (u v b) -> p u v b", u=2, b=NW),
                                                    cols_c(Ch, k), ALU.subtract)
                        ins.then_inc(unit_free, 1)
                    dve.wait_ge(unit_free, count("nmqkac", hg, UNITS - 1))

                    for c in range(6):
                        if c < 4:
                            cg = hg * 4 + c
                            dve.wait_ge(st_rdy, cg + 1)
                            if cg >= 3:
                                dve.wait_ge(val_rdy, cg - 2)
                            a = AB[:, :, :, c * 8:c * 8 + 8].rearrange("p h o b -> p h b o")
                            for hp in range(2):
                                ins = dve.tensor_tensor(
                                    S_[cg % 3][:, hp * BANK:(hp + 1) * BANK].rearrange("p (b o) -> p b o", o=PW),
                                    bank(2 * (cg % 2) + hp).rearrange("p (b o) -> p b o", o=PW),
                                    a[:, hp, :, :], ALU.add)
                            ins.then_inc(s_added, 1)
                        if c < 4 and hg == 0:
                            ins = dve.tensor_scalar(*spread(TL, 0, 1, c, False), None, ALU.mult)
                            if c == 3:
                                ins.then_inc(en_rdy, 1)
                        if 1 <= c < 5:
                            cg = hg * 4 + c - 1
                            dve.wait_ge(mean_rdy, cg + 1)
                            dve.tensor_tensor(S_[cg % 3], S_[cg % 3], bank(4, 2), ALU.subtract).then_inc(centred, 1)
                        if c >= 2:
                            cg = hg * 4 + c - 2
                            dve.wait_ge(std_rdy, cg + 1)
                            dve.reciprocal(rsc[cg % 2], rsc[cg % 2]).then_inc(scale_rdy, 1)
                            dve.wait_ge(scale_rdy, cg + 1)
                            dve.wait_ge(val_rdy, cg + 1)
                            if cg >= 2:
                                dve.wait_ge(o_lo, cg - 1)
                            v = "p (w i j) -> p w i j"
                            ins = dve.tensor_tensor(O32[cg % 2].rearrange("p (i w j) -> p w i j", i=8, w=8),
                                                    bank(6).rearrange(v, w=8, i=8), rsc[cg % 2].rearrange(v, w=8, i=8), ALU.mult)
                            ins.then_inc(o_read, 1)
                dve.wait_ge(bfin_added, 1)
                for n in range(2):
                    dve.wait_ge(proj_rdy, n + 1)
                    dve.tensor_tensor(X[:, 8 * n:8 * n + 8, :], X[:, 8 * n:8 * n + 8, :],
                                      bank(n).rearrange("p (j c) -> p j c", c=C), ALU.add).then_inc(x_rdy, 1)
                dve.wait_ge(x_rdy, 2)

            def wide8(a):
                return a.unsqueeze(2).broadcast_to([P, NT, 8])

            def top_two(n, o):
                dve.wait_ge(lg_rdy, n + 1)
                gb = (g0b.unsqueeze(1).broadcast_to([P, NT, 8]), None)[n]
                src = o[:, 0:128].rearrange("p (j e) -> p j e", e=8)
                if n == 0:
                    ins = dve.tensor_tensor(lg, src, gb, ALU.add)
                else:
                    ins = dve.tensor_copy(lg, src)
                ins.then_inc(lg_read, 1)
                dve.wait_ge(lg_read, n + 1)
                link(dve.tensor_reduce(m1[:], lg, AX_X, ALU.max))
                dve.tensor_tensor(ex, lg, wide8(m1[:]), ALU.subtract).then_inc(ex_in, 1)
                yield
                iw = idxw.unsqueeze(1).broadcast_to([P, NT, 8])

                def first_largest(a, m, oh):
                    link(dve.tensor_tensor(eq, a, wide8(m[:]), ALU.is_equal))
                    link(dve.tensor_tensor(sc, eq, iw, ALU.mult))
                    link(dve.tensor_reduce(sm[:], sc, AX_X, ALU.max))
                    link(dve.tensor_tensor(oh, sc, wide8(sm[:]), ALU.is_equal))

                first_largest(lg, m1, oh1)
                yield
                f = "p j e -> p (j e)"
                link(dve.scalar_tensor_tensor(l2.rearrange(f), oh1.rearrange(f), -3e38, lg.rearrange(f), ALU.mult, ALU.add))
                link(dve.tensor_reduce(m2[:], l2, AX_X, ALU.max))
                yield
                first_largest(l2, m2, oh2)
                link(dve.tensor_tensor(eq, oh1, oh2, ALU.add))
                if n:
                    dve.tensor_copy(picked[:, 0:8 * NT], eq.rearrange("p j e -> p (j e)")).then_inc(pick_rdy, 1)
                yield
                dve.wait_ge(ex_rdy, n + 1)
                link(dve.tensor_reduce(sm[:], ex, AX_X, ALU.add))
                link(dve.reciprocal(sm[:], sm[:]))
                link(dve.tensor_tensor(ex, ex, wide8(sm[:]), ALU.mult))
                link(dve.tensor_tensor(cw, ex, eq, ALU.mult))
                if n:
                    link(dve.tensor_reduce(sm[:], cw, AX_X, ALU.add))
                    link(dve.tensor_scalar(sm[:], sm[:], 1e-9, None, ALU.add))
                    link(dve.reciprocal(sm[:], sm[:]))
                    link(dve.tensor_tensor(cw, cw, wide8(sm[:]), ALU.mult))

            def weigh(tiles, at_block):
                dve.wait_ge(y_used, at_block)
                for t in tiles:
                    gates = cw[:, t, :].unsqueeze(2).broadcast_to([P, 8, C])
                    if t >= 2:
                        dve.wait_ge(y_summed, t - 1)
                    dve.tensor_tensor(weighed[t % 2].rearrange("p (e c) -> p e c", e=8),
                                      bank(2 + t % 6).rearrange("p (e c) -> p e c", e=8), gates, ALU.mult).then_inc(y_read, 1)
                for t in tiles:
                    dve.wait_ge(y_read, t + 1)
                    if t >= 2:
                        dve.wait_ge(x_rdy, XD[1] + t - 1)
                    dve.tensor_reduce(red[:, t % 2, :], weighed[t % 2].rearrange("p (e c) -> p c e", e=8), AX_X,
                                      ALU.add).then_inc(y_summed, 1)
                for t in tiles:
                    dve.wait_ge(y_summed, t + 1)
                    dve.tensor_tensor(X[:, t, :], X[:, t, :], red[:, t % 2, :], ALU.add).then_inc(x_rdy, 1)

            def ffn0():
                dve.wait_ge(gh_hi, 1)
                dve.scalar_tensor_tensor(GW[:], GH[:], mask[:, 4:5], small[:, 0:16], ALU.mult, ALU.add).then_inc(gw_rdy, 1)
                dve.tensor_scalar(wb, small[:, 48:50], wlat, TWO_PI / 64, ALU.mult, ALU.mult).then_inc(wb_rdy, 1)
                dve.wait_ge(f0_hi, 1)
                dve.scalar_tensor_tensor(b2r[:], b2H, mask[0:2, 9:10], b2f, ALU.mult, ALU.add).then_inc(f0_rdy, 1)
                norm(1)
                dve.wait_ge(ln_lo, 2 * NG)
                columns_lo(1)
                gating = top_two(0, bank(7))
                next(gating)
                for it in range(32):
                    next(gating, None)
                    dve.wait_ge(g_hi, it + 1)
                    if it >= 2:
                        dve.wait_ge(y_used, it - 1)
                    dve.tensor_tensor(gl[it % 2], g32[it % 2], gh[it % 2], ALU.subtract).then_inc(g_lo, 1)
                    if it >= 9 and it % 8 in (1, 2):
                        t = 4 * (it // 8 - 1) + 2 * (it % 8 - 1)
                        weigh((t, t + 1), 8 * (it // 8))
                        if it % 8 == 2:
                            dve.wait_ge(x_rdy, XD[1] + 4 * (it // 8))
                            centre(2, [it // 8 - 1])
                weigh((12, 13), 32)
                weigh((14, 15), 32)
                dve.wait_ge(x_rdy, XD[2])

            def convolution():
                norm(2, centred_before=NG - 1)
                columns_lo(2)
                dve.wait_ge(pw_rdy, 1)
                for k in (1, 3):
                    dve.wait_ge(a_rdy, k + 1)
                    dve.tensor_copy(spectrum(k), bank(4 + k)[0:64, :].rearrange("p (i n) -> p i n", i=8)).then_inc(xf_rdy, 1)
                dve.wait_ge(b_rdy, 1)
                dve.wait_ge(sx_zero, 1)
                for n in range(8, 16):
                    ins = dve.tensor_copy(*mixing(n))
                ins.then_inc(sx_dve, 1)
                for mb in range(4):
                    dve.wait_ge(z_act, mb + 1)
                    dve.tensor_scalar(Z3[:, 8 * mb:8 * mb + 8, 0:32], Z3[:, 8 * mb:8 * mb + 8, 64:96], -1.0, None,
                                      ALU.mult).then_inc(z_dve, 1)
                for mb in (1, 3):
                    dve.wait_ge(d_rdy, mb + 1)
                    dve.tensor_copy(modes(mb), bank((6, 7, 0, 1)[mb])[0:64, :].rearrange("p (m n) -> p m n", n=64)).then_inc(yt_in, 1)
                dve.wait_ge(t_rdy, 2)
                dve.tensor_copy(YT[:, 4:8, :, :].rearrange("p g r n -> p (g r n)"), bank(3)).then_inc(yt_rdy, 1)
                for n in range(2):
                    dve.wait_ge(e_rdy, n + 1)
                    dve.tensor_tensor(X[:, 8 * n:8 * n + 8, :], X[:, 8 * n:8 * n + 8, :],
                                      bank(4 + n).rearrange("p (j c) -> p j c", c=C), ALU.add).then_inc(x_rdy, 1)
                dve.wait_ge(x_rdy, XD[3])

            def ffn1():
                norm(3)
                dve.wait_ge(ln_lo, 4 * NG)
                columns_lo(3)
                dve.wait_ge(ld_rt, 48)
                dve.memset(picked[:, 8 * NT:], 0.0)
                list(top_two(1, bank(7)))

                c32 = lambda a: a.rearrange("p (c e) -> p c e", e=8)
                link(dve.tensor_tensor(prod.rearrange("p (k n) -> p k n", k=2), oh12,
                                       cw.rearrange("p j e -> p (j e)").unsqueeze(1).broadcast_to([P, 2, P]), ALU.mult))
                link(dve.tensor_reduce(gate2, c32(prod), AX_X, ALU.add))
                link(dve.tensor_copy(gate2h, gate2))
                link(dve.tensor_tensor(gate_rest, gate2, gate2h, ALU.subtract))
                dve.tensor_scalar(gate2l, gate_rest, 2048.0, None, ALU.mult)
                dve.wait_ge(rank_rdy, 1)
                link(dve.tensor_copy(rank, bank(6)[:, 0:(NT + 1) * 8]))
                link(dve.tensor_tensor(above, rank[:, 8 * NT:].unsqueeze(2).broadcast_to([P, 8, 16]), k128, ALU.is_gt))
                link(dve.tensor_reduce(nblk, above, AX_X, ALU.add))
                link(dve.tensor_tensor(partial, before, nblk.unsqueeze(1).broadcast_to([P, 8, 8]), ALU.mult))
                link(dve.tensor_reduce(first, partial, AX_X, ALU.add))
                r3 = rank[:, 0:8 * NT].rearrange("p (j e) -> p j e", e=8)
                link(dve.scalar_tensor_tensor(r3, first.unsqueeze(1).broadcast_to([P, NT, 8]), float(P), r3, ALU.mult, ALU.add))
                link(dve.tensor_tensor(prod.rearrange("p (k n) -> p k n", k=2), oh12,
                                       rank[:, 0:8 * NT].unsqueeze(1).broadcast_to([P, 2, P]), ALU.mult))
                link(dve.tensor_reduce(slot, c32(prod), AX_X, ALU.add))
                link(dve.tensor_copy(slot_i, slot))
                dve.tensor_scalar(blk_i, slot_i, 7, None, ALU.arith_shift_right)
                link(dve.tensor_scalar(pos_i, slot_i, P - 1, None, ALU.bitwise_and))
                dve.tensor_copy(blk_h, blk_i)
                link(dve.tensor_copy(pos_h, pos_i))
                shape = [P, NBLK, 32]
                link(dve.tensor_tensor(OB, numbers[:, 0:NBLK, :], blk_h.unsqueeze(1).broadcast_to(shape), ALU.is_equal))
                for v, a in enumerate((row_id, gate2h, gate2l)):
                    dve.tensor_tensor(OBX[:, v, :, :], OB, a.unsqueeze(1).broadcast_to(shape), ALU.mult)
                ins = dve.tensor_tensor(OR, numbers, pos_h.unsqueeze(1).broadcast_to([P, P, 32]), ALU.is_equal)
                ins.then_inc(map_in, 1)
                link(dve.tensor_tensor(end, first, nblk, ALU.add))
                link(dve.tensor_tensor(past, iota[0:1, 0:8 * NW8].unsqueeze(2).broadcast_to([1, 8 * NW8, 8]),
                                       end[0:1, :].unsqueeze(1).broadcast_to([1, 8 * NW8, 8]), ALU.is_ge))
                link(dve.tensor_reduce(exp_f, past, AX_X, ALU.add))
                link(dve.tensor_scalar(exp_f, exp_f, 7.0, None, ALU.min))
                link(dve.tensor_tensor(exp_f, exp_f, digit, ALU.mult))
                link(dve.tensor_reduce(word_f, exp_f.rearrange("p (w b) -> p w b", b=8), AX_X, ALU.add))
                dve.tensor_copy(word_i, word_f).then_inc(exp_rdy, 1)
                dve.wait_ge(map_rdy, 1)
                link(dve.tensor_scalar(pad_row, bank(7)[:, 0:NBLK], 0.0, own_row, ALU.is_equal, ALU.mult))
                dve.scalar_tensor_tensor(row_i, pad_row, float(P - 1), bank(7)[:, 0:NBLK], ALU.add, ALU.add).then_inc(row_rdy, 1)
                link(dve.tensor_copy(gate, bank(7)[:, NBLK:2 * NBLK]))
                dve.scalar_tensor_tensor(gate, bank(7)[:, 2 * NBLK:3 * NBLK], 1.0 / 2048, gate, ALU.mult,
                                         ALU.add).then_inc(gate_rdy, 1)

                def columns(b, odd):
                    dve.wait_ge(tp_rdy, b + 1)
                    if not (isinstance(b, int) and b < 2):
                        dve.wait_ge(hh_rdy, 2 * b - 2)
                    dve.tensor_copy(xb[odd], bank(4 + odd).bitcast(F16)[:, 0:256]).then_inc(xb_rdy, 1)

                def low(b, odd, half):
                    dve.wait_ge(gg_hi, 2 * b + half + 1)
                    if not (isinstance(b, int) and b < 2):
                        dve.wait_ge(yy_used, 2 * b + half - 3)
                    n = 2 * odd + half
                    dve.tensor_tensor(fl[n], f32[half], fh[n], ALU.subtract).then_inc(gg_lo, 1)

                def outputs(b, u4):
                    dve.wait_ge(ys_hi, b + 1)
                    dve.scalar_tensor_tensor(ys[u4], bank(6 + u4 % 2)[:, C:2 * C], gate[:, bass.ds(b, 1)], ys[u4],
                                             ALU.mult, ALU.add).then_inc(ys_rdy, 1)

                def step(b, u4, is_last=False):
                    odd = u4 % 2
                    if not (isinstance(b, int) and b < 3):
                        outputs(b - 3, (u4 + 1) % 4)
                    if not is_last:
                        columns(b + 1, 1 - odd)
                    for half in range(2):
                        dve.wait_ge(s_rdy, 2 * b + half + 1)
                        if not (isinstance(b, int) and b == 0):
                            dve.wait_ge(gg_lo, 2 * b + half - 1)
                        dve.tensor_tensor(f32[half], bank(2 + half)[:, 0:HALF], s32[half], ALU.mult).then_inc(gg_rdy, 1)
                        if half:
                            low(b, odd, 0)
                        elif not (isinstance(b, int) and b == 0):
                            low(b - 1, 1 - odd, 1)

                columns(0, 0)
                for b in range(4):
                    step(b, b)
                with dve.Fori(1, NBLK // 4) as i:
                    for u in range(4):
                        step(4 * i + u, u)
                for b in range(NBLK // 4 * 4, NBLK):
                    step(b, b % 4, is_last=(b == NBLK - 1))
                low(NBLK - 1, (NBLK - 1) % 2, 1)
                for b in (NBLK - 3, NBLK - 2, NBLK - 1):
                    outputs(b, b % 4)

            attention()
            ffn0()
            convolution()
            ffn1()


def kernel(**inputs):
    import numpy as np
    import concourse.bacc as _bacc
    from concourse import mybir as _mybir
    from concourse.bass_utils import run_bass_kernel_spmd as _run

    I = {k: np.asarray(v) for k, v in inputs.items()}
    f32 = np.float32
    p = np.arange(128)
    arr = {}

    def tile_order(x):
        return x.reshape(2, 2, 16, 32, 64).transpose(0, 1, 3, 2, 4).reshape(128, 1024)

    arr["x"] = tile_order(I["x"])
    arr["wprep"] = np.concatenate([I["L0_conv_W_prep"]] * 2, 0)
    bp = I["L0_conv_b_prep"].reshape(5, 2, 128)
    arr["bprep"] = bp[:4].transpose(2, 0, 1).reshape(128, 8)
    arr["bv"] = np.stack([bp[4].reshape(256)] * 2)
    arr["ones"] = np.ones((2, 128), np.float16)
    y = p // 8 % 2
    arr["bfin"] = np.broadcast_to(I["L0_conv_b_fin"][None], (128, 64))
    intr = I["L0_conv_intrinsic"]
    tn = intr[:, ::-1, ::-1, 1:33].transpose(0, 3, 1, 2).reshape(2, 128, 225)
    tm = intr[:, :, :, 33:65].transpose(0, 3, 1, 2).reshape(2, 128, 225)
    arr["tables"] = np.stack([tn, tm], 0).transpose(2, 0, 1, 3).reshape(128, 900)
    ii = np.arange(8)
    r = ii[None, :] - ii[:, None] + 7
    bt = intr[:, r[:, None, :, None], r[None, :, None, :], 0]
    arr["biasT"] = bt.reshape(4, 2, 8, 8, 64).transpose(2, 1, 3, 0, 4).reshape(128, 256)
    o, h2 = (p // 16) * 8 + p % 8, p // 8 % 2
    arr["sel"] = (np.arange(128)[None] == (h2 * 64 + o)[:, None]).astype(np.float16)
    arr["ident"] = np.eye(128, dtype=np.float16)
    m = np.zeros((128, 16), f32)
    for c in range(4):
        m[:, c] = (p // 32 == c)
    m[:, 4] = -(p >= 64).astype(f32)
    m[:, 5], m[:, 6] = y == 0, y == 1
    m[:, 7], m[:, 8] = EPS_A, EPS_C
    m[1, 9] = -1
    arr["mask"] = m
    arr["cen"] = (y[:, None] == y[None, :]).astype(f32) / f32(64)
    arr["varm"] = (y[:, None] == np.arange(64)[None, :] // 32).astype(f32) / f32(63)
    arr["wfin"] = I["L0_conv_W_fin"].reshape(2, 128, 64).transpose(1, 0, 2).reshape(128, 128)

    arr["identf"] = np.eye(64, dtype=f32)
    W1 = I["L0_ffn_W1"].transpose(1, 0, 2).reshape(64, 1024)
    arr["w1g"] = np.concatenate([W1, W1])
    arr["w2g"] = I["L0_ffn_W2"].transpose(1, 0, 2).reshape(128, 512)
    arr["b2g"] = np.stack([I["L0_ffn_b2"].reshape(512)] * 2)
    sm = np.zeros((128, 64), f32)
    sm[:, 0:8] = np.concatenate([I["L0_ffn_gate_w"]] * 2)
    sm[:, 8:16] = np.concatenate([I["L1_ffn_router_w"].T] * 2)
    sm[:, 16:24] = I["L0_ffn_gate_b"][None]
    sm[:, 24:32] = I["L0_ffn_b1"].T
    sm[:, 32:40] = 8 - np.arange(8)
    sm[:, 40] = I["L1_conv_w"][p % 32]
    for b in range(2):
        sm[:, 42 + b] = (p // 2 % 2 == b) & (p % 2 == 0)
        sm[:, 44 + b] = (p // 2 % 2 == b) & (p % 2 == 1)
        sm[:, 48 + b] = p // 32 == b
    arr["small"] = sm
    n, mm = np.arange(64)[:, None], np.arange(32)[None]
    ang = 2 * np.pi * n * mm / 64
    F = np.stack([np.cos(ang), -np.sin(ang)], -1).reshape(64, 64).astype(f32)
    Fh = F.astype(np.float16)
    arr["dft"] = np.concatenate([Fh, (F - Fh.astype(f32)).astype(np.float16)])
    cm = np.where(np.arange(32) == 0, 1.0, 2.0)[:, None]
    gi = np.zeros((4, 32, 2, 4, 64), f32)
    for q in range(4):
        gi[q, :, 0, q] = cm * np.cos(ang.T)
        gi[q, :, 1, q] = -cm * np.sin(ang.T)
    arr["gi"] = gi.reshape(128, 512)
    pct = I["L1_conv_pct"]
    arr["pctr"] = pct[:, :32][p // 4].reshape(128, 1024)
    pt = pct[:, :32].transpose(2, 1, 0).reshape(32, 1024)
    arr["pctt"] = np.concatenate([pt, pt])
    wc = I["L1_conv_weights"].reshape(32, 32, 8, 4, 32, 2)
    arr["wc"] = wc.transpose(3, 0, 4, 2, 5, 1).reshape(128, 32 * 8 * 64)
    w13 = np.zeros((2, 64, 8, 768), f32)
    w13[0, :, :, :682] = I["L1_ffn_w1"].transpose(2, 0, 1)
    w13[1, :, :, :682] = I["L1_ffn_w3"].transpose(2, 0, 1)
    w13 = w13.transpose(1, 0, 2, 3).reshape(64, 12288)
    arr["w13"] = np.concatenate([w13, w13])
    w2 = np.zeros((8, 768, 64), f32)
    w2[:, :682] = I["L1_ffn_w2"].transpose(0, 2, 1)
    arr["w2"] = w2.reshape(8, 6, 128, 64).transpose(2, 0, 1, 3).reshape(128, 3072)

    rt = np.zeros((128, 288), f32)
    rt[:, 0:128] = np.arange(128)
    rt[:, 128:144] = 128 * np.arange(16)
    rt[:, 144:208] = (np.arange(8)[None, :] < np.arange(8)[:, None]).reshape(64)
    rt[:, 240] = p - 127
    rt[:, 241:281] = 8 ** (np.arange(40) % 8)
    arr["routing"] = rt
    arr["routing16"] = np.concatenate([p[:, None] < p[None, :], np.ones((128, 128)),
                                       1 + 16 * p[:, None] + np.arange(32)[None] % 16], 1).astype(np.float16)
    arr["numbers"] = np.broadcast_to(np.repeat(np.arange(128), 32)[None], (128, 4096)).astype(np.float16)
    arr["zeros"] = np.zeros((1088, 128), f32)

    nc = _bacc.Bacc("TRN2", target_bir_lowering=False, num_devices=1)
    inp, feeds = {}, {}
    for name, a in arr.items():
        a = np.ascontiguousarray(a)
        feeds[f"in_{name}"] = a
        inp[name] = nc.dram_tensor(f"in_{name}", a.shape, _mybir.dt.from_np(a.dtype), kind="ExternalInput").ap()
    out = nc.dram_tensor("out", (128 + 2048, 64), _mybir.dt.float32, kind="ExternalOutput").ap()
    build(nc, inp, out)
    r = _run(nc, [feeds], core_ids=[0])
    y = r.results[0]["out"][128:]
    return y.reshape(2, 2, 32, 16, 64).transpose(0, 1, 3, 2, 4).reshape(2, 32, 32, 64)
```
